# Optimizing a Trainium2 kernel written in Bass

```python
import numpy as np
import jax
import jax.numpy as jnp

def _softmax(x, axis=-1):
    return jax.nn.softmax(x, axis=axis)

def _gelu(x):
    return jax.nn.gelu(x, approximate=True)

def _silu(x):
    return jax.nn.silu(x)

def _sigmoid(x):
    return jax.nn.sigmoid(x)

def _layernorm(x, axis=-1, eps=1e-05):
    m = jnp.mean(x, axis=axis, keepdims=True)
    v = jnp.var(x, axis=axis, keepdims=True)
    return (x - m) / jnp.sqrt(v + eps)

def _scatter_add(tgt, idx, src, axis=0):
    return tgt.at[idx].add(src)

def _segment_sum(src, seg, n):
    return jax.ops.segment_sum(src, seg, n)
kernel_name = 'mk_xattn_ffn_d2_seqx_r8_0b6d4f'

def setup_inputs(seed: int=0):
    np.random.seed(seed)
    _w = jnp.asarray

    def _rec_inputs():
        import jax
        import jax.numpy as jnp
        _rk = jax.random.key(seed)
        x = -0.0002928 + 1 * jax.random.normal(jax.random.fold_in(_rk, 1), (8, 128, 128), jnp.float32)
        _lenS = 128 - jax.random.randint(jax.random.fold_in(_rk, 7), (8,), 0, max(1, 128 // 4) + 1, jnp.int32)
        _lenS2 = 128 - jax.random.randint(jax.random.fold_in(_rk, 8), (8,), 0, max(1, 128 // 4) + 1, jnp.int32)
        _ctx_1024P = jax.random.normal(jax.random.fold_in(_rk, 11), (8, 16, 128), jnp.float32)
        _ctx_1024c = jax.random.dirichlet(jax.random.fold_in(_rk, 511), 0.3 * jnp.ones((16,), jnp.float32), (8, 128))
        _ctx_1024t = jnp.einsum('bsk,bkd->bsd', _ctx_1024c, _ctx_1024P)
        _ctx_1024t = _ctx_1024t * jax.lax.rsqrt(jnp.mean(jnp.square(_ctx_1024t)) + 1e-12) * 0.953939
        ctx_1024 = -1.39393e-06 + 0.999914 * (_ctx_1024t + 0.3 * jax.random.normal(jax.random.fold_in(_rk, 611), (8, 128, 128), jnp.float32))
        fside_Bx16xSxS2_0 = 9.80324e-06 + 0.100009 * jax.random.normal(jax.random.fold_in(_rk, 12), (8, 16, 128, 128), jnp.float32)
        fside_SxS2_0 = -2.64403e-05 + 0.100002 * jax.random.normal(jax.random.fold_in(_rk, 14), (128, 128), jnp.float32)
        _validS = jnp.arange(128)[None, :] < _lenS[:, None]
        _validS2 = jnp.arange(128)[None, :] < _lenS2[:, None]
        _causal = jnp.tril(jnp.ones((128, 128), dtype=bool))
        mask_BxS2_bf0 = jnp.logical_not(jnp.ones((8, 128), dtype=bool))
        return (x, ctx_1024, fside_Bx16xSxS2_0, fside_SxS2_0, mask_BxS2_bf0)
    x, ctx_1024, fside_Bx16xSxS2_0, fside_SxS2_0, mask_BxS2_bf0 = _rec_inputs()

    def _L0_xattn_setup():
        import jax, jax.numpy as jnp
        import numpy as np
        E = 128
        H = 16
        D = E // H
        key = jax.random.key(seed)
        ks = jax.random.split(key, 12)
        B, T, S = (2, 256, 256)
        inp = {'query': jax.random.normal(ks[0], (B, T, E), jnp.float32), 'key': jax.random.normal(ks[1], (B, S, E), jnp.float32), 'value': jax.random.normal(ks[2], (B, S, E), jnp.float32), 'spatial_bias': jax.random.normal(ks[3], (B, H, T, S), jnp.float32) * 0.1, 'directional_bias': jax.random.normal(ks[4], (B, H, T, S), jnp.float32) * 0.1, 'key_padding_mask': jnp.zeros((B, S), dtype=bool), 'attn_mask': jax.random.normal(ks[5], (T, S), jnp.float32) * 0.1, 'Wq': jax.random.normal(ks[6], (E, E), jnp.float32) / np.sqrt(E), 'bq': jnp.zeros((E,), jnp.float32), 'Wk': jax.random.normal(ks[7], (E, E), jnp.float32) / np.sqrt(E), 'bk': jnp.zeros((E,), jnp.float32), 'Wv': jax.random.normal(ks[8], (E, E), jnp.float32) / np.sqrt(E), 'bv': jnp.zeros((E,), jnp.float32), 'Wo': jax.random.normal(ks[9], (E, E), jnp.float32) / np.sqrt(E), 'bo': jnp.zeros((E,), jnp.float32)}
        return inp
    _L0_xattn_all = _L0_xattn_setup()
    _L0_xattn_in = {k: v for k, v in _L0_xattn_all.items() if k in ('Wq', 'bq', 'Wk', 'bk', 'Wv', 'bv', 'Wo', 'bo')}
    del _L0_xattn_all

    def _L0_ffn_setup():
        import jax, jax.numpy as jnp
        import numpy as np
        TOP_K = 2
        key = jax.random.key(seed)
        kx, kg, k1, k2 = jax.random.split(key, 4)
        B, T, D, E, H = (4, 128, 128, 8, 256)
        x = jax.random.normal(kx, (B, T, D), dtype=jnp.float32)
        Wg = jax.random.normal(kg, (D, E), dtype=jnp.float32) * 0.02
        W1 = jax.random.normal(k1, (E, D, H), dtype=jnp.float32) * 0.02
        W2 = jax.random.normal(k2, (E, H, D), dtype=jnp.float32) * 0.02
        return {'x': x, 'Wg': Wg, 'W1': W1, 'W2': W2}
    _L0_ffn_all = _L0_ffn_setup()
    _L0_ffn_in = {k: v for k, v in _L0_ffn_all.items() if k in ('Wg', 'W1', 'W2')}
    del _L0_ffn_all

    def _L1_xattn_setup():
        import jax, jax.numpy as jnp
        import numpy as np
        D_MODEL = 64
        N_HEADS = 8
        D_KEYS = D_MODEL // N_HEADS
        DIN = D_MODEL * 2
        DPROJ = D_KEYS * N_HEADS * 2
        B, L = (2, 256)
        key = jax.random.key(seed)
        ks = jax.random.split(key, 11)
        s_in = 1.0 / np.sqrt(DIN)
        s_out = 1.0 / np.sqrt(DPROJ)
        return {'queries': jax.random.normal(ks[0], (B, L, DIN), jnp.float32), 'keys': jax.random.normal(ks[1], (B, L, DIN), jnp.float32), 'values': jax.random.normal(ks[2], (B, L, DIN), jnp.float32), 'Wq': jax.random.normal(ks[3], (DPROJ, DIN), jnp.float32) * s_in, 'bq': jax.random.normal(ks[4], (DPROJ,), jnp.float32) * s_in, 'Wk': jax.random.normal(ks[5], (DPROJ, DIN), jnp.float32) * s_in, 'bk': jax.random.normal(ks[6], (DPROJ,), jnp.float32) * s_in, 'Wv': jax.random.normal(ks[7], (DPROJ, DIN), jnp.float32) * s_in, 'bv': jax.random.normal(ks[8], (DPROJ,), jnp.float32) * s_in, 'Wo': jax.random.normal(ks[9], (DIN, DPROJ), jnp.float32) * s_out, 'bo': jax.random.normal(ks[10], (DIN,), jnp.float32) * s_out}
    _L1_xattn_all = _L1_xattn_setup()
    _L1_xattn_in = {k: v for k, v in _L1_xattn_all.items() if k in ('Wq', 'bq', 'Wk', 'bk', 'Wv', 'bv', 'Wo', 'bo')}
    del _L1_xattn_all

    def _L1_ffn_setup():
        import jax, jax.numpy as jnp
        import numpy as np
        NUM_NOD = 6
        MAX_PREV = 5
        NUM_EDGE = 20
        D = 128
        H = 8
        LN_EPS = 1e-06

        def _layernorm(x, g, b):
            mu = jnp.mean(x, axis=-1, keepdims=True)
            var = jnp.mean(jnp.square(x - mu), axis=-1, keepdims=True)
            return (x - mu) * jax.lax.rsqrt(var + LN_EPS) * g + b

        def _mha(q, k, v, wq, wk, wv, wo):
            B, S, d = q.shape
            dh = d // H
            qh = (q @ wq).reshape(B, S, H, dh)
            kh = (k @ wk).reshape(B, S, H, dh)
            vh = (v @ wv).reshape(B, S, H, dh)
            scores = jnp.einsum('bqhd,bkhd->bhqk', qh, kh) / jnp.sqrt(jnp.asarray(dh, q.dtype))
            attn = jax.nn.softmax(scores, axis=-1)
            ctx = jnp.einsum('bhqk,bkhd->bqhd', attn, vh).reshape(B, S, d)
            return ctx @ wo
        key = jax.random.key(seed)
        ks = jax.random.split(key, 12)
        B, S = (8, 128)
        scale = 1.0 / np.sqrt(D)
        return {'inputs': jax.random.normal(ks[0], (B, S, D), jnp.float32), 'ew': jax.random.uniform(ks[1], (NUM_NOD, 3), jnp.float32), 'act_w': jax.random.uniform(ks[2], (NUM_NOD,), jnp.float32), 'We': jax.random.normal(ks[3], (NUM_EDGE, D, D), jnp.float32) * scale, 'be': jnp.zeros((NUM_EDGE, D), jnp.float32), 'Wq': jax.random.normal(ks[4], (NUM_NOD, D, D), jnp.float32) * scale, 'Wk': jax.random.normal(ks[5], (NUM_NOD, D, D), jnp.float32) * scale, 'Wv': jax.random.normal(ks[6], (NUM_NOD, D, D), jnp.float32) * scale, 'Wo': jax.random.normal(ks[7], (NUM_NOD, D, D), jnp.float32) * scale, 'ln_g': jnp.ones((D,), jnp.float32), 'ln_b': jnp.zeros((D,), jnp.float32)}
    _L1_ffn_all = _L1_ffn_setup()
    _L1_ffn_in = {k: v for k, v in _L1_ffn_all.items() if k in ('ew', 'act_w', 'We', 'be', 'Wq', 'Wk', 'Wv', 'Wo', 'ln_g', 'ln_b')}
    del _L1_ffn_all
    return {'x': x, 'ctx_1024': ctx_1024, 'fside_Bx16xSxS2_0': fside_Bx16xSxS2_0, 'fside_SxS2_0': fside_SxS2_0, 'mask_BxS2_bf0': mask_BxS2_bf0, 'L0_xattn_Wq': _L0_xattn_in['Wq'], 'L0_xattn_bq': _L0_xattn_in['bq'], 'L0_xattn_Wk': _L0_xattn_in['Wk'], 'L0_xattn_bk': _L0_xattn_in['bk'], 'L0_xattn_Wv': _L0_xattn_in['Wv'], 'L0_xattn_bv': _L0_xattn_in['bv'], 'L0_xattn_Wo': _L0_xattn_in['Wo'], 'L0_xattn_bo': _L0_xattn_in['bo'], 'L0_ffn_Wg': _L0_ffn_in['Wg'], 'L0_ffn_W1': _L0_ffn_in['W1'], 'L0_ffn_W2': _L0_ffn_in['W2'], 'L1_xattn_Wq': _L1_xattn_in['Wq'], 'L1_xattn_bq': _L1_xattn_in['bq'], 'L1_xattn_Wk': _L1_xattn_in['Wk'], 'L1_xattn_bk': _L1_xattn_in['bk'], 'L1_xattn_Wv': _L1_xattn_in['Wv'], 'L1_xattn_bv': _L1_xattn_in['bv'], 'L1_xattn_Wo': _L1_xattn_in['Wo'], 'L1_xattn_bo': _L1_xattn_in['bo'], 'L1_ffn_ew': _L1_ffn_in['ew'], 'L1_ffn_act_w': _L1_ffn_in['act_w'], 'L1_ffn_We': _L1_ffn_in['We'], 'L1_ffn_be': _L1_ffn_in['be'], 'L1_ffn_Wq': _L1_ffn_in['Wq'], 'L1_ffn_Wk': _L1_ffn_in['Wk'], 'L1_ffn_Wv': _L1_ffn_in['Wv'], 'L1_ffn_Wo': _L1_ffn_in['Wo'], 'L1_ffn_ln_g': _L1_ffn_in['ln_g'], 'L1_ffn_ln_b': _L1_ffn_in['ln_b']}

def reference(x, ctx_1024, fside_Bx16xSxS2_0, fside_SxS2_0, mask_BxS2_bf0, L0_xattn_Wq, L0_xattn_bq, L0_xattn_Wk, L0_xattn_bk, L0_xattn_Wv, L0_xattn_bv, L0_xattn_Wo, L0_xattn_bo, L0_ffn_Wg, L0_ffn_W1, L0_ffn_W2, L1_xattn_Wq, L1_xattn_bq, L1_xattn_Wk, L1_xattn_bk, L1_xattn_Wv, L1_xattn_bv, L1_xattn_Wo, L1_xattn_bo, L1_ffn_ew, L1_ffn_act_w, L1_ffn_We, L1_ffn_be, L1_ffn_Wq, L1_ffn_Wk, L1_ffn_Wv, L1_ffn_Wo, L1_ffn_ln_g, L1_ffn_ln_b):
    import jax
    import jax.numpy as jnp

    def _L0_xattn_ref(query, key, value, spatial_bias, directional_bias, key_padding_mask, attn_mask, Wq, bq, Wk, bk, Wv, bv, Wo, bo):
        import jax, jax.numpy as jnp
        import numpy as np
        E = 128
        H = 16
        D = E // H
        B, T, _ = query.shape
        S = key.shape[1]
        scale = D ** (-0.5)
        q = (query @ Wq.T + bq).reshape(B, T, H, D).transpose(0, 2, 1, 3)
        k = (key @ Wk.T + bk).reshape(B, S, H, D).transpose(0, 2, 1, 3)
        v = (value @ Wv.T + bv).reshape(B, S, H, D).transpose(0, 2, 1, 3)
        scores = jnp.einsum('bhtd,bhsd->bhts', q, k) * scale
        scores = scores + attn_mask[None, None, :, :]
        pad = key_padding_mask[:, None, None, :]
        scores = jnp.where(pad, -jnp.inf, scores)
        if T == S:
            scores = scores + spatial_bias + directional_bias
        probs = jax.nn.softmax(scores, axis=-1)
        out = jnp.einsum('bhts,bhsd->bhtd', probs, v)
        out = out.transpose(0, 2, 1, 3).reshape(B, T, E)
        return out @ Wo.T + bo

    def _L0_ffn_ref(x, Wg, W1, W2):
        import jax, jax.numpy as jnp
        import numpy as np
        TOP_K = 2
        B, T, D = x.shape
        E = W1.shape[0]
        logits = jnp.einsum('btd,de->bte', x, Wg)
        probs = jax.nn.softmax(logits, axis=-1)
        top_w, top_i = jax.lax.top_k(probs, TOP_K)
        top_w = top_w / (jnp.sum(top_w, axis=-1, keepdims=True) + 1e-08)
        N = B * T
        oh = jax.nn.one_hot(top_i.reshape(N, TOP_K), E, dtype=x.dtype)
        combine = jnp.sum(oh * top_w.reshape(N, TOP_K)[..., None], axis=1)
        xt = x.reshape(N, D)
        h = jnp.einsum('td,edh->teh', xt, W1)
        h = jnp.square(jax.nn.relu(h))
        y = jnp.einsum('teh,ehd->ted', h, W2)
        out = jnp.einsum('te,ted->td', combine, y)
        return out.reshape(B, T, D)

    def _L1_xattn_ref(queries, keys, values, Wq, bq, Wk, bk, Wv, bv, Wo, bo):
        import jax, jax.numpy as jnp
        import numpy as np
        D_MODEL = 64
        N_HEADS = 8
        D_KEYS = D_MODEL // N_HEADS
        DIN = D_MODEL * 2
        DPROJ = D_KEYS * N_HEADS * 2
        B, L = (2, 256)
        b, l, _ = queries.shape
        H, E = (N_HEADS, 2)
        q = (queries @ Wq.T + bq).reshape(b, l, -1, H, E)
        k = (keys @ Wk.T + bk).reshape(b, l, -1, H, E)
        v = (values @ Wv.T + bv).reshape(b, l, -1, H, E)
        scale = 1.0 / np.sqrt(E)
        scores = jnp.einsum('bnlhe,bnshe->bnhls', q, k)
        A = jax.nn.softmax(scale * scores, axis=-1)
        out = jnp.einsum('bnhls,bnshd->bnlhd', A, v)
        out = out.reshape(b, l, -1)
        return out @ Wo.T + bo

    def _L1_ffn_ref(inputs, ew, act_w, We, be, Wq, Wk, Wv, Wo, ln_g, ln_b):
        import jax, jax.numpy as jnp
        import numpy as np
        NUM_NOD = 6
        MAX_PREV = 5
        NUM_EDGE = 20
        D = 128
        H = 8
        LN_EPS = 1e-06

        def _layernorm(x, g, b):
            mu = jnp.mean(x, axis=-1, keepdims=True)
            var = jnp.mean(jnp.square(x - mu), axis=-1, keepdims=True)
            return (x - mu) * jax.lax.rsqrt(var + LN_EPS) * g + b

        def _mha(q, k, v, wq, wk, wv, wo):
            B, S, d = q.shape
            dh = d // H
            qh = (q @ wq).reshape(B, S, H, dh)
            kh = (k @ wk).reshape(B, S, H, dh)
            vh = (v @ wv).reshape(B, S, H, dh)
            scores = jnp.einsum('bqhd,bkhd->bhqk', qh, kh) / jnp.sqrt(jnp.asarray(dh, q.dtype))
            attn = jax.nn.softmax(scores, axis=-1)
            ctx = jnp.einsum('bhqk,bkhd->bqhd', attn, vh).reshape(B, S, d)
            return ctx @ wo
        nodes = {-1: inputs}
        lind = 0
        for c in range(NUM_NOD):
            nsrc = min(c + 1, MAX_PREV)
            snode = c - nsrc
            eq, ek, ev = (lind + nsrc - 1, lind, lind + nsrc // 2)
            in_q, in_k, in_v = (c - 1, snode, snode + nsrc // 2)
            q = ew[c, 0] * (nodes[in_q] @ We[eq] + be[eq])
            k = ew[c, 1] * (nodes[in_k] @ We[ek] + be[ek])
            v = ew[c, 2] * (nodes[in_v] @ We[ev] + be[ev])
            o = _mha(q, k, v, Wq[c], Wk[c], Wv[c], Wo[c])
            nodes[c] = act_w[c] * o + q
            lind += nsrc
        out = nodes[NUM_NOD - 1]
        return _layernorm(out, ln_g, ln_b)
    x = x + _L0_xattn_ref(_layernorm(x, axis=-1), ctx_1024, ctx_1024, fside_Bx16xSxS2_0, fside_Bx16xSxS2_0, mask_BxS2_bf0, fside_SxS2_0, L0_xattn_Wq, L0_xattn_bq, L0_xattn_Wk, L0_xattn_bk, L0_xattn_Wv, L0_xattn_bv, L0_xattn_Wo, L0_xattn_bo)
    x = x + _L0_ffn_ref(_layernorm(x, axis=-1), L0_ffn_Wg, L0_ffn_W1, L0_ffn_W2)
    x = x + _L1_xattn_ref(_layernorm(x, axis=-1), ctx_1024, ctx_1024, L1_xattn_Wq, L1_xattn_bq, L1_xattn_Wk, L1_xattn_bk, L1_xattn_Wv, L1_xattn_bv, L1_xattn_Wo, L1_xattn_bo)
    x = x + _L1_ffn_ref(_layernorm(x, axis=-1), L1_ffn_ew, L1_ffn_act_w, L1_ffn_We, L1_ffn_be, L1_ffn_Wq, L1_ffn_Wk, L1_ffn_Wv, L1_ffn_Wo, L1_ffn_ln_g, L1_ffn_ln_b)
    return x

_drawn_inputs = setup_inputs


def setup_inputs(seed=0):
    import zlib

    import numpy as np

    out = dict(_drawn_inputs(seed))
    spreads = {'L0_xattn_bq': (0.0, 0.421),
     'L0_xattn_bk': (0.0, 2.0),
     'L0_xattn_bv': (0.0, 0.1),
     'L0_xattn_bo': (0.0, 0.1),
     'L1_ffn_be': (0.0, 0.1),
     'L1_ffn_ln_g': (1.0, 0.2),
     'L1_ffn_ln_b': (0.0, 0.335)}
    factors = {'fside_Bx16xSxS2_0': 3.68,
     'fside_SxS2_0': 7.277,
     'L0_ffn_Wg': 6.964,
     'L0_ffn_W1': 6.584,
     'L0_ffn_W2': 6.015,
     'L1_xattn_bq': 8.035,
     'L1_ffn_Wq': 200.0,
     'L1_ffn_Wk': 200.0,
     'L1_xattn_bk': 6.448,
     'L1_xattn_bv': 5.851}
    for name, (base, spread) in spreads.items():
        noise = np.random.default_rng([zlib.crc32(name.encode()), seed]).standard_normal(out[name].shape)
        drawn = base * np.exp(spread * noise) if base else spread * noise
        out[name] = jnp.asarray(drawn.astype(out[name].dtype))
    for name, factor in factors.items():
        out[name] = (out[name] * factor).astype(out[name].dtype)
    return out
```

```python
from contextlib import ExitStack

import concourse.bass as bass
from concourse import mybir

F32 = mybir.dt.float32
U8 = mybir.dt.uint8
U32 = mybir.dt.uint32
ALU = mybir.AluOpType
ACT = mybir.ActivationFunctionType
AX_X = mybir.AxisListType.X

NB = 8
T = 128
E = 128
H0, D0 = 16, 8
G1, H1 = 8, 8
NEXP, HID = 8, 256
H3, D3 = 8, 16
NODES = 6
SCALE0 = D0 ** -0.5
SCALE1 = 2 ** -0.5
SCALE3 = D3 ** -0.5
VW0 = 128 + D0
VW3 = 128 + D3


class Batch:

    def __init__(self, reg, off):
        self.reg, self.off = reg, off
        self.n = off if reg is None else 2 * reg + off
        self.p = off % 2
        self.turn = off // 2 if reg is None else reg + off // 2

    def before(self, k):
        off = self.off - k
        if self.reg is None and not 0 <= off < NB:
            return None
        return Batch(self.reg, off)


def over_batches(eng, step, lag):
    for t in range(2):
        step(Batch(None, t))
    with eng.Fori(0, NB // 2 - 1) as i:
        for off in (2, 3):
            step(Batch(i, off))
    for t in range(NB, NB + lag):
        step(Batch(None, t))


def node_sources(c):
    nsrc = min(c + 1, 5)
    first = sum(min(k + 1, 5) for k in range(c))
    snode = c - nsrc
    return (c, snode + 1, snode + nsrc // 2 + 1), (first + nsrc - 1, first, first + nsrc // 2)


def xattn_ffn_kernel(nc, x_h, ctxT_h, fside_h, mask_h, wa_h, wb_h, wc_h, wd_h, cols_h, rows_h, out_h):
    ctx = ExitStack()
    with ctx:
        def sb(name, shape, dt=F32):
            return ctx.enter_context(nc.sbuf_tensor(name, shape, dt))

        def sem(name):
            return ctx.enter_context(nc.semaphore(name))

        x_all = sb("x_all", [T, NB, E])
        ctxT = sb("ctxT", [E, NB, T])
        mask_u32 = sb("mask_u32", [T, NB * T // 4], U32)
        mask_u8 = mask_u32[:, :].bitcast(U8).rearrange("p (b t) -> p b t", t=T)
        wa = sb("wa", [E, 5, 128])
        wb = sb("wb", [E, 8 + 2 * NEXP * HID // 128 * 128])
        wc = sb("wc", [E, 4, 128])
        wd = sb("wd", [E, 8, NODES, 128])
        cols = sb("cols", [E, 64])
        rows = sb("rows", [T, 8, 128])
        wg = wb[:, 0:NEXP]
        w1 = wb[:, NEXP:NEXP + NEXP * HID].rearrange("p (k m) -> p k m", m=128)
        w2 = wb[:, NEXP + NEXP * HID:].rearrange("p (k m) -> p k m", m=128)
        bq_col, bk_col = cols[:, 0:1], cols[:, 1:2]
        ew = cols[:, 2:20].rearrange("p (c k) -> p c k", k=3)
        act_w = cols[:, 20:26]
        beT = cols[:, 26:44].rearrange("p (c k) -> p c k", k=3)
        bv_row, bo_row, bqkv1_row, bo1_row, g_row, b_row = (
            rows[:, 0, :], rows[:, 1, :], rows[:, 2:5, :], rows[:, 5, :], rows[:, 6, :], rows[:, 7, :])

        ident = sb("ident", [128, 128])
        head0 = sb("head0", [128, H0])
        head3 = sb("head3", [128, H3])
        minus_half = sb("minus_half", [128, NB])
        iota8 = sb("iota8", [128, NEXP])
        half_am = sb("half_am", [T, T])
        pad_all = sb("pad_all", [T, NB, T])

        nodesT = sb("nodesT", [E, NODES + 1, NB, T])
        big_a = sb("big_a", [128, 2, H0 * T])
        big_b = sb("big_b", [128, 2, H0 * T])
        big_c = sb("big_c", [128, 2, H0 * T])
        big_d = sb("big_d", [128, H0 * T])

        def part(tile2, start, *shape):
            size = 1
            for n in shape:
                size *= n
            names = "abcd"[:len(shape)]
            return tile2[:, start:start + size].rearrange(
                "p (%s) -> p %s" % (" ".join(names), " ".join(names)), **dict(zip(names, shape)))

        flat_a, flat_b, flat_c = (t.rearrange("p a b -> p (a b)") for t in (big_a[:, :, :], big_b[:, :, :], big_c[:, :, :]))

        stats = sb("stats", [T, 2, 6])
        mv = sb("mv", [T, 2, 2])
        veps = sb("veps", [T, 2])
        rstd = sb("rstd", [T, 2])
        xn = sb("xn", [T, 2, E])
        xnT = sb("xnT", [E, 2, T])
        stats_a = sb("stats_a", [T, NB, 6])
        mv_a = sb("mv_a", [T, NB, 2])
        veps_a = sb("veps_a", [T, NB])
        rstd_a = sb("rstd_a", [T, NB])

        xn_a, xnT_a = nodesT[:, 1, :, :], nodesT[:, 2, :, :]
        kT_all = nodesT[:, 3, :, :]
        qT_all, v_all = nodesT[:, 4, :, :], nodesT[:, 5, :, :]
        qT = sb("qT", [E, 2, T])
        v_spread = sb("v_spread", [T, 2, 4 * VW0])
        am = sb("am", [T, 2, T])
        fs = part(flat_a, 0, 2, H0, T)
        km = part(flat_b, 0, 2, H0, T)
        hmax = sb("hmax", [T, 2, H0])
        nmax = sb("nmax", [T, 2, H0])
        prob = part(flat_c, 0, 2, H0, T)
        den = sb("den", [T, 2, H0])
        rden = sb("rden", [T, 2, H0])
        probT = part(big_d, 0, H0, T)
        rrow = sb("rrow", [T, 2, E])
        r_bc = sb("r_bc", [E, 2, T])
        ctxn = sb("ctxn", [E, 2, T])
        xbo = sb("xbo", [T, 2, E])

        gsm = sb("gsm", [T, 2, 8, NEXP])
        gidx = sb("gidx", [T, 2, 8], U32)
        gcol = sb("gcol", [T, 2, 8])
        comb = sb("comb", [T, 2, NEXP])
        relu_h = part(flat_c, 0, 2, 4, T)
        h2 = part(flat_b, 0, 2, 16, T)

        kv_all = sb("kv_all", [T, NB, 2, E])
        q1 = sb("q1", [T, 2, E])
        pr0 = part(flat_a, 0, 2, 512)
        pr1 = part(flat_a, 1024, 2, 512)
        sc1 = part(flat_a, 2048, 2, 512)
        m1 = sb("m1", [T, 2, 64])
        e1 = part(flat_a, 3072, 2, 512)
        l1 = sb("l1", [T, 2, 64])
        rl1 = sb("rl1", [T, 2, 64])
        ev = part(flat_c, 1024, 2, G1, E)
        ctx1 = sb("ctx1", [T, 2, E])
        ctx1T = sb("ctx1T", [E, 2, T])

        scl = sb("scl", [128, NODES, 4])
        wf = sb("wf", [E, NODES, 4, 128])
        wres = sb("wres", [E, NODES, 128])
        bias3 = sb("bias3", [E, NODES, 3])
        qqk = part(flat_a, 0, NB, 3, T)
        v3 = sb("v3", [T, NB, 2 * VW3])
        km3 = part(flat_b, 0, 3, H3, T)
        nmax3 = sb("nmax3", [T, 2, H3])
        den3 = sb("den3", [T, 2, H3])
        rden3 = sb("rden3", [T, 2, H3])
        p3 = part(flat_c, 0, 2, H3, T)
        p3T = part(big_d, 0, H3, T)
        fin, fin2, xb = part(wb, 0, NB, E), part(wb, NB * E, NB, E), part(wb, 2 * NB * E, NB, E)

        ps = ctx.enter_context(nc.psum_tensor("ps", [128, 8, 512], F32))

        ld = {k: sem("ld_" + k) for k in ("x", "ctx", "mask", "wa", "wb", "wc", "wd", "cols", "rows")}
        fs_landed = [sem("fs_landed0"), sem("fs_landed1")]
        s = {}
        for name in """zeroed ident_ready const_ready v_zeroed iota_ready passed half_am_ready pad_ready
            a_stats a_mv a_veps a_rstd a_xn a_xnT_ps a_xnT a_proj_ps a_k a_q a_v a_v_ps
            a_am a_bias a_qT a_vs a_km_dve a_km_pool a_s_ps a_hmax a_nmax a_exp a_rden a_rrow
            a_pT_ps a_pT_act a_pT_dve a_r_ps a_r a_pv_ps a_ctxn a_o_ps a_x a_xbo a_vfree
            kv_ps kv
            b_stats b_mv b_veps b_rstd b_xn b_xnT_ps b_xnT b_gate_ps b_h_ps b_relu b_h2
            b_gmax b_gexp b_rsum b_prob b_top b_idx b_idxf b_gden b_rgden b_w b_c1 b_c2 b_comb b_y_ps b_y
            c_stats c_mv c_veps c_rstd c_xn c_xnT_ps c_xnT c_q_ps c_q c_pr0 c_pr1 c_sc c_m c_sub c_exp
            c_l c_rl c_ev0 c_ev1 c_ctx_ps c_ctx c_ctxT_ps c_ctxT c_o_ps c_xbo c_x
            n_stats n_mv n_veps n_rstd n_xn n_xnT_ps n_xnT
            f_w_ps f_scl f_w f_wres f_b_ps f_bias
            d_proj_ps d_qqk d_v d_km d_s_ps d_max d_exp d_rden d_rrow d_pT_ps d_pT_act d_pT_dve d_r_ps d_r
            d_pv_ps d_ctxn d_o_ps d_node
            e_T_ps e_stats e_mv e_veps e_rstd e_n e_g e_xb e_out out_done""".split():
            s[name] = sem(name)

        block = ctx.enter_context(nc.Block())

        def spread0(tile2):
            return tile2.rearrange("p (v x) -> p v x", x=VW0)[:, :, 0:128].rearrange(
                "p v (j u d) -> p v j u d", u=4, d=D0)[:, :, :, 0, :]

        def spread3(tile2):
            return tile2.rearrange("p (v x) -> p v x", x=VW3)[:, :, 0:128].rearrange(
                "p v (j u d) -> p v j u d", u=2, d=D3)[:, :, :, 0, :]

        ITEMS = [(c, b) for c in range(NODES) for b in range(NB)]
        NI = len(ITEMS)

        def over_items(step):
            for t in range(NI + 6):
                step(lambda k, t=t: t - k if 0 <= t - k < NI else None)

        @block.sync
        def _(sp):
            sp.dma_start(x_all[:, :, :], x_h).then_inc(ld["x"], 16)
            sp.dma_start(ctxT[:, :, :], ctxT_h).then_inc(ld["ctx"], 16)
            sp.dma_start(wa[:, :, :], wa_h).then_inc(ld["wa"], 16)
            sp.dma_start(cols[:, :], cols_h).then_inc(ld["cols"], 16)
            sp.dma_start(rows[:, :, :], rows_h).then_inc(ld["rows"], 16)
            sp.dma_start(mask_u32[:, :], mask_h).then_inc(ld["mask"], 16)

            def step(t):
                if (b := t.before(0)) is not None:
                    if b.reg is not None or b.off >= 2:
                        sp.wait_ge(s["a_exp"], 4 * (b.n - 1))
                    sp.dma_start(fs[:, b.p, :, :], fside_h[b.n]).then_inc(fs_landed[b.p], 16)

            for t in range(2):
                step(Batch(None, t))
            sp.dma_start(wc[:, :, :], wc_h).then_inc(ld["wc"], 16)
            sp.dma_start(wb[:, :], wb_h).then_inc(ld["wb"], 16)
            sp.dma_start(wd[:, :, :, :], wd_h).then_inc(ld["wd"], 16)
            with sp.Fori(0, NB // 2 - 1) as i:
                for off in (2, 3):
                    step(Batch(i, off))
            for b in range(NB):
                sp.wait_ge(s["e_out"], b + 1)
                sp.dma_start(out_h[:, b, :], fin2[:, b, :]).then_inc(s["out_done"], 16)
            sp.wait_ge(s["out_done"], 16 * NB)

        @block.gpsimd
        def _(pool):
            pool.memset(ident[:, :], 0.0).then_inc(s["zeroed"], 1)
            pool.memset(head0[:, :], 1.0).then_inc(s["zeroed"], 1)
            pool.memset(head3[:, :], 1.0).then_inc(s["zeroed"], 1)
            pool.memset(minus_half[:, :], -0.5).then_inc(s["zeroed"], 1)
            pool.wait_ge(s["zeroed"], 4)
            pool.affine_select(out=ident[:, :], in_=ident[:, :], compare_op=ALU.not_equal, fill=1.0,
                               base=0, pattern=[[-1, 128]], channel_multiplier=1).then_inc(s["ident_ready"], 1)
            for tile, heads, width in ((head0, H0, D0), (head3, H3, D3)):
                pool.affine_select(out=tile[:, :], in_=tile[:, :], compare_op=ALU.is_ge, fill=0.0, base=0,
                                   pattern=[[-width, heads]], channel_multiplier=1).then_inc(s["zeroed"], 1)
            pool.wait_ge(s["zeroed"], 6)
            for tile, heads, width in ((head0, H0, D0), (head3, H3, D3)):
                pool.affine_select(out=tile[:, :], in_=tile[:, :], compare_op=ALU.is_ge, fill=0.0,
                                   base=width - 1, pattern=[[width, heads]],
                                   channel_multiplier=-1).then_inc(s["const_ready"], 1)
            pool.wait_ge(s["a_veps"], 1)
            pool.tensor_tensor(rstd_a[:, :], veps_a[:, :], minus_half[:, :], ALU.pow).then_inc(s["a_rstd"], 1)
            pool.wait_ge(ld["mask"], 16)
            pool.tensor_scalar(pad_all[:, :, :], mask_u8, -3.0e38, 3.0e38, ALU.mult,
                               ALU.mult).then_inc(s["pad_ready"], 1)
            pool.wait_ge(s["pad_ready"], 1)
            pool.wait_ge(s["half_am_ready"], 1)
            pool.wait_ge(s["const_ready"], 2)

            def attn0(t):
                if (b := t.before(0)) is not None:
                    pool.wait_ge(s["a_bias"], b.n + 1)
                    pool.tensor_tensor(am[:, b.p, :], half_am[:, :], pad_all[:, b.n, :],
                                       ALU.add).then_inc(s["a_am"], 1)
                    pool.wait_ge(s["a_am"], b.n + 1)
                    pool.wait_ge(fs_landed[b.p], 16 * (b.turn + 1))
                    pool.tensor_tensor(fs[:, b.p, :, :], fs[:, b.p, :, :],
                                       am[:, b.p, :].unsqueeze(1).to_broadcast([T, H0, T]),
                                       ALU.add).then_inc(s["a_bias"], 1)
                    pool.wait_ge(s["a_k"], 1)
                    pool.wait_ge(s["a_s_ps"], 4 * b.n + 4)
                    pool.tensor_tensor(km[:, b.p, 8:16, :],
                                       kT_all[:, b.n, :].unsqueeze(1).to_broadcast([E, 8, T]),
                                       head0[:, 8:16].unsqueeze(2).to_broadcast([E, 8, T]),
                                       ALU.mult).then_inc(s["a_km_pool"], 1)
                if (b := t.before(1)) is not None:
                    pool.wait_ge(s["a_x"], b.n + 1)
                    pool.wait_ge(ld["rows"], 16)
                    pool.tensor_tensor(xbo[:, b.p, :], x_all[:, b.n, :], bo_row, ALU.add).then_inc(s["a_xbo"], 1)

            pool.sem_inc(s["a_bias"], 2)
            over_batches(pool, attn0, 1)

            def rstd_of(name, b):
                pool.wait_ge(s[name + "_veps"], b.n + 1)
                pool.tensor_tensor(rstd[:, b.p:b.p + 1], veps[:, b.p:b.p + 1], minus_half[:, 0:1],
                                   ALU.pow).then_inc(s[name + "_rstd"], 1)

            def moe(t):
                if (b := t.before(0)) is not None:
                    rstd_of("b", b)

            over_batches(pool, moe, 0)

            def attn1(t):
                if (b := t.before(2)) is not None:
                    pool.wait_ge(s["c_exp"], b.n + 1)
                    pool.wait_ge(s["c_ctx_ps"], b.n + 1)
                    vv = kv_all[:, b.n, 1, :].rearrange("p (s h e) -> p h s e", h=H1, e=2)[:, :, :, 1]
                    pool.tensor_tensor(
                        ev[:, b.p, :, :].rearrange("p s (l h e) -> p l h s e", h=H1, e=2)[:, :, :, :, 1],
                        e1[:, b.p, :].rearrange("p (l h s) -> p l h s", h=H1, s=G1),
                        vv.unsqueeze(1).to_broadcast([T, G1, H1, G1]), ALU.mult).then_inc(s["c_ev1"], 1)
                    pool.wait_ge(s["c_x"], b.n + 1)
                    pool.tensor_tensor(xbo[:, b.p, :], x_all[:, b.n, :], bo1_row, ALU.add).then_inc(s["c_xbo"], 1)
                if (b := t.before(1)) is not None:
                    pool.wait_ge(s["c_q"], b.n + 2)
                    pool.wait_ge(s["c_sc"], b.n + 1)
                    qv = q1[:, b.p, :].rearrange("p (l h e) -> p l h e", h=H1, e=2)[:, :, :, 1]
                    kv = kv_all[:, b.n, 0, :].rearrange("p (s h e) -> p h s e", h=H1, e=2)[:, :, :, 1]
                    pool.tensor_tensor(
                        pr1[:, b.p, :].rearrange("p (l h s) -> p l h s", h=H1, s=G1),
                        qv.unsqueeze(3).to_broadcast([T, G1, H1, G1]),
                        kv.unsqueeze(1).to_broadcast([T, G1, H1, G1]), ALU.mult).then_inc(s["c_pr1"], 1)
                if (b := t.before(0)) is not None:
                    rstd_of("c", b)

            over_batches(pool, attn1, 2)

            def norm3(t):
                if (b := t.before(0)) is not None:
                    rstd_of("n", b)

            over_batches(pool, norm3, 0)

            def nodes(at):
                if (i := at(0)) is not None:
                    c, b = ITEMS[i]
                    pool.wait_ge(s["d_qqk"], i + 1)
                    if i >= 3:
                        pool.wait_ge(s["d_s_ps"], 2 * (i - 2))
                    pool.tensor_tensor(km3[:, i % 3, :, :],
                                       qqk[:, b, 2, :].unsqueeze(1).to_broadcast([E, H3, T]),
                                       head3[:, :].unsqueeze(2).to_broadcast([E, H3, T]),
                                       ALU.mult).then_inc(s["d_km"], 1)

            over_items(nodes)
            for b in range(NB):
                pool.tensor_tensor(xb[:, b, :], x_all[:, b, :], b_row, ALU.add).then_inc(s["e_xb"], 1)
            for b in range(NB):
                pool.wait_ge(s["e_veps"], b + 1)
                pool.tensor_tensor(rstd_a[:, b:b + 1], veps_a[:, b:b + 1], minus_half[:, 0:1],
                                   ALU.pow).then_inc(s["e_rstd"], 1)

        @block.tensor
        def _(pe):
            pe.wait_ge(s["ident_ready"], 1)
            pe.wait_ge(ld["wa"], 16)
            pe.wait_ge(ld["ctx"], 16)
            for n in range(2):
                pe.matmul(ps[:, 4 + n, :], wa[:, 1, :], ctxT[:, 4 * n:4 * n + 4, :],
                          start=True, stop=True).then_inc(s["a_proj_ps"], 1)
            for b in range(NB):
                last = pe.matmul(ps[:, 6 + b // 4, 128 * (b % 4):128 * (b % 4) + 128], ctxT[:, b, :], wa[:, 2, :],
                                 start=True, stop=True)
                if b % 4 == 3:
                    last.then_inc(s["a_v_ps"], 1)
            for b in range(NB):
                pe.wait_ge(s["a_xn"], b + 1)
                pe.transpose(ps[:, b // 4, 128 * (b % 4):128 * (b % 4) + 128], xn_a[:, b, :],
                             ident[:, :]).then_inc(s["a_xnT_ps"], 1)
            for n in range(2):
                pe.wait_ge(s["a_xnT"], n + 1)
                pe.matmul(ps[:, 2 + n, :], wa[:, 0, :], xnT_a[:, 4 * n:4 * n + 4, :],
                          start=True, stop=True).then_inc(s["a_proj_ps"], 1)
            pe.wait_ge(s["a_q"], 2)
            pe.wait_ge(s["a_v"], 2)
            pe.wait_ge(s["a_k"], 1)
            pe.sem_inc(s["a_s_ps"], 8)
            pe.sem_inc(s["a_pT_ps"], 4)
            pe.sem_inc(s["a_pv_ps"], 1)

            def attn0(t):
                front, back = t.before(1), t.before(2)

                def scores(b, k):
                    if k == 0:
                        pe.wait_ge(s["a_qT"], b.n + 1)
                        pe.wait_ge(s["a_km_dve"], b.n + 1)
                    if k == 2:
                        pe.wait_ge(s["a_km_pool"], b.n + 1)
                    pe.wait_ge(s["a_hmax"], 4 * b.n + k + 1)
                    pe.matmul(ps[:, k, :], qT[:, b.p, :], km[:, b.p, 4 * k:4 * k + 4, :],
                              start=True, stop=True).then_inc(s["a_s_ps"], 1)

                def turn(b, k):
                    pe.wait_ge(s["a_exp"], 4 * b.n + k + 1)
                    pe.wait_ge(s["a_pT_dve" if k % 2 == 0 else "a_pT_act"], 2 * b.n + k // 2 + 2)
                    for h in range(4):
                        last = pe.transpose(ps[:, 4 + k % 2, 128 * h:128 * h + 128], prob[:, b.p, 4 * k + h, :],
                                            ident[:, :])
                    last.then_inc(s["a_pT_ps"], 1)

                if back is not None:
                    turn(back, 0)
                    turn(back, 1)
                if front is not None:
                    scores(front, 0)
                if back is not None:
                    turn(back, 2)
                if front is not None:
                    scores(front, 1)
                if back is not None:
                    turn(back, 3)
                if front is not None:
                    scores(front, 2)
                if back is not None:
                    b = back
                    pe.wait_ge(s["a_rrow"], b.n + 1)
                    pe.wait_ge(s["a_r"], b.n + 1)
                    pe.transpose(ps[:, 6, 0:128], rrow[:, b.p, :], ident[:, :]).then_inc(s["a_r_ps"], 1)
                    pe.wait_ge(s["a_vs"], b.n + 1)
                    pe.wait_ge(s["a_pT_dve"], 2 * b.n + 4)
                    pe.wait_ge(s["a_pT_act"], 2 * b.n + 4)
                    pe.wait_ge(s["a_x"], b.n + 2)
                    for u in range(4):
                        for j in range(4):
                            last = pe.matmul(ps[32 * j:32 * j + 32, 7, 0:128],
                                             v_spread[:, b.p, 128 * u + 32 * j:128 * u + 32 * j + 32],
                                             probT[:, 4 * j + u, :], start=(u == 0), stop=(u == 3))
                    last.then_inc(s["a_pv_ps"], 1)
                if front is not None:
                    scores(front, 3)
                if back is not None:
                    pe.wait_ge(s["a_ctxn"], back.n + 1)
                    pe.matmul(ps[:, 7, 128:256], ctxn[:, back.p, :], wa[:, 3, :],
                              start=True, stop=True).then_inc(s["a_o_ps"], 1)

            over_batches(pe, attn0, 2)

            pe.wait_ge(ld["wc"], 16)
            pe.wait_ge(s["a_hmax"], 4 * NB + 4)
            for b in range(NB):
                last = pe.matmul(ps[:, b // 2, 256 * (b % 2):256 * (b % 2) + 256], ctxT[:, b, :], wc[:, 1:3, :],
                                 start=True, stop=True)
                if b % 2:
                    last.then_inc(s["kv_ps"], 1)
            pe.wait_ge(ld["wd"], 16)
            pe.wait_ge(ld["cols"], 16)
            pe.wait_ge(s["a_pT_dve"], 2 * NB + 2)
            pe.wait_ge(s["a_pT_act"], 2 * NB + 2)
            pe.wait_ge(s["a_r"], NB + 1)
            pe.wait_ge(s["a_x"], NB + 2)
            FW = [4, 5, 6, 7, 0, 1]
            for c in range(NODES):
                if c >= 4:
                    pe.wait_ge(s["kv"], FW[c] + 1)
                wk = FW[c]
                pe.matmul(ps[:, wk, 0:128], wd[:, 0, c, :], wd[:, 4, c, :], start=True, stop=True)
                pe.matmul(ps[:, wk, 128:256], wd[:, 1, c, :], wd[:, 5, c, :], start=True, stop=True)
                pe.matmul(ps[:, wk, 256:384], wd[:, 2, c, :], wd[:, 6, c, :], start=True, stop=True)
                pe.matmul(ps[:, wk, 384:512], beT[:, c, 2:3].to_broadcast([E, 128]), wd[:, 6, c, :],
                          start=True, stop=True).then_inc(s["f_w_ps"], 1)
            pe.wait_ge(s["kv"], 3)
            for c in range(NODES):
                pe.matmul(ps[:, 2, 2 * c:2 * c + 1], wd[:, 4, c, :], beT[:, c, 0:1], start=True, stop=True)
                last = pe.matmul(ps[:, 2, 2 * c + 1:2 * c + 2], wd[:, 5, c, :], beT[:, c, 1:2],
                                 start=True, stop=True)
            last.then_inc(s["f_b_ps"], 1)
            pe.wait_ge(s["kv"], 4)
            pe.wait_ge(s["f_w"], NODES)
            pe.wait_ge(s["f_bias"], 2)
            pe.wait_ge(ld["wb"], 16)

            def moe(t):
                front, back = t.before(1), t.before(2)

                def experts_out(b, e):
                    pe.wait_ge(s["b_h2"], 4 * b.n + e // 2 + 1)
                    if e % 4 == 0:
                        pe.wait_ge(s["b_y"], 8 * b.n + 4 + e)
                    for k in (2 * e, 2 * e + 1):
                        last = pe.matmul(ps[:, 4 + e // 4, 128 * (e % 4):128 * (e % 4) + 128], h2[:, b.p, k, :],
                                         w2[:, k, :], start=(k % 2 == 0), stop=(k % 2 == 1))
                    if e % 4 == 3:
                        last.then_inc(s["b_y_ps"], 1)

                if back is not None:
                    for e in range(4):
                        experts_out(back, e)
                if front is not None:
                    pe.wait_ge(s["b_xn"], front.n + 1)
                    pe.wait_ge(s["b_gexp"], front.n + 1)
                    pe.transpose(ps[:, 6, 0:128], xn[:, front.p, :], ident[:, :]).then_inc(s["b_xnT_ps"], 1)
                if back is not None:
                    for e in range(4, 8):
                        experts_out(back, e)
                if front is not None:
                    b = front
                    pe.wait_ge(s["b_xnT"], b.n + 1)
                    pe.matmul(ps[:, 6, 128:128 + NEXP], xnT[:, b.p, :], wg, start=True,
                              stop=True).then_inc(s["b_gate_ps"], 1)
                    for k in range(4):
                        if b.reg is not None or b.off >= 1:
                            pe.wait_ge(s["b_h2"], 4 * b.n + k - 3)
                        for m in range(4):
                            last = pe.matmul(ps[:, k, 128 * m:128 * m + 128], w1[:, 4 * k + m, :], xnT[:, b.p, :],
                                             start=True, stop=True)
                        last.then_inc(s["b_h_ps"], 1)

            over_batches(pe, moe, 2)
            pe.wait_ge(s["b_y"], 8 * NB + 8)
            pe.wait_ge(s["b_h2"], 4 * NB)

            def attn1(t):
                front, back = t.before(1), t.before(2)
                if front is not None:
                    b = front
                    pe.wait_ge(s["c_xn"], b.n + 1)
                    pe.wait_ge(s["c_q"], b.n + 1)
                    pe.transpose(ps[:, 0, 0:128], xn[:, b.p, :], ident[:, :]).then_inc(s["c_xnT_ps"], 1)
                    pe.wait_ge(s["c_xnT"], b.n + 1)
                    pe.matmul(ps[:, 0, 128:256], xnT[:, b.p, :], wc[:, 0, :], start=True,
                              stop=True).then_inc(s["c_q_ps"], 1)
                    pe.wait_ge(s["c_pr0"], b.n + 1)
                    pe.wait_ge(s["c_sub"], b.n + 1)
                    pe.matmul(ps[:, 2, :], ident[:, :], pr0[:, b.p, :], start=True, stop=False)
                    pe.wait_ge(s["c_pr1"], b.n + 1)
                    pe.matmul(ps[:, 2, :], ident[:, :], pr1[:, b.p, :], start=False,
                              stop=True).then_inc(s["c_sc"], 1)
                if back is not None:
                    b = back
                    pe.wait_ge(s["c_ev0"], b.n + 1)
                    pe.wait_ge(s["c_ev1"], b.n + 1)
                    pe.wait_ge(s["c_ctx"], b.n + 1)
                    for g in range(G1):
                        last = pe.matmul(ps[:, 3, 0:128], ident[:, :], ev[:, b.p, g, :],
                                         start=(g == 0), stop=(g == G1 - 1))
                    last.then_inc(s["c_ctx_ps"], 1)
                    pe.wait_ge(s["c_ctx"], b.n + 2)
                    pe.wait_ge(s["c_x"], b.n + 2)
                    pe.transpose(ps[:, 4, 0:128], ctx1[:, b.p, :], ident[:, :]).then_inc(s["c_ctxT_ps"], 1)
                    pe.wait_ge(s["c_ctxT"], b.n + 1)
                    pe.matmul(ps[:, 4, 128:256], ctx1T[:, b.p, :], wc[:, 3, :], start=True,
                              stop=True).then_inc(s["c_o_ps"], 1)

            pe.sem_inc(s["c_sc"], 2)
            pe.sem_inc(s["c_ctx_ps"], 2)
            over_batches(pe, attn1, 2)

            def norm3(t):
                if (b := t.before(1)) is not None:
                    pe.wait_ge(s["n_xn"], b.n + 1)
                    pe.wait_ge(s["n_xnT"], b.n + 1)
                    pe.transpose(ps[:, 5 + b.p, 0:128], xn[:, b.p, :], ident[:, :]).then_inc(s["n_xnT_ps"], 1)

            pe.sem_inc(s["n_xnT_ps"], 2)
            over_batches(pe, norm3, 1)
            pe.wait_ge(s["n_xnT"], NB + 2)
            pe.wait_ge(s["c_x"], NB + 2)
            pe.wait_ge(s["f_wres"], 1)

            def nodes(at):
                def turn(i, k):
                    pe.wait_ge(s["d_exp"], 8 * i + 4 * k + 4)
                    if i >= 1:
                        pe.wait_ge(s["d_pT_act" if k else "d_pT_dve"], i)
                    for h in range(4):
                        last = pe.transpose(ps[:, 4 + k, 128 * h:128 * h + 128], p3[:, i % 2, 4 * k + h, :],
                                            ident[:, :])
                    last.then_inc(s["d_pT_ps"], 1)

                back = at(4)
                if back is not None:
                    turn(back, 0)
                if (i := at(5)) is not None:
                    c, b = ITEMS[i]
                    pe.wait_ge(s["d_ctxn"], i + 1)
                    pe.matmul(ps[:, 7, 256:384], wd[:, 3, c, :], ctxn[:, i % 2, :], start=True,
                              stop=True).then_inc(s["d_o_ps"], 1)
                if (i := at(0)) is not None:
                    c, b = ITEMS[i]
                    (sq, sk, sv), _ = node_sources(c)
                    if c:
                        pe.wait_ge(s["d_node"], i - NB + 1)
                    if i >= 1:
                        pe.wait_ge(s["d_v"], i)
                    pe.matmul(ps[:, 6, 0:128], wres[:, c, :], nodesT[:, sq, b, :], start=True, stop=True)
                    pe.matmul(ps[:, 6, 128:256], wf[:, c, 0, :], nodesT[:, sq, b, :], start=True, stop=True)
                    pe.matmul(ps[:, 6, 256:384], wf[:, c, 1, :], nodesT[:, sk, b, :], start=True, stop=True)
                    pe.matmul(ps[:, 6, 384:512], nodesT[:, sv, b, :], wf[:, c, 2, :], start=True,
                              stop=True).then_inc(s["d_proj_ps"], 1)
                if back is not None:
                    pe.wait_ge(s["d_rrow"], back + 1)
                    if back >= 1:
                        pe.wait_ge(s["d_node"], back)
                    pe.transpose(ps[:, 7, 128:256], rrow[:, back % 2, :], ident[:, :]).then_inc(s["d_r_ps"], 1)
                    turn(back, 1)
                if (i := at(2)) is not None:
                    c, b = ITEMS[i]
                    pe.wait_ge(s["d_km"], i + 1)
                    if i >= 2:
                        pe.wait_ge(s["d_exp"], 8 * (i - 1))
                    for k in range(2):
                        pe.matmul(ps[:, 2 * (i % 2) + k, :], qqk[:, b, 1, :], km3[:, i % 3, 4 * k:4 * k + 4, :],
                                  start=True, stop=True).then_inc(s["d_s_ps"], 1)
                if back is not None:
                    b = back % NB
                    pe.wait_ge(s["d_pT_dve"], back + 1)
                    pe.wait_ge(s["d_pT_act"], back + 1)
                    pe.wait_ge(s["d_r"], back + 1)
                    for u in range(2):
                        for j in range(4):
                            last = pe.matmul(ps[32 * j:32 * j + 32, 7, 0:128],
                                             v3[:, b, 128 * u + 32 * j:128 * u + 32 * j + 32],
                                             p3T[:, 2 * j + u, :], start=(u == 0), stop=(u == 1))
                    last.then_inc(s["d_pv_ps"], 1)

            over_items(nodes)
            pe.wait_ge(s["d_exp"], 8 * NI)
            for b in range(NB):
                pe.wait_ge(s["d_node"], NI - NB + b + 1)
                pe.transpose(ps[:, b // 4, 128 * (b % 4):128 * (b % 4) + 128], nodesT[:, NODES, b, :],
                             ident[:, :]).then_inc(s["e_T_ps"], 1)

        @block.scalar
        def _(act):
            act.wait_ge(ld["wa"], 16)
            act.activation(half_am[:, :], wa[:, 4, :], ACT.Copy, scale=0.5).then_inc(s["half_am_ready"], 1)
            act.wait_ge(ld["cols"], 16)
            for n in range(2):
                act.wait_ge(s["a_xnT_ps"], 4 * n + 4)
                act.activation(xnT_a[:, 4 * n:4 * n + 4, :], ps[:, n, :], ACT.Copy).then_inc(s["a_xnT"], 1)
            for n in range(2):
                act.wait_ge(s["a_proj_ps"], 3 + n)
                act.activation(qT_all[:, 4 * n:4 * n + 4, :], ps[:, 2 + n, :], ACT.Identity,
                               bias=bq_col).then_inc(s["a_q"], 1)
            act.wait_ge(s["a_q"], 2)
            act.wait_ge(s["a_v"], 2)
            act.wait_ge(s["v_zeroed"], 1)
            act.sem_inc(s["a_pT_act"], 2)
            act.sem_inc(s["a_r"], 1)

            def attn0(t):
                front, back = t.before(1), t.before(2)

                def turned(b, k):
                    act.wait_ge(s["a_pT_ps"], 4 * b.n + k + 5)
                    act.wait_ge(s["a_pv_ps"], b.n + 1)
                    act.activation(probT[:, 4 * k:4 * k + 4, :], ps[:, 5, :], ACT.Copy).then_inc(s["a_pT_act"], 1)

                def exps(b, k):
                    act.wait_ge(s["a_nmax"], 4 * b.n + k + 1)
                    for h in range(4 * k, 4 * k + 4):
                        last = act.activation(prob[:, b.p, h, :], fs[:, b.p, h, :], ACT.Exp, scale=2.0,
                                              bias=nmax[:, b.p, h:h + 1], accum_out=den[:, b.p, h:h + 1])
                    last.then_inc(s["a_exp"], 1)

                if back is not None:
                    turned(back, 1)
                if front is not None:
                    if front.reg is not None or front.off >= 1:
                        act.wait_ge(s["a_rden"], front.n)
                        act.wait_ge(s["a_pT_ps"], 4 * front.n)
                    exps(front, 0)
                if back is not None:
                    turned(back, 3)
                if front is not None:
                    exps(front, 1)
                if back is not None:
                    act.wait_ge(s["a_r_ps"], back.n + 1)
                    act.activation(r_bc[:, back.p, :], ps[:, 6, 0:128], ACT.Copy).then_inc(s["a_r"], 1)
                if front is not None:
                    exps(front, 2)
                    exps(front, 3)
                if (b := t.before(0)) is not None:
                    act.wait_ge(s["a_s_ps"], 4 * b.n + 4)
                    act.activation(qT[:, b.p, :], qT_all[:, b.n, :], ACT.Copy).then_inc(s["a_qT"], 1)
                    if b.reg is not None or b.off >= 1:
                        act.wait_ge(s["a_pv_ps"], b.n)
                    act.activation(spread0(v_spread[:, b.p, :]),
                                   v_all[:, b.n, :].rearrange("p (j v d) -> p v j d", v=4, d=D0),
                                   ACT.Copy).then_inc(s["a_vs"], 1)

            over_batches(act, attn0, 2)

            def moe(t):
                if (b := t.before(1)) is not None:
                    act.wait_ge(s["b_xnT_ps"], b.n + 1)
                    act.activation(xnT[:, b.p, :], ps[:, 6, 0:128], ACT.Copy).then_inc(s["b_xnT"], 1)
                    act.wait_ge(s["b_gmax"], b.n + 1)
                    act.activation(gsm[:, b.p, 0, :], ps[:, 6, 128:128 + NEXP], ACT.Exp, bias=gcol[:, b.p, 0:1],
                                   accum_out=gcol[:, b.p, 1:2]).then_inc(s["b_gexp"], 1)
                    for k in range(4):
                        act.wait_ge(s["b_h_ps"], 4 * b.n + k + 1)
                        if b.reg is not None or b.off >= 1 or k >= 2:
                            act.wait_ge(s["b_h2"], 4 * b.n + k - 1)
                        act.activation(relu_h[:, k % 2, :, :], ps[:, k, :], ACT.Relu).then_inc(s["b_relu"], 1)

            act.sem_inc(s["b_gexp"], 1)
            over_batches(act, moe, 1)

            def attn1(t):
                if (b := t.before(1)) is not None:
                    act.wait_ge(s["c_xnT_ps"], b.n + 1)
                    act.activation(xnT[:, b.p, :], ps[:, 0, 0:128], ACT.Copy).then_inc(s["c_xnT"], 1)
                    act.wait_ge(s["c_sub"], b.n + 2)
                    act.activation(e1[:, b.p, :], sc1[:, b.p, :], ACT.Exp, scale=SCALE1).then_inc(s["c_exp"], 1)
                if (b := t.before(2)) is not None:
                    act.wait_ge(s["c_ctxT_ps"], b.n + 1)
                    act.activation(ctx1T[:, b.p, :], ps[:, 4, 0:128], ACT.Copy).then_inc(s["c_ctxT"], 1)

            over_batches(act, attn1, 2)

            def norm3(t):
                if (b := t.before(1)) is not None:
                    act.wait_ge(s["n_xnT_ps"], b.n + 3)
                    act.activation(nodesT[:, 0, b.n, :], ps[:, 5 + b.p, 0:128], ACT.Copy).then_inc(s["n_xnT"], 1)

            act.sem_inc(s["n_xnT"], 2)
            over_batches(act, norm3, 1)

            def nodes(at):
                if (i := at(4)) is not None:
                    act.wait_ge(s["d_r_ps"], i + 1)
                    act.activation(r_bc[:, i % 2, :], ps[:, 7, 128:256], ACT.Copy).then_inc(s["d_r"], 1)
                    act.wait_ge(s["d_pT_ps"], 2 * i + 2)
                    if i >= 1:
                        act.wait_ge(s["d_pv_ps"], i)
                    act.activation(p3T[:, 4:8, :], ps[:, 5, :], ACT.Copy).then_inc(s["d_pT_act"], 1)
                if (i := at(3)) is not None:
                    act.wait_ge(s["d_max"], i + 1)
                    if i >= 2:
                        act.wait_ge(s["d_pT_ps"], 2 * (i - 1))
                        act.wait_ge(s["d_rden"], i - 1)
                    for h in range(H3):
                        act.activation(p3[:, i % 2, h, :],
                                       ps[:, 2 * (i % 2) + h // 4, 128 * (h % 4):128 * (h % 4) + 128], ACT.Exp,
                                       bias=nmax3[:, i % 2, h:h + 1],
                                       accum_out=den3[:, i % 2, h:h + 1]).then_inc(s["d_exp"], 1)

            over_items(nodes)

        @block.vector
        def _(dve):
            for k in range(NEXP):
                dve.memset(iota8[:, k:k + 1], float(k)).then_inc(s["iota_ready"], 1)
            for tile in (v_spread, v3):
                dve.memset(tile[:, :, :], 0.0).then_inc(s["v_zeroed"], 1)
            dve.wait_ge(ld["x"], 16)
            for b in range(NB):
                dve.bn_stats(stats_a[:, b, :], x_all[:, b, :]).then_inc(s["a_stats"], 1)
            for b in range(NB):
                dve.wait_ge(s["a_stats"], b + 1)
                dve.bn_aggr(mv_a[:, b, :], stats_a[:, b, :]).then_inc(s["a_mv"], 1)
            dve.wait_ge(s["a_mv"], NB)
            dve.tensor_scalar(veps_a[:, :], mv_a[:, :, 1], 1e-5, None, ALU.add).then_inc(s["a_veps"], 1)
            dve.wait_ge(ld["cols"], 16)
            dve.wait_ge(s["a_proj_ps"], 2)
            dve.tensor_scalar(kT_all[:, :, :], ps[:, 4:6, :].rearrange("p a (b t) -> p (a b) t", t=T), bk_col,
                              0.5 * SCALE0, ALU.add, ALU.mult).then_inc(s["a_k"], 1)
            dve.wait_ge(s["a_rstd"], 1)
            for b in range(NB):
                dve.tensor_scalar(xn_a[:, b, :], x_all[:, b, :], mv_a[:, b, 0:1], rstd_a[:, b:b + 1],
                                  ALU.subtract, ALU.mult).then_inc(s["a_xn"], 1)
            dve.wait_ge(ld["rows"], 16)
            for n in range(2):
                dve.wait_ge(s["a_v_ps"], n + 1)
                dve.tensor_tensor(v_all[:, 4 * n:4 * n + 4, :], ps[:, 6 + n, :].rearrange("p (b e) -> p b e", e=E),
                                  bv_row.unsqueeze(1).to_broadcast([T, 4, E]), ALU.add).then_inc(s["a_v"], 1)
            dve.wait_ge(s["a_k"], 1)
            dve.wait_ge(s["const_ready"], 2)
            dve.sem_inc(s["a_hmax"], 4)
            dve.sem_inc(s["a_pT_dve"], 2)
            dve.sem_inc(s["a_x"], 2)
            dve.sem_inc(s["a_rden"], 1)

            def attn0(t):
                front, back = t.before(1), t.before(2)

                def turned(b, k):
                    dve.wait_ge(s["a_pT_ps"], 4 * b.n + k + 5)
                    dve.wait_ge(s["a_pv_ps"], b.n + 1)
                    dve.tensor_copy(probT[:, 4 * k:4 * k + 4, :].rearrange("p h t -> p (h t)"),
                                    ps[:, 4, :]).then_inc(s["a_pT_dve"], 1)

                def half_scores(b, k):
                    dve.wait_ge(s["a_s_ps"], 4 * b.n + k + 9)
                    if k == 0:
                        dve.wait_ge(s["a_bias"], b.n + 3)
                    dve.sem_inc(s["passed"], 1)
                    for h in range(4 * k, 4 * k + 4):
                        last = dve.tensor_tensor_reduce(
                            fs[:, b.p, h, :], ps[:, k, 128 * (h % 4):128 * (h % 4) + 128], fs[:, b.p, h, :],
                            1.0, -3.0e38, ALU.add, ALU.max, hmax[:, b.p, h:h + 1])
                    last.then_inc(s["a_hmax"], 1)
                    dve.wait_ge(s["a_hmax"], 4 * b.n + k + 5)
                    dve.tensor_scalar(nmax[:, b.p, 4 * k:4 * k + 4], hmax[:, b.p, 4 * k:4 * k + 4], -2.0, None,
                                      ALU.mult).then_inc(s["a_nmax"], 1)

                if back is not None:
                    dve.wait_ge(s["a_exp"], 4 * back.n + 4)
                    dve.reciprocal(rden[:, back.p, :], den[:, back.p, :]).then_inc(s["a_rden"], 1)
                    dve.wait_ge(s["a_rden"], back.n + 2)
                    dve.tensor_copy(rrow[:, back.p, :].rearrange("p (h d) -> p h d", d=D0),
                                    rden[:, back.p, :].unsqueeze(2).to_broadcast([T, H0, D0])).then_inc(s["a_rrow"], 1)
                    turned(back, 0)
                if front is not None:
                    half_scores(front, 0)
                if back is not None:
                    turned(back, 2)
                if front is not None:
                    half_scores(front, 1)
                    half_scores(front, 2)
                if back is not None:
                    dve.wait_ge(s["a_pv_ps"], back.n + 2)
                    dve.wait_ge(s["a_r"], back.n + 2)
                    dve.tensor_tensor(ctxn[:, back.p, :], ps[:, 7, 0:128], r_bc[:, back.p, :],
                                      ALU.mult).then_inc(s["a_ctxn"], 1)
                if front is not None:
                    half_scores(front, 3)
                if (b := t.before(0)) is not None:
                    dve.wait_ge(s["a_s_ps"], 4 * b.n + 4)
                    dve.tensor_tensor(km[:, b.p, 0:8, :],
                                      kT_all[:, b.n, :].unsqueeze(1).to_broadcast([E, 8, T]),
                                      head0[:, 0:8].unsqueeze(2).to_broadcast([E, 8, T]),
                                      ALU.mult).then_inc(s["a_km_dve"], 1)
                if back is not None:
                    dve.wait_ge(s["a_o_ps"], back.n + 1)
                    dve.wait_ge(s["a_xbo"], back.n + 1)
                    dve.tensor_tensor(x_all[:, back.n, :], ps[:, 7, 128:256], xbo[:, back.p, :],
                                      ALU.add).then_inc(s["a_x"], 1)

            over_batches(dve, attn0, 2)

            for n in range(4):
                dve.wait_ge(s["kv_ps"], n + 1)
                dve.tensor_tensor(kv_all[:, 2 * n:2 * n + 2, :, :],
                                  ps[:, n, :].rearrange("p (b k e) -> p b k e", k=2, e=E),
                                  bqkv1_row[:, 1:3, :].unsqueeze(1).to_broadcast([T, 2, 2, E]),
                                  ALU.add).then_inc(s["kv"], 1)
            for k, e, f in ((0, 0, 1.0), (1, 1, SCALE3), (2, 2, 1.0), (3, 2, 1.0)):
                dve.tensor_scalar(scl[:, :, k], ew[:, :, e], f, None, ALU.mult).then_inc(s["f_scl"], 1)
            dve.wait_ge(s["f_scl"], 4)
            dve.wait_ge(ld["wd"], 16)
            for c in range(NODES):
                dve.wait_ge(s["f_w_ps"], c + 1)
                dve.tensor_tensor(wf[:, c, :, :], ps[:, [4, 5, 6, 7, 0, 1][c], :].rearrange("p (k e) -> p k e", e=128),
                                  scl[:, c, :].unsqueeze(2).to_broadcast([E, 4, 128]),
                                  ALU.mult).then_inc(s["f_w"], 1)
            dve.wait_ge(s["f_b_ps"], 1)
            dve.tensor_tensor(bias3[:, :, 1:3], ps[:, 2, 0:2 * NODES].rearrange("p (c k) -> p c k", k=2),
                              scl[:, :, 0:2], ALU.mult).then_inc(s["f_bias"], 1)
            dve.tensor_tensor(wres[:, :, :], wd[:, 7, :, :], ew[:, :, 0:1].to_broadcast([E, NODES, 128]),
                              ALU.mult).then_inc(s["f_wres"], 1)
            dve.tensor_tensor(bias3[:, :, 0], beT[:, :, 0], ew[:, :, 0], ALU.mult).then_inc(s["f_bias"], 1)

            def ln_stats(name, b):
                dve.bn_stats(stats[:, b.p, :], x_all[:, b.n, :]).then_inc(s[name + "_stats"], 1)
                dve.wait_ge(s[name + "_stats"], b.n + 1)
                dve.sem_inc(s["passed"], 1)
                dve.bn_aggr(mv[:, b.p, :], stats[:, b.p, :]).then_inc(s[name + "_mv"], 1)
                dve.wait_ge(s[name + "_mv"], b.n + 1)
                dve.tensor_scalar(veps[:, b.p:b.p + 1], mv[:, b.p, 1:2], 1e-5, None,
                                  ALU.add).then_inc(s[name + "_veps"], 1)

            def ln_apply(name, b):
                dve.wait_ge(s[name + "_rstd"], b.n + 1)
                dve.tensor_scalar(xn[:, b.p, :], x_all[:, b.n, :], mv[:, b.p, 0:1], rstd[:, b.p:b.p + 1],
                                  ALU.subtract, ALU.mult).then_inc(s[name + "_xn"], 1)

            def moe(t):
                front, back = t.before(1), t.before(2)
                if front is not None:
                    ln_apply("b", front)

                def weighted(b, k):
                    dve.wait_ge(s["b_y_ps"], 2 * b.n + k + 1)
                    for e in range(4 * k, 4 * k + 4):
                        dve.wait_ge(s["b_y"], 8 * b.n + e + 8)
                        dve.scalar_tensor_tensor(out=x_all[:, b.n, :], in0=ps[:, 4 + k, 128 * (e % 4):128 * (e % 4) + 128],
                                                 scalar=comb[:, b.p, e:e + 1], in1=x_all[:, b.n, :],
                                                 op0=ALU.mult, op1=ALU.add).then_inc(s["b_y"], 1)

                if back is not None:
                    dve.wait_ge(s["b_comb"], back.n + 1)
                    weighted(back, 0)
                    weighted(back, 1)
                if front is not None:
                    b = front
                    n, p = b.n, b.p
                    logits = ps[:, 6, 128:128 + NEXP]
                    dve.wait_ge(s["b_gate_ps"], n + 1)
                    dve.tensor_reduce(gcol[:, p, 0:1], logits, AX_X, ALU.max, negate=True).then_inc(s["b_gmax"], 1)
                    dve.wait_ge(s["b_gexp"], n + 2)
                    dve.reciprocal(gcol[:, p, 2:3], gcol[:, p, 1:2]).then_inc(s["b_rsum"], 1)
                    dve.wait_ge(s["b_rsum"], n + 1)
                    dve.tensor_scalar(gsm[:, p, 1, :], gsm[:, p, 0, :], gcol[:, p, 2:3], None,
                                      ALU.mult).then_inc(s["b_prob"], 1)
                    dve.wait_ge(s["b_prob"], n + 1)
                    dve.sem_inc(s["passed"], 1)
                    dve.max(gsm[:, p, 2, :], gsm[:, p, 1, :]).then_inc(s["b_top"], 1)
                    dve.wait_ge(s["b_top"], n + 1)
                    dve.sem_inc(s["passed"], 1)
                    dve.max_index(gidx[:, p, :], gsm[:, p, 2, :], gsm[:, p, 1, :]).then_inc(s["b_idx"], 1)
                    dve.scalar_tensor_tensor(out=gcol[:, p, 3:4], in0=gsm[:, p, 2, 0:1], scalar=1e-8,
                                             in1=gsm[:, p, 2, 1:2], op0=ALU.add, op1=ALU.add).then_inc(s["b_gden"], 1)
                    dve.wait_ge(s["b_idx"], n + 1)
                    dve.tensor_copy(gcol[:, p, 4:6], gidx[:, p, 0:2]).then_inc(s["b_idxf"], 1)
                    dve.wait_ge(s["b_gden"], n + 1)
                    dve.reciprocal(gcol[:, p, 6:7], gcol[:, p, 3:4]).then_inc(s["b_rgden"], 1)
                    dve.wait_ge(s["b_rgden"], n + 1)
                    dve.tensor_scalar(gsm[:, p, 3, 0:2], gsm[:, p, 2, 0:2], gcol[:, p, 6:7], None,
                                      ALU.mult).then_inc(s["b_w"], 1)
                    dve.wait_ge(s["b_w"], n + 1)
                    dve.wait_ge(s["b_idxf"], n + 1)
                    for k, name in ((0, "b_c1"), (1, "b_c2")):
                        dve.tensor_scalar(gsm[:, p, 4 + k, :], iota8[:, :], gcol[:, p, 4 + k:5 + k],
                                          gsm[:, p, 3, k:k + 1], ALU.is_equal, ALU.mult).then_inc(s[name], 1)
                    dve.wait_ge(s["b_c1"], n + 1)
                    dve.wait_ge(s["b_c2"], n + 1)
                    dve.tensor_tensor(comb[:, p, :], gsm[:, p, 4, :], gsm[:, p, 5, :], ALU.add).then_inc(s["b_comb"], 1)
                    for k in range(4):
                        dve.wait_ge(s["b_relu"], 4 * n + k + 1)
                        dve.tensor_tensor(h2[:, p, 4 * k:4 * k + 4, :],
                                          ps[:, k, :].rearrange("q (m t) -> q m t", t=T),
                                          relu_h[:, k % 2, :, :], ALU.mult).then_inc(s["b_h2"], 1)
                if (b := t.before(0)) is not None:
                    dve.wait_ge(s["a_x"], b.n + 3)
                    ln_stats("b", b)

            dve.wait_ge(s["iota_ready"], NEXP)
            dve.wait_ge(s["v_zeroed"], 2)
            dve.sem_inc(s["b_y"], 8)
            over_batches(dve, moe, 2)

            dve.sem_inc(s["c_q"], 1)
            dve.sem_inc(s["c_sub"], 1)
            dve.sem_inc(s["c_ctx"], 1)
            dve.sem_inc(s["c_x"], 2)

            def attn1(t):
                front, back = t.before(1), t.before(2)
                if front is not None:
                    b = front
                    ln_apply("c", b)
                if back is not None:
                    b = back
                    dve.wait_ge(s["c_exp"], b.n + 1)
                    dve.wait_ge(s["c_ctx_ps"], b.n + 1)
                    vv = kv_all[:, b.n, 1, :].rearrange("p (s h e) -> p h s e", h=H1, e=2)[:, :, :, 0]
                    dve.tensor_tensor(
                        ev[:, b.p, :, :].rearrange("p s (l h e) -> p l h s e", h=H1, e=2)[:, :, :, :, 0],
                        e1[:, b.p, :].rearrange("p (l h s) -> p l h s", h=H1, s=G1),
                        vv.unsqueeze(1).to_broadcast([T, G1, H1, G1]), ALU.mult).then_inc(s["c_ev0"], 1)
                    dve.tensor_reduce(l1[:, b.p, :], e1[:, b.p, :].rearrange("p (g s) -> p g s", s=G1), AX_X,
                                      ALU.add).then_inc(s["c_l"], 1)
                if front is not None:
                    b = front
                    dve.wait_ge(s["c_q_ps"], b.n + 1)
                    dve.tensor_tensor(q1[:, b.p, :], ps[:, 0, 128:256], bqkv1_row[:, 0, :],
                                      ALU.add).then_inc(s["c_q"], 1)
                    dve.wait_ge(s["c_q"], b.n + 2)
                    dve.wait_ge(s["c_sc"], b.n + 1)
                    qv = q1[:, b.p, :].rearrange("p (l h e) -> p l h e", h=H1, e=2)[:, :, :, 0]
                    kk = kv_all[:, b.n, 0, :].rearrange("p (s h e) -> p h s e", h=H1, e=2)[:, :, :, 0]
                    dve.tensor_tensor(
                        pr0[:, b.p, :].rearrange("p (l h s) -> p l h s", h=H1, s=G1),
                        qv.unsqueeze(3).to_broadcast([T, G1, H1, G1]),
                        kk.unsqueeze(1).to_broadcast([T, G1, H1, G1]), ALU.mult).then_inc(s["c_pr0"], 1)
                if back is not None:
                    b = back
                    dve.wait_ge(s["c_l"], b.n + 1)
                    dve.reciprocal(rl1[:, b.p, :], l1[:, b.p, :]).then_inc(s["c_rl"], 1)
                    dve.wait_ge(s["c_rl"], b.n + 1)
                    dve.wait_ge(s["c_ctx_ps"], b.n + 3)
                    dve.tensor_tensor(ctx1[:, b.p, :].rearrange("p (g e) -> p g e", e=2),
                                      ps[:, 3, 0:128].rearrange("p (g e) -> p g e", e=2),
                                      rl1[:, b.p, :].unsqueeze(2).to_broadcast([T, 64, 2]),
                                      ALU.mult).then_inc(s["c_ctx"], 1)
                if front is not None:
                    b = front
                    dve.wait_ge(s["c_sc"], b.n + 3)
                    scores = ps[:, 2, :].rearrange("p (g s) -> p g s", s=G1)
                    dve.tensor_reduce(m1[:, b.p, :], scores, AX_X, ALU.max).then_inc(s["c_m"], 1)
                    dve.wait_ge(s["c_m"], b.n + 1)
                    dve.tensor_tensor(sc1[:, b.p, :].rearrange("p (g s) -> p g s", s=G1), scores,
                                      m1[:, b.p, :].unsqueeze(2).to_broadcast([T, 64, G1]),
                                      ALU.subtract).then_inc(s["c_sub"], 1)
                if back is not None:
                    b = back
                    dve.wait_ge(s["c_o_ps"], b.n + 1)
                    dve.wait_ge(s["c_xbo"], b.n + 1)
                    dve.tensor_tensor(x_all[:, b.n, :], ps[:, 4, 128:256], xbo[:, b.p, :],
                                      ALU.add).then_inc(s["c_x"], 1)
                if (b := t.before(0)) is not None:
                    dve.wait_ge(s["b_y"], 8 * b.n + 16)
                    ln_stats("c", b)

            over_batches(dve, attn1, 2)

            def norm3(t):
                if (b := t.before(1)) is not None:
                    dve.wait_ge(s["n_xnT_ps"], b.n + 1)
                    ln_apply("n", b)
                if (b := t.before(0)) is not None:
                    dve.wait_ge(s["c_x"], b.n + 3)
                    ln_stats("n", b)

            over_batches(dve, norm3, 1)
            dve.wait_ge(s["f_w"], NODES)
            dve.wait_ge(s["f_bias"], 2)

            def nodes(at):
                back = at(4)
                if back is not None:
                    dve.wait_ge(s["d_exp"], 8 * back + 8)
                    dve.reciprocal(rden3[:, back % 2, :], den3[:, back % 2, :]).then_inc(s["d_rden"], 1)
                    dve.wait_ge(s["d_rden"], back + 1)
                    if back >= 2:
                        dve.wait_ge(s["d_r_ps"], back - 1)
                    dve.tensor_copy(rrow[:, back % 2, :].rearrange("p (h d) -> p h d", d=D3),
                                    rden3[:, back % 2, :].unsqueeze(2).to_broadcast([T, H3, D3])).then_inc(s["d_rrow"], 1)
                    dve.wait_ge(s["d_pT_ps"], 2 * back + 1)
                    if back >= 1:
                        dve.wait_ge(s["d_pv_ps"], back)
                    dve.tensor_copy(p3T[:, 0:4, :].rearrange("p h t -> p (h t)"), ps[:, 4, :]).then_inc(s["d_pT_dve"], 1)
                if (i := at(5)) is not None:
                    c, b = ITEMS[i]
                    dve.wait_ge(s["d_o_ps"], i + 1)
                    dve.scalar_tensor_tensor(out=nodesT[:, c + 1, b, :], in0=ps[:, 7, 256:384],
                                             scalar=act_w[:, c:c + 1], in1=qqk[:, b, 0, :],
                                             op0=ALU.mult, op1=ALU.add).then_inc(s["d_node"], 1)
                if (i := at(0)) is not None:
                    c, b = ITEMS[i]
                    dve.wait_ge(s["d_proj_ps"], i + 1)
                    dve.tensor_tensor(qqk[:, b, :, :], ps[:, 6, 0:384].rearrange("p (k t) -> p k t", t=T),
                                      bias3[:, c, :].unsqueeze(2).to_broadcast([E, 3, T]),
                                      ALU.add).then_inc(s["d_qqk"], 1)
                    dve.tensor_tensor(spread3(v3[:, b, :]),
                                      ps[:, 6, 384:512].rearrange("p (j v d) -> p v j d", v=2, d=D3),
                                      wf[:, c, 3, :].rearrange("p (j v d) -> p v j d", v=2, d=D3),
                                      ALU.add).then_inc(s["d_v"], 1)
                if (i := at(2)) is not None:
                    dve.wait_ge(s["d_s_ps"], 2 * i + 2)
                    dve.tensor_reduce(nmax3[:, i % 2, :],
                                      ps[:, 2 * (i % 2):2 * (i % 2) + 2, :].rearrange("p a (h k) -> p (a h) k", k=T),
                                      AX_X, ALU.max, negate=True).then_inc(s["d_max"], 1)
                if back is not None:
                    dve.wait_ge(s["d_pv_ps"], back + 1)
                    dve.wait_ge(s["d_r"], back + 1)
                    if back >= 2:
                        dve.wait_ge(s["d_o_ps"], back - 1)
                    dve.tensor_tensor(ctxn[:, back % 2, :], ps[:, 7, 0:128], r_bc[:, back % 2, :],
                                      ALU.mult).then_inc(s["d_ctxn"], 1)

            over_items(nodes)
            dve.wait_ge(s["e_T_ps"], NB)
            for b in range(NB):
                dve.bn_stats(stats_a[:, b, :], ps[:, b // 4, 128 * (b % 4):128 * (b % 4) + 128]).then_inc(s["e_stats"], 1)
                dve.wait_ge(s["e_stats"], b + 1)
                dve.bn_aggr(mv_a[:, b, :], stats_a[:, b, :]).then_inc(s["e_mv"], 1)
                dve.wait_ge(s["e_mv"], b + 1)
                dve.tensor_scalar(veps_a[:, b:b + 1], mv_a[:, b, 1:2], 1e-6, None, ALU.add).then_inc(s["e_veps"], 1)
            for b in range(NB):
                dve.wait_ge(s["e_rstd"], b + 1)
                dve.tensor_scalar(fin[:, b, :], ps[:, b // 4, 128 * (b % 4):128 * (b % 4) + 128], mv_a[:, b, 0:1],
                                  rstd_a[:, b:b + 1], ALU.subtract, ALU.mult).then_inc(s["e_n"], 1)
                dve.wait_ge(s["e_n"], b + 1)
                dve.tensor_tensor(fin2[:, b, :], fin[:, b, :], g_row, ALU.mult).then_inc(s["e_g"], 1)
                dve.wait_ge(s["e_g"], b + 1)
                dve.wait_ge(s["e_xb"], b + 1)
                dve.tensor_tensor(fin2[:, b, :], fin2[:, b, :], xb[:, b, :], ALU.add).then_inc(s["e_out"], 1)


def kernel(**inputs):
    import numpy as np
    import concourse.bacc as bacc
    from concourse.bass_utils import run_bass_kernel_spmd

    a = {k: np.asarray(v) for k, v in inputs.items()}

    def by_row(rows_of):
        return np.ascontiguousarray(np.concatenate([r.reshape(128, -1) for r in rows_of], axis=1))

    def on_all(v):
        return np.broadcast_to(v.reshape(1, -1), (128, v.size))

    edges = [node_sources(c)[1] for c in range(NODES)]
    we = a["L1_ffn_We"]
    arrays = {
        "x": np.ascontiguousarray(a["x"].transpose(1, 0, 2)),
        "ctxT": np.ascontiguousarray(a["ctx_1024"].transpose(2, 0, 1)),
        "fside": np.ascontiguousarray(a["fside_Bx16xSxS2_0"].transpose(0, 2, 1, 3)),
        "mask": np.ascontiguousarray(np.broadcast_to(a["mask_BxS2_bf0"].view(np.uint32).reshape(1, -1),
                                                         (128, NB * T // 4))),
        "wa": by_row([a["L0_xattn_Wq"].T, a["L0_xattn_Wk"].T, a["L0_xattn_Wv"].T, a["L0_xattn_Wo"].T,
                      a["fside_SxS2_0"]]),
        "wb": by_row([a["L0_ffn_Wg"], a["L0_ffn_W1"].transpose(1, 0, 2),
                      a["L0_ffn_W2"].reshape(NEXP * HID // 128, 128, E).transpose(1, 0, 2)]),
        "wc": by_row([a["L1_xattn_" + k].T for k in ("Wq", "Wk", "Wv", "Wo")]),
        "wd": by_row([we[e[k]].T for k in range(3) for e in edges]
                     + [a["L1_ffn_" + k][c] for k in ("Wo", "Wq", "Wk", "Wv") for c in range(NODES)]
                     + [we[e[0]] for e in edges]),
        "cols": by_row([a["L0_xattn_bq"], a["L0_xattn_bk"], on_all(a["L1_ffn_ew"]), on_all(a["L1_ffn_act_w"])]
                       + [a["L1_ffn_be"][e[k]] for e in edges for k in range(3)]
                       + [np.zeros((128, 20), np.float32)]),
        "rows": by_row([on_all(a[k]) for k in ("L0_xattn_bv", "L0_xattn_bo", "L1_xattn_bq", "L1_xattn_bk",
                                               "L1_xattn_bv", "L1_xattn_bo", "L1_ffn_ln_g", "L1_ffn_ln_b")]),
    }
    shapes = {"wa": (128, 5, 128), "wc": (128, 4, 128), "wd": (128, 8, NODES, 128), "rows": (128, 8, 128)}
    arrays = {k: v.reshape(shapes.get(k, v.shape)) for k, v in arrays.items()}
    nc = bacc.Bacc("TRN2", target_bir_lowering=False, num_devices=1)
    args = [nc.dram_tensor("in_" + k, v.shape, mybir.dt.from_np(v.dtype), kind="ExternalInput").ap()
            for k, v in arrays.items()]
    out = nc.dram_tensor("out", (T, NB, E), F32, kind="ExternalOutput").ap()
    xattn_ffn_kernel(nc, *args, out)
    r = run_bass_kernel_spmd(nc, [{"in_" + k: v for k, v in arrays.items()}], core_ids=[0])
    return np.ascontiguousarray(r.results[0]["out"].transpose(1, 0, 2))
```

```python
from contextlib import ExitStack

import concourse.bass as bass
from concourse import mybir

F32 = mybir.dt.float32
U8 = mybir.dt.uint8
U32 = mybir.dt.uint32
ALU = mybir.AluOpType
ACT = mybir.ActivationFunctionType
AX_X = mybir.AxisListType.X

NB = 8
T = 128
E = 128
H0, D0 = 16, 8
G1, H1 = 8, 8
NEXP, HID = 8, 256
H3, D3 = 8, 16
NODES = 6
SCALE0 = D0 ** -0.5
SCALE1 = 2 ** -0.5
SCALE3 = D3 ** -0.5
VW0 = 128 + D0
VW3 = 128 + D3


class Batch:

    def __init__(self, reg, off):
        self.reg, self.off = reg, off
        self.n = off if reg is None else 2 * reg + off
        self.p = off % 2
        self.turn = off // 2 if reg is None else reg + off // 2

    def before(self, k):
        off = self.off - k
        if self.reg is None and not 0 <= off < NB:
            return None
        return Batch(self.reg, off)


def over_batches(eng, step, lag, second=None, last=None, first=0):
    ahead = 4 if lag > 2 else 2
    for t in range(first, ahead):
        if t == 1 and second:
            second()
        step(Batch(None, t))
    with eng.Fori(0, (NB - ahead) // 2) as i:
        for off in (ahead, ahead + 1):
            step(Batch(i, off))
    for t in range(NB, NB + lag):
        if t == NB + lag - 1 and last:
            last()
        step(Batch(None, t))


def node_sources(c):
    nsrc = min(c + 1, 5)
    first = sum(min(k + 1, 5) for k in range(c))
    snode = c - nsrc
    return (c, snode + 1, snode + nsrc // 2 + 1), (first + nsrc - 1, first, first + nsrc // 2)


def xattn_ffn_kernel(nc, x_h, ctxT_h, fside_h, mask_h, wa_h, wb_h, wc_h, wd_h, cols_h, rows_h, out_h):
    ctx = ExitStack()
    with ctx:
        def sb(name, shape, dt=F32):
            return ctx.enter_context(nc.sbuf_tensor(name, shape, dt))

        def sem(name):
            return ctx.enter_context(nc.semaphore(name))

        x_all = sb("x_all", [T, NB, E])
        ctxT = sb("ctxT", [E, NB, T])
        mask_u32 = sb("mask_u32", [T, NB * T // 4], U32)
        mask_u8 = mask_u32[:, :].bitcast(U8).rearrange("p (b t) -> p b t", t=T)
        wa = sb("wa", [E, 5, 128])
        wb = sb("wb", [E, 8 + 2 * NEXP * HID // 128 * 128])
        wc = sb("wc", [E, 4, 128])
        wd = sb("wd", [E, 8, NODES, 128])
        cols = sb("cols", [E, 64])
        rows = sb("rows", [T, 8, 128])
        wg = wb[:, 0:NEXP]
        w1 = wb[:, NEXP:NEXP + NEXP * HID].rearrange("p (k m) -> p k m", m=128)
        w2 = wb[:, NEXP + NEXP * HID:].rearrange("p (k m) -> p k m", m=128)
        bq_col, bk_col = cols[:, 0:1], cols[:, 1:2]
        ew = cols[:, 2:20].rearrange("p (c k) -> p c k", k=3)
        act_w = cols[:, 20:26]
        beT = cols[:, 26:44].rearrange("p (c k) -> p c k", k=3)
        bv_row, bo_row, bqkv1_row, bo1_row, g_row, b_row = (
            rows[:, 0, :], rows[:, 1, :], rows[:, 2:5, :], rows[:, 5, :], rows[:, 6, :], rows[:, 7, :])

        ident = sb("ident", [128, 128])
        bk_half = sb("bk_half", [128, 1])
        head0 = sb("head0", [128, H0])
        head3 = sb("head3", [128, H3])
        minus_half = sb("minus_half", [128, NB])
        iota8 = sb("iota8", [128, NEXP])
        half_am = sb("half_am", [T, T])
        pad_all = sb("pad_all", [T, NB, T])

        nodesT = sb("nodesT", [E, NODES + 1, NB, T])
        big_a = sb("big_a", [128, 2, H0 * T])
        big_b = sb("big_b", [128, 2, H0 * T])
        big_c = sb("big_c", [128, 2, H0 * T])
        big_d = sb("big_d", [128, H0 * T])

        def part(tile2, start, *shape):
            size = 1
            for n in shape:
                size *= n
            names = "abcd"[:len(shape)]
            return tile2[:, start:start + size].rearrange(
                "p (%s) -> p %s" % (" ".join(names), " ".join(names)), **dict(zip(names, shape)))

        flat_a, flat_b, flat_c = (t.rearrange("p a b -> p (a b)") for t in (big_a[:, :, :], big_b[:, :, :], big_c[:, :, :]))

        stats = sb("stats", [T, 2, 6])
        mv = sb("mv", [T, 2, 2])
        veps = sb("veps", [T, 2])
        rstd = sb("rstd", [T, 2])
        xn = sb("xn", [T, 2, E])
        xnT = sb("xnT", [E, 2, T])
        stats_a = sb("stats_a", [T, NB, 6])
        mv_a = sb("mv_a", [T, NB, 2])
        veps_a = sb("veps_a", [T, NB])
        rstd_a = sb("rstd_a", [T, NB])

        xn_a, xnT_a = nodesT[:, 1, :, :], nodesT[:, 2, :, :]
        kT_all = nodesT[:, 3, :, :]
        qT_all, v_all = nodesT[:, 4, :, :], nodesT[:, 5, :, :]
        qT = sb("qT", [E, 2, T])
        v_spread = sb("v_spread", [T, 2, 4 * VW0])
        am = sb("am", [T, 2, T])
        fs = part(flat_a, 0, 2, H0, T)
        km = part(flat_b, 0, 2, H0, T)
        nmax = sb("nmax", [T, 2, H0])
        prob = part(flat_c, 0, 2, H0, T)
        den = sb("den", [T, 2, H0])
        rden = sb("rden", [T, 2, H0])
        probT = part(big_d, 0, H0, T)
        rrow = sb("rrow", [T, 2, E])
        r_bc = sb("r_bc", [E, 2, T])
        ctxn = sb("ctxn", [E, 2, T])
        xbo = sb("xbo", [T, 2, E])

        gsm = sb("gsm", [T, 2, 8, NEXP])
        gidx = sb("gidx", [T, 2, 8], U32)
        gcol = sb("gcol", [T, 2, 8])
        comb = sb("comb", [T, 2, NEXP])
        relu_h = part(flat_c, 0, 2, 4, T)
        h2 = part(flat_b, 0, 2, 16, T)

        kv_all = sb("kv_all", [T, NB, 2, E])
        q1 = sb("q1", [T, 2, E])
        pr0 = part(flat_a, 0, 2, 512)
        pr1 = part(flat_a, 1024, 2, 512)
        sc1 = part(flat_a, 2048, 2, 512)
        m1 = sb("m1", [T, 2, 64])
        e1 = part(flat_a, 3072, 2, 512)
        l1 = sb("l1", [T, 2, 64])
        rl1 = sb("rl1", [T, 2, 64])
        ev = part(flat_c, 1024, 2, G1, E)
        ctx1 = sb("ctx1", [T, 2, E])
        ctx1T = sb("ctx1T", [E, 2, T])

        scl = sb("scl", [128, NODES, 4])
        wf = sb("wf", [E, NODES, 4, 128])
        wres = sb("wres", [E, NODES, 128])
        bias3 = sb("bias3", [E, NODES, 3])
        qqk = part(flat_a, 0, NB, 3, T)
        v3 = sb("v3", [T, NB, 2 * VW3])
        km3 = part(flat_b, 0, 3, H3, T)
        nmax3 = sb("nmax3", [T, 2, H3])
        den3 = sb("den3", [T, 2, H3])
        rden3 = sb("rden3", [T, 2, H3])
        p3 = part(flat_c, 0, 2, H3, T)
        p3T = part(big_d, 0, H3, T)
        fin, fin2, xb = part(wb, 0, NB, E), part(wb, NB * E, NB, E), part(wb, 2 * NB * E, NB, E)

        ps = ctx.enter_context(nc.psum_tensor("ps", [128, 8, 512], F32))

        ld = {k: sem("ld_" + k) for k in ("x", "ctx", "mask", "wa", "wb", "wc", "wd", "cols", "rows")}
        fs_landed = [[sem("fs_landed%d%d" % (p, half)) for half in range(2)] for p in range(2)]
        s = {}
        for name in """zeroed ident_ready const_ready v_zeroed iota_ready passed half_am_ready pad_ready
            a_stats a_mv a_veps a_rstd a_xn a_xnT_ps a_xnT a_proj_ps a_bk a_k a_q a_v a_v_ps
            a_am a_bias a_qT a_vs a_km_dve a_km_pool a_s_ps a_nmax a_exp a_rden a_rrow
            a_pT_ps a_pT_act a_pT_dve a_r_ps a_r a_pv_ps a_ctxn a_o_ps a_x a_xbo a_vfree
            kv_ps kv
            b_stats b_mv b_veps b_rstd b_xn b_xnT_ps b_xnT b_gate_ps b_h_ps b_relu b_h2
            b_gmax b_gexp b_rsum b_prob b_top b_idx b_idxf b_gden b_rgden b_w b_c1 b_c2 b_comb b_y_ps b_y
            c_stats c_mv c_veps c_rstd c_xn c_xnT_ps c_xnT c_q_ps c_q c_pr0 c_pr1 c_sc c_m c_sub c_exp
            c_l c_rl c_ev0 c_ev1 c_ctx_ps c_ctx c_ctxT_ps c_ctxT c_o_ps c_xbo c_x
            n_stats n_mv n_veps n_rstd n_xn n_xnT_ps n_xnT
            f_w_ps f_scl f_w f_wres f_b_ps f_bias
            d_proj_ps d_qqk d_v d_km d_s_ps d_max d_exp d_rden d_rrow d_pT_ps d_pT_act d_pT_dve d_r_ps d_r
            d_pv_ps d_ctxn d_o_ps d_node
            e_T_ps e_fin e_stats e_mv e_veps e_rstd e_g e_xb e_out out_done""".split():
            s[name] = sem(name)

        block = ctx.enter_context(nc.Block())

        def spread0(tile2):
            return tile2.rearrange("p (v x) -> p v x", x=VW0)[:, :, 0:128].rearrange(
                "p v (j u d) -> p v j u d", u=4, d=D0)[:, :, :, 0, :]

        def spread3(tile2):
            return tile2.rearrange("p (v x) -> p v x", x=VW3)[:, :, 0:128].rearrange(
                "p v (j u d) -> p v j u d", u=2, d=D3)[:, :, :, 0, :]

        FOLD_BANKS = (4, 5, 7)
        ITEMS = [(c, b) for c in range(NODES) for b in range(NB)]
        NI = len(ITEMS)

        def over_items(step):
            for t in range(NI + 8):
                step(lambda k, t=t: t - k if 0 <= t - k < NI else None)

        def to_norm(at, k):
            i = at(-k)
            return i if i is not None and k <= i < NB else None

        def to_finish(at, k):
            i = at(k)
            return i % NB if i is not None and i // NB == NODES - 1 else None

        @block.sync
        def _(sp):
            sp.dma_start(x_all[:, :, :], x_h).then_inc(ld["x"], 16)
            sp.dma_start(ctxT[:, :, :], ctxT_h).then_inc(ld["ctx"], 16)
            sp.dma_start(wa[:, :, :], wa_h).then_inc(ld["wa"], 16)
            sp.dma_start(cols[:, :], cols_h).then_inc(ld["cols"], 16)
            sp.dma_start(rows[:, :, :], rows_h).then_inc(ld["rows"], 16)
            sp.dma_start(mask_u32[:, :], mask_h).then_inc(ld["mask"], 16)

            def step(t):
                if (b := t.before(0)) is not None:
                    for half in range(2):
                        if b.reg is not None or b.off >= 2:
                            sp.wait_ge(s["a_exp"], 4 * b.n + 2 * half - 6)
                        sp.dma_start(fs[:, b.p, 8 * half:8 * half + 8, :],
                                     fside_h[b.n][:, 8 * half:8 * half + 8, :]).then_inc(fs_landed[b.p][half], 16)

            for t in range(2):
                step(Batch(None, t))
            sp.dma_start(wc[:, :, :], wc_h).then_inc(ld["wc"], 16)
            sp.dma_start(wb[:, :], wb_h).then_inc(ld["wb"], 16)
            sp.dma_start(wd[:, :, :, :], wd_h).then_inc(ld["wd"], 16)
            with sp.Fori(0, NB // 2 - 1) as i:
                for off in (2, 3):
                    step(Batch(i, off))
            for b in range(NB):
                sp.wait_ge(s["e_out"], b + 1)
                sp.dma_start(out_h[:, b, :], fin2[:, b, :]).then_inc(s["out_done"], 16)
            sp.wait_ge(s["out_done"], 16 * NB)

        @block.gpsimd
        def _(pool):
            pool.memset(ident[:, :], 0.0).then_inc(s["zeroed"], 1)
            pool.memset(head0[:, :], 1.0).then_inc(s["zeroed"], 1)
            pool.memset(head3[:, :], 1.0).then_inc(s["zeroed"], 1)
            pool.memset(minus_half[:, :], -0.5).then_inc(s["zeroed"], 1)
            pool.wait_ge(s["zeroed"], 4)
            pool.affine_select(out=ident[:, :], in_=ident[:, :], compare_op=ALU.not_equal, fill=1.0,
                               base=0, pattern=[[-1, 128]], channel_multiplier=1).then_inc(s["ident_ready"], 1)
            for tile, heads, width in ((head0, H0, D0), (head3, H3, D3)):
                pool.affine_select(out=tile[:, :], in_=tile[:, :], compare_op=ALU.is_ge, fill=0.0, base=0,
                                   pattern=[[-width, heads]], channel_multiplier=1).then_inc(s["zeroed"], 1)
            pool.wait_ge(s["zeroed"], 6)
            for tile, heads, width in ((head0, H0, D0), (head3, H3, D3)):
                pool.affine_select(out=tile[:, :], in_=tile[:, :], compare_op=ALU.is_ge, fill=0.0,
                                   base=width - 1, pattern=[[width, heads]],
                                   channel_multiplier=-1).then_inc(s["const_ready"], 1)
            pool.wait_ge(s["a_veps"], 1)
            pool.tensor_tensor(rstd_a[:, :], veps_a[:, :], minus_half[:, :], ALU.pow).then_inc(s["a_rstd"], 1)
            pool.wait_ge(ld["mask"], 16)
            pool.tensor_scalar(pad_all[:, :, :], mask_u8, -3.0e38, 3.0e38, ALU.mult,
                               ALU.mult).then_inc(s["pad_ready"], 1)
            pool.wait_ge(s["pad_ready"], 1)
            pool.wait_ge(s["half_am_ready"], 1)
            pool.wait_ge(s["const_ready"], 2)

            def attn0(t):
                if (b := t.before(0)) is not None:
                    pool.wait_ge(s["a_k"], 2)
                    pool.wait_ge(s["a_s_ps"], 4 * b.n + 4)
                    pool.tensor_tensor(km[:, b.p, 8:16, :],
                                       kT_all[:, b.n, :].unsqueeze(1).to_broadcast([E, 8, T]),
                                       head0[:, 8:16].unsqueeze(2).to_broadcast([E, 8, T]),
                                       ALU.mult).then_inc(s["a_km_pool"], 1)
                if (b := t.before(2)) is not None:
                    pool.wait_ge(s["a_x"], b.n + 1)
                    pool.wait_ge(ld["rows"], 16)
                    pool.tensor_tensor(xbo[:, b.p, :], x_all[:, b.n, :], bo_row, ALU.add).then_inc(s["a_xbo"], 1)
                if (b := t.before(0)) is not None:
                    pool.wait_ge(s["a_bias"], 2 * b.n + 2)
                    pool.tensor_tensor(am[:, b.p, :], half_am[:, :], pad_all[:, b.n, :],
                                       ALU.add).then_inc(s["a_am"], 1)
                    pool.wait_ge(s["a_am"], b.n + 1)
                    for half in range(2):
                        pool.wait_ge(fs_landed[b.p][half], 16 * (b.turn + 1))
                        heads = fs[:, b.p, 8 * half:8 * half + 8, :]
                        pool.tensor_tensor(heads, heads, am[:, b.p, :].unsqueeze(1).to_broadcast([T, 8, T]),
                                           ALU.add).then_inc(s["a_bias"], 1)

            pool.sem_inc(s["a_bias"], 4)
            over_batches(pool, attn0, 2)

            def rstd_of(name, b):
                pool.wait_ge(s[name + "_veps"], b.n + 1)
                pool.tensor_tensor(rstd[:, b.p:b.p + 1], veps[:, b.p:b.p + 1], minus_half[:, 0:1],
                                   ALU.pow).then_inc(s[name + "_rstd"], 1)

            def moe(t):
                if (b := t.before(0)) is not None:
                    rstd_of("b", b)

            over_batches(pool, moe, 0)

            def attn1(t):
                if (b := t.before(2)) is not None:
                    pool.wait_ge(s["c_exp"], b.n + 1)
                    pool.wait_ge(s["c_ctx_ps"], b.n + 1)
                    vv = kv_all[:, b.n, 1, :].rearrange("p (s h e) -> p h s e", h=H1, e=2)[:, :, :, 1]
                    pool.tensor_tensor(
                        ev[:, b.p, :, :].rearrange("p s (l h e) -> p l h s e", h=H1, e=2)[:, :, :, :, 1],
                        e1[:, b.p, :].rearrange("p (l h s) -> p l h s", h=H1, s=G1),
                        vv.unsqueeze(1).to_broadcast([T, G1, H1, G1]), ALU.mult).then_inc(s["c_ev1"], 1)
                    pool.wait_ge(s["c_x"], b.n + 1)
                    pool.tensor_tensor(xbo[:, b.p, :], x_all[:, b.n, :], bo1_row, ALU.add).then_inc(s["c_xbo"], 1)
                if (b := t.before(0)) is not None:
                    rstd_of("c", b)
                    pool.wait_ge(s["c_q"], b.n + 2)
                    pool.wait_ge(s["c_sc"], b.n + 1)
                    qv = q1[:, b.p, :].rearrange("p (l h e) -> p l h e", h=H1, e=2)[:, :, :, 1]
                    kv = kv_all[:, b.n, 0, :].rearrange("p (s h e) -> p h s e", h=H1, e=2)[:, :, :, 1]
                    pool.tensor_tensor(
                        pr1[:, b.p, :].rearrange("p (l h s) -> p l h s", h=H1, s=G1),
                        qv.unsqueeze(3).to_broadcast([T, G1, H1, G1]),
                        kv.unsqueeze(1).to_broadcast([T, G1, H1, G1]), ALU.mult).then_inc(s["c_pr1"], 1)

            def norm3(b):
                rstd_of("n", Batch(None, b))

            def norm3_start():
                for b in range(2):
                    norm3(b)

            over_batches(pool, attn1, 2, last=norm3_start)

            def nodes(at):
                if (b := to_norm(at, 2)) is not None:
                    norm3(b)
                if (i := at(0)) is not None:
                    c, b = ITEMS[i]
                    pool.wait_ge(s["d_qqk"], i + 1)
                    if i >= 3:
                        pool.wait_ge(s["d_s_ps"], 2 * (i - 2))
                    pool.tensor_tensor(km3[:, i % 3, :, :],
                                       qqk[:, b, 2, :].unsqueeze(1).to_broadcast([E, H3, T]),
                                       head3[:, :].unsqueeze(2).to_broadcast([E, H3, T]),
                                       ALU.mult).then_inc(s["d_km"], 1)
                if (b := to_finish(at, 7)) is not None:
                    pool.tensor_tensor(xb[:, b, :], x_all[:, b, :], b_row, ALU.add).then_inc(s["e_xb"], 1)
                    pool.wait_ge(s["e_veps"], b + 1)
                    pool.tensor_tensor(rstd_a[:, b:b + 1], veps_a[:, b:b + 1], minus_half[:, 0:1],
                                       ALU.pow).then_inc(s["e_rstd"], 1)

            over_items(nodes)

        @block.tensor
        def _(pe):
            pe.wait_ge(s["ident_ready"], 1)
            pe.wait_ge(ld["wa"], 16)
            pe.wait_ge(ld["ctx"], 16)
            for n in range(2):
                pe.matmul(ps[:, 4 + n, :], wa[:, 1, :], ctxT[:, 4 * n:4 * n + 4, :],
                          start=True, stop=True).then_inc(s["a_proj_ps"], 1)
            for b in range(NB):
                last = pe.matmul(ps[:, 6 + b // 4, 128 * (b % 4):128 * (b % 4) + 128], ctxT[:, b, :], wa[:, 2, :],
                                 start=True, stop=True)
                if b % 4 == 3:
                    last.then_inc(s["a_v_ps"], 1)
            for b in range(NB):
                pe.wait_ge(s["a_xn"], b + 1)
                pe.transpose(ps[:, b // 4, 128 * (b % 4):128 * (b % 4) + 128], xn_a[:, b, :],
                             ident[:, :]).then_inc(s["a_xnT_ps"], 1)
            for n in range(2):
                pe.wait_ge(s["a_xnT"], n + 1)
                pe.matmul(ps[:, 2 + n, :], wa[:, 0, :], xnT_a[:, 4 * n:4 * n + 4, :],
                          start=True, stop=True).then_inc(s["a_proj_ps"], 1)
            pe.wait_ge(s["a_q"], 2)
            pe.wait_ge(s["a_v"], 2)
            pe.wait_ge(s["a_k"], 2)
            pe.sem_inc(s["a_s_ps"], 8)
            pe.sem_inc(s["a_pT_ps"], 4)
            pe.sem_inc(s["a_pv_ps"], 1)

            def attn0(t):
                front, back, done = t.before(1), t.before(2), t.before(3)

                def scores(b, k):
                    if k == 0:
                        pe.wait_ge(s["a_qT"], b.n + 1)
                        pe.wait_ge(s["a_km_dve"], b.n + 1)
                    if k == 2:
                        pe.wait_ge(s["a_km_pool"], b.n + 1)
                    pe.wait_ge(s["a_nmax"], 4 * b.n + k + 1)
                    pe.matmul(ps[:, k, :], qT[:, b.p, :], km[:, b.p, 4 * k:4 * k + 4, :],
                              start=True, stop=True).then_inc(s["a_s_ps"], 1)

                def turn(b, k):
                    pe.wait_ge(s["a_exp"], 4 * b.n + k + 1)
                    pe.wait_ge(s["a_pT_dve" if k % 2 == 0 else "a_pT_act"], 2 * b.n + k // 2 + 2)
                    for h in range(4):
                        last = pe.transpose(ps[:, 4 + k % 2, 128 * h:128 * h + 128], prob[:, b.p, 4 * k + h, :],
                                            ident[:, :])
                    last.then_inc(s["a_pT_ps"], 1)

                if front is not None:
                    scores(front, 0)
                    scores(front, 1)
                if done is not None:
                    b = done
                    pe.wait_ge(s["a_vs"], b.n + 1)
                    pe.wait_ge(s["a_pT_dve"], 2 * b.n + 4)
                    pe.wait_ge(s["a_pT_act"], 2 * b.n + 4)
                    pe.wait_ge(s["a_x"], b.n + 2)
                    for u in range(4):
                        for j in range(4):
                            last = pe.matmul(ps[32 * j:32 * j + 32, 7, 0:128],
                                             v_spread[:, b.p, 128 * u + 32 * j:128 * u + 32 * j + 32],
                                             probT[:, 4 * j + u, :], start=(u == 0), stop=(u == 3))
                    last.then_inc(s["a_pv_ps"], 1)
                if back is not None:
                    turn(back, 0)
                    turn(back, 1)
                if done is not None:
                    pe.wait_ge(s["a_ctxn"], done.n + 1)
                    pe.matmul(ps[:, 7, 128:256], ctxn[:, done.p, :], wa[:, 3, :],
                              start=True, stop=True).then_inc(s["a_o_ps"], 1)
                if front is not None:
                    scores(front, 2)
                if back is not None:
                    turn(back, 2)
                    turn(back, 3)
                    pe.wait_ge(s["a_rrow"], back.n + 1)
                    pe.wait_ge(s["a_r"], back.n + 1)
                    pe.transpose(ps[:, 6, 0:128], rrow[:, back.p, :], ident[:, :]).then_inc(s["a_r_ps"], 1)
                if front is not None:
                    scores(front, 3)

            def keys_values1():
                pe.wait_ge(ld["wc"], 16)
                pe.wait_ge(s["a_nmax"], 4 * NB + 4)
                for b in range(NB):
                    last = pe.matmul(ps[:, b // 2, 256 * (b % 2):256 * (b % 2) + 256], ctxT[:, b, :],
                                     wc[:, 1:3, :], start=True, stop=True)
                    if b % 2:
                        last.then_inc(s["kv_ps"], 1)

            over_batches(pe, attn0, 3, last=keys_values1)
            pe.wait_ge(ld["wb"], 16)
            pe.wait_ge(s["kv"], 4)
            pe.wait_ge(s["a_r"], NB + 1)

            def fold_weights():
                pe.wait_ge(ld["wd"], 16)
                pe.wait_ge(ld["cols"], 16)
                pe.wait_ge(s["a_pT_dve"], 2 * NB + 2)
                pe.wait_ge(s["a_pT_act"], 2 * NB + 2)
                pe.wait_ge(s["a_x"], NB + 2)
                for c in range(NODES):
                    bank = FOLD_BANKS[c % 3]
                    if c >= 3:
                        pe.wait_ge(s["f_w"], c - 2)
                    pe.matmul(ps[:, bank, 0:128], wd[:, 0, c, :], wd[:, 4, c, :], start=True, stop=True)
                    pe.matmul(ps[:, bank, 128:256], wd[:, 1, c, :], wd[:, 5, c, :], start=True, stop=True)
                    pe.matmul(ps[:, bank, 256:384], wd[:, 2, c, :], wd[:, 6, c, :], start=True, stop=True)
                    pe.matmul(ps[:, bank, 384:512], beT[:, c, 2:3].to_broadcast([E, 128]), wd[:, 6, c, :],
                              start=True, stop=True).then_inc(s["f_w_ps"], 1)
                pe.wait_ge(s["f_w"], NODES)
                for c in range(NODES):
                    pe.matmul(ps[:, 7, 2 * c:2 * c + 1], wd[:, 4, c, :], beT[:, c, 0:1], start=True, stop=True)
                    last = pe.matmul(ps[:, 7, 2 * c + 1:2 * c + 2], wd[:, 5, c, :], beT[:, c, 1:2],
                                     start=True, stop=True)
                last.then_inc(s["f_b_ps"], 1)

            def moe(t):
                front, back = t.before(1), t.before(2)

                def experts_out(b, e):
                    pe.wait_ge(s["b_h2"], 4 * b.n + e // 2 + 1)
                    if e % 4 == 0:
                        pe.wait_ge(s["b_y"], 8 * b.n + 4 + e)
                    for k in (2 * e, 2 * e + 1):
                        last = pe.matmul(ps[:, 4 + e // 4, 128 * (e % 4):128 * (e % 4) + 128], h2[:, b.p, k, :],
                                         w2[:, k, :], start=(k % 2 == 0), stop=(k % 2 == 1))
                    if e % 4 == 3:
                        last.then_inc(s["b_y_ps"], 1)

                def experts_in(b, k):
                    if b.reg is not None or b.off >= 1:
                        pe.wait_ge(s["b_h2"], 4 * b.n + k - 3)
                    for m in range(4):
                        last = pe.matmul(ps[:, k, 128 * m:128 * m + 128], w1[:, 4 * k + m, :], xnT[:, b.p, :],
                                         start=True, stop=True)
                    last.then_inc(s["b_h_ps"], 1)

                if front is not None:
                    pe.wait_ge(s["b_xnT"], front.n + 1)
                    pe.matmul(ps[:, 6, 128:128 + NEXP], xnT[:, front.p, :], wg, start=True,
                              stop=True).then_inc(s["b_gate_ps"], 1)
                for k in range(4):
                    if front is not None:
                        experts_in(front, k)
                    if back is not None:
                        experts_out(back, 2 * k)
                        experts_out(back, 2 * k + 1)
                if (b := t.before(0)) is not None:
                    pe.wait_ge(s["b_xn"], b.n + 1)
                    pe.wait_ge(s["b_gexp"], b.n + 1)
                    pe.transpose(ps[:, 6, 0:128], xn[:, b.p, :], ident[:, :]).then_inc(s["b_xnT_ps"], 1)

            def attn1(t):
                cur, front, back = t.before(0), t.before(1), t.before(2)
                if front is not None:
                    b = front
                    pe.wait_ge(s["c_pr0"], b.n + 1)
                    pe.wait_ge(s["c_sub"], b.n + 1)
                    pe.matmul(ps[:, 2, :], ident[:, :], pr0[:, b.p, :], start=True, stop=False)
                    pe.wait_ge(s["c_pr1"], b.n + 1)
                    pe.matmul(ps[:, 2, :], ident[:, :], pr1[:, b.p, :], start=False,
                              stop=True).then_inc(s["c_sc"], 1)
                if back is not None:
                    b = back
                    pe.wait_ge(s["c_ev0"], b.n + 1)
                    pe.wait_ge(s["c_ev1"], b.n + 1)
                    pe.wait_ge(s["c_ctx"], b.n + 1)
                    for g in range(G1):
                        last = pe.matmul(ps[:, 3, 0:128], ident[:, :], ev[:, b.p, g, :],
                                         start=(g == 0), stop=(g == G1 - 1))
                    last.then_inc(s["c_ctx_ps"], 1)
                    pe.wait_ge(s["c_ctx"], b.n + 2)
                    pe.wait_ge(s["c_x"], b.n + 2)
                    pe.transpose(ps[:, 4, 0:128], ctx1[:, b.p, :], ident[:, :]).then_inc(s["c_ctxT_ps"], 1)
                if cur is not None:
                    b = cur
                    pe.wait_ge(s["c_xn"], b.n + 1)
                    pe.wait_ge(s["c_q"], b.n + 1)
                    pe.transpose(ps[:, 0, 0:128], xn[:, b.p, :], ident[:, :]).then_inc(s["c_xnT_ps"], 1)
                if back is not None:
                    b = back
                    pe.wait_ge(s["c_ctxT"], b.n + 1)
                    pe.matmul(ps[:, 4, 128:256], ctx1T[:, b.p, :], wc[:, 3, :], start=True,
                              stop=True).then_inc(s["c_o_ps"], 1)
                if cur is not None:
                    b = cur
                    pe.wait_ge(s["c_xnT"], b.n + 1)
                    pe.matmul(ps[:, 0, 128:256], xnT[:, b.p, :], wc[:, 0, :], start=True,
                              stop=True).then_inc(s["c_q_ps"], 1)

            def attn1_start():
                pe.wait_ge(s["b_h2"], 4 * NB)
                pe.sem_inc(s["c_sc"], 2)
                pe.sem_inc(s["c_ctx_ps"], 2)
                attn1(Batch(None, 0))

            def norm3(b):
                pe.wait_ge(s["n_xn"], b + 1)
                if b >= 1:
                    pe.wait_ge(s["n_xnT"], b)
                pe.transpose(ps[:, 7, 384:512], xn[:, b % 2, :], ident[:, :]).then_inc(s["n_xnT_ps"], 1)

            over_batches(pe, moe, 2, second=fold_weights, last=attn1_start)
            pe.wait_ge(s["b_y"], 8 * NB + 8)
            over_batches(pe, attn1, 2, last=lambda: norm3(0), first=1)
            pe.wait_ge(s["c_x"], NB + 2)
            pe.wait_ge(s["f_wres"], 1)

            def nodes(at):
                def turn(i, k):
                    pe.wait_ge(s["d_exp"], 8 * i + 4 * k + 4)
                    if i >= 1:
                        pe.wait_ge(s["d_pT_act" if k else "d_pT_dve"], i)
                    for h in range(4):
                        last = pe.transpose(ps[:, 4 + k, 128 * h:128 * h + 128], p3[:, i % 2, 4 * k + h, :],
                                            ident[:, :])
                    last.then_inc(s["d_pT_ps"], 1)

                back = at(4)
                if back is not None:
                    turn(back, 0)
                if (i := at(0)) is not None:
                    c, b = ITEMS[i]
                    (sq, sk, sv), _ = node_sources(c)
                    if c:
                        pe.wait_ge(s["d_node"], i - NB + 1)
                    else:
                        pe.wait_ge(s["n_xnT"], b + 1)
                    if i >= 1:
                        pe.wait_ge(s["d_v"], i)
                    pe.matmul(ps[:, 6, 0:128], wres[:, c, :], nodesT[:, sq, b, :], start=True, stop=True)
                    pe.matmul(ps[:, 6, 128:256], wf[:, c, 0, :], nodesT[:, sq, b, :], start=True, stop=True)
                    pe.matmul(ps[:, 6, 256:384], wf[:, c, 1, :], nodesT[:, sk, b, :], start=True, stop=True)
                    pe.matmul(ps[:, 6, 384:512], nodesT[:, sv, b, :], wf[:, c, 2, :], start=True,
                              stop=True).then_inc(s["d_proj_ps"], 1)
                if (i := at(5)) is not None:
                    c, b = ITEMS[i]
                    pe.wait_ge(s["d_ctxn"], i + 1)
                    pe.matmul(ps[:, 7, 256:384], wd[:, 3, c, :], ctxn[:, i % 2, :], start=True,
                              stop=True).then_inc(s["d_o_ps"], 1)
                if back is not None:
                    turn(back, 1)

                def scores(i, k):
                    c, b = ITEMS[i]
                    pe.wait_ge(s["d_km"], i + 1)
                    if i >= 2:
                        pe.wait_ge(s["d_exp"], 8 * (i - 2) + 4 * k + 4)
                    pe.matmul(ps[:, 2 * (i % 2) + k, :], qqk[:, b, 1, :], km3[:, i % 3, 4 * k:4 * k + 4, :],
                              start=True, stop=True).then_inc(s["d_s_ps"], 1)

                if (i := at(2)) is not None:
                    scores(i, 0)
                if back is not None:
                    pe.wait_ge(s["d_rrow"], back + 1)
                    if back >= 1:
                        pe.wait_ge(s["d_node"], back)
                    pe.transpose(ps[:, 7, 128:256], rrow[:, back % 2, :], ident[:, :]).then_inc(s["d_r_ps"], 1)
                if (b := to_norm(at, 1)) is not None:
                    norm3(b)
                if (b := to_finish(at, 6)) is not None:
                    pe.wait_ge(s["d_node"], min(NI - NB + b + 2, NI))
                    if b >= 1:
                        pe.wait_ge(s["e_fin"], b)
                    pe.transpose(ps[:, 7, 384:512], nodesT[:, NODES, b, :], ident[:, :]).then_inc(s["e_T_ps"], 1)
                if (i := at(2)) is not None:
                    scores(i, 1)
                if back is not None:
                    b = back % NB
                    pe.wait_ge(s["d_pT_dve"], back + 1)
                    pe.wait_ge(s["d_pT_act"], back + 1)
                    pe.wait_ge(s["d_r"], back + 1)
                    if (n := to_norm(at, 1)) is not None:
                        pe.wait_ge(s["n_xnT"], n + 1)
                    if (n := to_finish(at, 6)) is not None:
                        pe.wait_ge(s["e_fin"], n + 1)
                    for u in range(2):
                        for j in range(4):
                            last = pe.matmul(ps[32 * j:32 * j + 32, 7, 0:128],
                                             v3[:, b, 128 * u + 32 * j:128 * u + 32 * j + 32],
                                             p3T[:, 2 * j + u, :], start=(u == 0), stop=(u == 1))
                    last.then_inc(s["d_pv_ps"], 1)

            over_items(nodes)
        @block.scalar
        def _(act):
            act.wait_ge(ld["wa"], 16)
            act.activation(half_am[:, :], wa[:, 4, :], ACT.Copy, scale=0.5).then_inc(s["half_am_ready"], 1)
            act.wait_ge(ld["cols"], 16)
            act.activation(bk_half[:, :], bk_col, ACT.Copy, scale=0.5 * SCALE0).then_inc(s["a_bk"], 1)
            act.wait_ge(s["a_bk"], 1)
            for n in range(2):
                act.wait_ge(s["a_proj_ps"], n + 1)
                act.activation(kT_all[:, 4 * n:4 * n + 4, :], ps[:, 4 + n, :], ACT.Identity, bias=bk_half[:, 0:1],
                               scale=0.5 * SCALE0).then_inc(s["a_k"], 1)
            for n in range(2):
                act.wait_ge(s["a_xnT_ps"], 4 * n + 4)
                act.activation(xnT_a[:, 4 * n:4 * n + 4, :], ps[:, n, :], ACT.Copy).then_inc(s["a_xnT"], 1)
                act.wait_ge(s["a_proj_ps"], 3 + n)
                act.activation(qT_all[:, 4 * n:4 * n + 4, :], ps[:, 2 + n, :], ACT.Identity,
                               bias=bq_col).then_inc(s["a_q"], 1)
            act.sem_inc(s["a_pT_act"], 2)
            act.sem_inc(s["a_r"], 1)

            def attn0(t):
                front, back = t.before(1), t.before(2)

                def turned(b, k):
                    act.wait_ge(s["a_pT_ps"], 4 * b.n + k + 5)
                    act.wait_ge(s["a_pv_ps"], b.n + 1)
                    act.activation(probT[:, 4 * k:4 * k + 4, :], ps[:, 5, :], ACT.Copy).then_inc(s["a_pT_act"], 1)

                def exps(b, k):
                    act.wait_ge(s["a_nmax"], 4 * b.n + k + 5)
                    for h in range(4 * k, 4 * k + 4):
                        last = act.activation(prob[:, b.p, h, :], fs[:, b.p, h, :], ACT.Exp, scale=-1.0,
                                              bias=nmax[:, b.p, h:h + 1], accum_out=den[:, b.p, h:h + 1])
                    last.then_inc(s["a_exp"], 1)

                if front is not None:
                    if front.reg is not None or front.off >= 1:
                        act.wait_ge(s["a_rden"], front.n)
                        act.wait_ge(s["a_pT_ps"], 4 * front.n)
                    exps(front, 0)
                if back is not None:
                    turned(back, 1)
                if front is not None:
                    exps(front, 1)
                    exps(front, 2)
                if back is not None:
                    turned(back, 3)
                    act.wait_ge(s["a_r_ps"], back.n + 1)
                    act.activation(r_bc[:, back.p, :], ps[:, 6, 0:128], ACT.Copy).then_inc(s["a_r"], 1)
                if front is not None:
                    exps(front, 3)

            over_batches(act, attn0, 2)

            def moe(t):
                if (b := t.before(1)) is not None:
                    act.wait_ge(s["b_gmax"], b.n + 1)
                    act.activation(gsm[:, b.p, 0, :], ps[:, 6, 128:128 + NEXP], ACT.Exp, bias=gcol[:, b.p, 0:1],
                                   accum_out=gcol[:, b.p, 1:2]).then_inc(s["b_gexp"], 1)
                    for k in range(4):
                        act.wait_ge(s["b_h_ps"], 4 * b.n + k + 1)
                        if b.reg is not None or b.off >= 1 or k >= 2:
                            act.wait_ge(s["b_h2"], 4 * b.n + k - 1)
                        act.activation(relu_h[:, k % 2, :, :], ps[:, k, :], ACT.Relu).then_inc(s["b_relu"], 1)
                if (b := t.before(0)) is not None:
                    act.wait_ge(s["b_xnT_ps"], b.n + 1)
                    act.activation(xnT[:, b.p, :], ps[:, 6, 0:128], ACT.Copy).then_inc(s["b_xnT"], 1)

            act.sem_inc(s["b_gexp"], 1)
            over_batches(act, moe, 1)

            def attn1(t):
                if (b := t.before(1)) is not None:
                    act.wait_ge(s["c_sub"], b.n + 2)
                    act.activation(e1[:, b.p, :], sc1[:, b.p, :], ACT.Exp, scale=SCALE1).then_inc(s["c_exp"], 1)
                if (b := t.before(2)) is not None:
                    act.wait_ge(s["c_ctxT_ps"], b.n + 1)
                    act.activation(ctx1T[:, b.p, :], ps[:, 4, 0:128], ACT.Copy).then_inc(s["c_ctxT"], 1)
                if (b := t.before(0)) is not None:
                    act.wait_ge(s["c_xnT_ps"], b.n + 1)
                    act.activation(xnT[:, b.p, :], ps[:, 0, 0:128], ACT.Copy).then_inc(s["c_xnT"], 1)

            def norm3(b):
                act.wait_ge(s["n_xnT_ps"], b + 1)
                act.activation(nodesT[:, 0, b, :], ps[:, 7, 384:512], ACT.Copy).then_inc(s["n_xnT"], 1)

            over_batches(act, attn1, 2, last=lambda: norm3(0))

            def nodes(at):
                def exps(i, k):
                    act.wait_ge(s["d_max"], 2 * i + k + 1)
                    if i >= 2:
                        act.wait_ge(s["d_pT_ps"], 2 * i - 3 + k)
                        act.wait_ge(s["d_rden"], i - 1)
                    for h in range(4):
                        act.activation(p3[:, i % 2, 4 * k + h, :],
                                       ps[:, 2 * (i % 2) + k, 128 * h:128 * h + 128], ACT.Exp,
                                       bias=nmax3[:, i % 2, 4 * k + h:4 * k + h + 1],
                                       accum_out=den3[:, i % 2, 4 * k + h:4 * k + h + 1]).then_inc(s["d_exp"], 1)

                if (i := at(3)) is not None:
                    exps(i, 0)
                if (i := at(4)) is not None:
                    act.wait_ge(s["d_pT_ps"], 2 * i + 2)
                    if i >= 1:
                        act.wait_ge(s["d_pv_ps"], i)
                    act.activation(p3T[:, 4:8, :], ps[:, 5, :], ACT.Copy).then_inc(s["d_pT_act"], 1)
                if (b := to_norm(at, 1)) is not None:
                    act.wait_ge(s["n_xnT_ps"], b + 1)
                if (b := to_finish(at, 6)) is not None:
                    act.wait_ge(s["e_T_ps"], b + 1)
                if (i := at(4)) is not None:
                    act.wait_ge(s["d_r_ps"], i + 1)
                    act.activation(r_bc[:, i % 2, :], ps[:, 7, 128:256], ACT.Copy).then_inc(s["d_r"], 1)
                if (b := to_norm(at, 1)) is not None:
                    norm3(b)
                if (b := to_finish(at, 6)) is not None:
                    act.activation(fin[:, b, :], ps[:, 7, 384:512], ACT.Copy).then_inc(s["e_fin"], 1)
                if (i := at(3)) is not None:
                    exps(i, 1)

            over_items(nodes)

        @block.vector
        def _(dve):
            for k in range(NEXP):
                dve.memset(iota8[:, k:k + 1], float(k)).then_inc(s["iota_ready"], 1)
            for tile in (v_spread, v3):
                dve.memset(tile[:, :, :], 0.0).then_inc(s["v_zeroed"], 1)
            dve.wait_ge(ld["x"], 16)
            for b in range(NB):
                dve.bn_stats(stats_a[:, b, :], x_all[:, b, :]).then_inc(s["a_stats"], 1)
            for b in range(NB):
                dve.wait_ge(s["a_stats"], b + 1)
                dve.bn_aggr(mv_a[:, b, :], stats_a[:, b, :]).then_inc(s["a_mv"], 1)
            dve.wait_ge(s["a_mv"], NB)
            dve.tensor_scalar(veps_a[:, :], mv_a[:, :, 1], 1e-5, None, ALU.add).then_inc(s["a_veps"], 1)
            dve.wait_ge(s["a_rstd"], 1)
            for b in range(NB):
                dve.tensor_scalar(xn_a[:, b, :], x_all[:, b, :], mv_a[:, b, 0:1], rstd_a[:, b:b + 1],
                                  ALU.subtract, ALU.mult).then_inc(s["a_xn"], 1)
            dve.wait_ge(ld["rows"], 16)
            for n in range(2):
                dve.wait_ge(s["a_v_ps"], n + 1)
                dve.tensor_tensor(v_all[:, 4 * n:4 * n + 4, :], ps[:, 6 + n, :].rearrange("p (b e) -> p b e", e=E),
                                  bv_row.unsqueeze(1).to_broadcast([T, 4, E]), ALU.add).then_inc(s["a_v"], 1)
            dve.wait_ge(s["const_ready"], 2)
            dve.wait_ge(s["v_zeroed"], 1)
            dve.wait_ge(s["a_v"], 2)
            dve.sem_inc(s["a_nmax"], 4)
            dve.sem_inc(s["a_pT_dve"], 2)
            dve.sem_inc(s["a_x"], 2)
            dve.sem_inc(s["a_rden"], 1)

            def attn0(t):
                front, back, done = t.before(1), t.before(2), t.before(3)

                def turned(b, k):
                    dve.wait_ge(s["a_pT_ps"], 4 * b.n + k + 5)
                    dve.wait_ge(s["a_pv_ps"], b.n + 1)
                    dve.tensor_copy(probT[:, 4 * k:4 * k + 4, :].rearrange("p h t -> p (h t)"),
                                    ps[:, 4, :]).then_inc(s["a_pT_dve"], 1)

                def neg_scores(b, k):
                    dve.wait_ge(s["a_s_ps"], 4 * b.n + k + 9)
                    if k % 2 == 0:
                        dve.wait_ge(s["a_bias"], 2 * b.n + k // 2 + 5)
                    dve.sem_inc(s["passed"], 1)
                    for h in range(4 * k, 4 * k + 4):
                        last = dve.tensor_tensor_reduce(
                            fs[:, b.p, h, :], ps[:, k, 128 * (h % 4):128 * (h % 4) + 128], fs[:, b.p, h, :],
                            -2.0, 3.0e38, ALU.add, ALU.min, nmax[:, b.p, h:h + 1])
                    last.then_inc(s["a_nmax"], 1)

                if front is not None:
                    neg_scores(front, 0)
                    neg_scores(front, 1)
                if done is not None:
                    dve.wait_ge(s["a_pv_ps"], done.n + 2)
                    dve.wait_ge(s["a_r"], done.n + 2)
                    dve.tensor_tensor(ctxn[:, done.p, :], ps[:, 7, 0:128], r_bc[:, done.p, :],
                                      ALU.mult).then_inc(s["a_ctxn"], 1)
                if back is not None:
                    dve.wait_ge(s["a_exp"], 4 * back.n + 4)
                    dve.reciprocal(rden[:, back.p, :], den[:, back.p, :]).then_inc(s["a_rden"], 1)
                    turned(back, 0)
                    dve.wait_ge(s["a_rden"], back.n + 2)
                    dve.tensor_copy(rrow[:, back.p, :].rearrange("p (h d) -> p h d", d=D0),
                                    rden[:, back.p, :].unsqueeze(2).to_broadcast([T, H0, D0])).then_inc(s["a_rrow"], 1)
                if done is not None:
                    dve.wait_ge(s["a_o_ps"], done.n + 1)
                    dve.wait_ge(s["a_xbo"], done.n + 1)
                    dve.tensor_tensor(x_all[:, done.n, :], ps[:, 7, 128:256], xbo[:, done.p, :],
                                      ALU.add).then_inc(s["a_x"], 1)
                if front is not None:
                    b = front
                    if b.reg is not None or b.off >= 1:
                        dve.wait_ge(s["a_pv_ps"], b.n)
                    dve.tensor_copy(spread0(v_spread[:, b.p, :]),
                                    v_all[:, b.n, :].rearrange("p (j v d) -> p v j d", v=4, d=D0)).then_inc(s["a_vs"], 1)
                    neg_scores(front, 2)
                if (b := t.before(0)) is not None:
                    dve.wait_ge(s["a_q"], 2)
                    dve.wait_ge(s["a_s_ps"], 4 * b.n + 4)
                    dve.tensor_copy(qT[:, b.p, :], qT_all[:, b.n, :]).then_inc(s["a_qT"], 1)
                    dve.wait_ge(s["a_k"], 2)
                    dve.tensor_tensor(km[:, b.p, 0:8, :],
                                      kT_all[:, b.n, :].unsqueeze(1).to_broadcast([E, 8, T]),
                                      head0[:, 0:8].unsqueeze(2).to_broadcast([E, 8, T]),
                                      ALU.mult).then_inc(s["a_km_dve"], 1)
                if back is not None:
                    turned(back, 2)
                if front is not None:
                    neg_scores(front, 3)

            def keys_values1():
                for n in range(4):
                    dve.wait_ge(s["kv_ps"], n + 1)
                    dve.tensor_tensor(kv_all[:, 2 * n:2 * n + 2, :, :],
                                      ps[:, n, :].rearrange("p (b k e) -> p b k e", k=2, e=E),
                                      bqkv1_row[:, 1:3, :].unsqueeze(1).to_broadcast([T, 2, 2, E]),
                                      ALU.add).then_inc(s["kv"], 1)

            over_batches(dve, attn0, 3, last=keys_values1)

            def fold_weights():
                for k, e, f in ((0, 0, 1.0), (1, 1, SCALE3), (2, 2, 1.0), (3, 2, 1.0)):
                    dve.tensor_scalar(scl[:, :, k], ew[:, :, e], f, None, ALU.mult).then_inc(s["f_scl"], 1)
                dve.wait_ge(s["f_scl"], 4)
                dve.wait_ge(ld["wd"], 16)
                for c in range(NODES):
                    dve.wait_ge(s["f_w_ps"], c + 1)
                    dve.tensor_tensor(wf[:, c, :, :], ps[:, FOLD_BANKS[c % 3], :].rearrange("p (k e) -> p k e", e=128),
                                      scl[:, c, :].unsqueeze(2).to_broadcast([E, 4, 128]),
                                      ALU.mult).then_inc(s["f_w"], 1)
                dve.wait_ge(s["f_b_ps"], 1)
                dve.tensor_tensor(bias3[:, :, 1:3], ps[:, 7, 0:2 * NODES].rearrange("p (c k) -> p c k", k=2),
                                  scl[:, :, 0:2], ALU.mult).then_inc(s["f_bias"], 1)
                dve.tensor_tensor(wres[:, :, :], wd[:, 7, :, :], ew[:, :, 0:1].to_broadcast([E, NODES, 128]),
                                  ALU.mult).then_inc(s["f_wres"], 1)
                dve.tensor_tensor(bias3[:, :, 0], beT[:, :, 0], ew[:, :, 0], ALU.mult).then_inc(s["f_bias"], 1)

            def ln_stats(name, b):
                dve.bn_stats(stats[:, b.p, :], x_all[:, b.n, :]).then_inc(s[name + "_stats"], 1)

            def ln_mean(name, b):
                dve.wait_ge(s[name + "_stats"], b.n + 1)
                dve.sem_inc(s["passed"], 1)
                dve.bn_aggr(mv[:, b.p, :], stats[:, b.p, :]).then_inc(s[name + "_mv"], 1)

            def ln_eps(name, b):
                dve.wait_ge(s[name + "_mv"], b.n + 1)
                dve.tensor_scalar(veps[:, b.p:b.p + 1], mv[:, b.p, 1:2], 1e-5, None,
                                  ALU.add).then_inc(s[name + "_veps"], 1)

            def ln_apply(name, b):
                dve.wait_ge(s[name + "_rstd"], b.n + 1)
                dve.tensor_scalar(xn[:, b.p, :], x_all[:, b.n, :], mv[:, b.p, 0:1], rstd[:, b.p:b.p + 1],
                                  ALU.subtract, ALU.mult).then_inc(s[name + "_xn"], 1)

            def moe(t):
                cur, front, back = t.before(0), t.before(1), t.before(2)

                def weighted(b, e):
                    if e % 4 == 0:
                        dve.wait_ge(s["b_y_ps"], 2 * b.n + e // 4 + 1)
                    dve.wait_ge(s["b_y"], 8 * b.n + e + 8)
                    dve.scalar_tensor_tensor(out=x_all[:, b.n, :], in0=ps[:, 4 + e // 4, 128 * (e % 4):128 * (e % 4) + 128],
                                             scalar=comb[:, b.p, e:e + 1], in1=x_all[:, b.n, :],
                                             op0=ALU.mult, op1=ALU.add).then_inc(s["b_y"], 1)

                def squares(b, k):
                    dve.wait_ge(s["b_relu"], 4 * b.n + k + 1)
                    dve.tensor_tensor(h2[:, b.p, 4 * k:4 * k + 4, :],
                                      ps[:, k, :].rearrange("q (m t) -> q m t", t=T),
                                      relu_h[:, k % 2, :, :], ALU.mult).then_inc(s["b_h2"], 1)

                if back is not None:
                    dve.wait_ge(s["b_comb"], back.n + 1)
                if cur is not None:
                    dve.wait_ge(s["a_x"], cur.n + 3)
                    ln_stats("b", cur)
                if front is not None:
                    b = front
                    n, p = b.n, b.p
                    logits = ps[:, 6, 128:128 + NEXP]
                    dve.wait_ge(s["b_gate_ps"], n + 1)
                    dve.tensor_reduce(gcol[:, p, 0:1], logits, AX_X, ALU.max, negate=True).then_inc(s["b_gmax"], 1)
                if cur is not None:
                    ln_mean("b", cur)
                if front is not None:
                    squares(front, 0)
                if cur is not None:
                    ln_eps("b", cur)
                if front is not None:
                    dve.wait_ge(s["b_gexp"], n + 2)
                    dve.reciprocal(gcol[:, p, 2:3], gcol[:, p, 1:2]).then_inc(s["b_rsum"], 1)
                    squares(front, 1)
                    dve.wait_ge(s["b_rsum"], n + 1)
                    dve.tensor_scalar(gsm[:, p, 1, :], gsm[:, p, 0, :], gcol[:, p, 2:3], None,
                                      ALU.mult).then_inc(s["b_prob"], 1)
                if back is not None:
                    weighted(back, 0)
                if front is not None:
                    dve.wait_ge(s["b_prob"], n + 1)
                    dve.sem_inc(s["passed"], 1)
                    dve.max(gsm[:, p, 2, :], gsm[:, p, 1, :]).then_inc(s["b_top"], 1)
                if back is not None:
                    weighted(back, 1)
                if front is not None:
                    dve.wait_ge(s["b_top"], n + 1)
                    dve.sem_inc(s["passed"], 1)
                    dve.max_index(gidx[:, p, :], gsm[:, p, 2, :], gsm[:, p, 1, :]).then_inc(s["b_idx"], 1)
                    dve.scalar_tensor_tensor(out=gcol[:, p, 3:4], in0=gsm[:, p, 2, 0:1], scalar=1e-8,
                                             in1=gsm[:, p, 2, 1:2], op0=ALU.add, op1=ALU.add).then_inc(s["b_gden"], 1)
                if back is not None:
                    weighted(back, 2)
                if front is not None:
                    squares(front, 2)
                    dve.wait_ge(s["b_idx"], n + 1)
                    dve.tensor_copy(gcol[:, p, 4:6], gidx[:, p, 0:2]).then_inc(s["b_idxf"], 1)
                    dve.wait_ge(s["b_gden"], n + 1)
                    dve.reciprocal(gcol[:, p, 6:7], gcol[:, p, 3:4]).then_inc(s["b_rgden"], 1)
                if back is not None:
                    weighted(back, 3)
                if front is not None:
                    dve.wait_ge(s["b_rgden"], n + 1)
                    dve.tensor_scalar(gsm[:, p, 3, 0:2], gsm[:, p, 2, 0:2], gcol[:, p, 6:7], None,
                                      ALU.mult).then_inc(s["b_w"], 1)
                if cur is not None:
                    ln_apply("b", cur)
                if front is not None:
                    dve.wait_ge(s["b_w"], n + 1)
                    dve.wait_ge(s["b_idxf"], n + 1)
                    for k, name in ((0, "b_c1"), (1, "b_c2")):
                        dve.tensor_scalar(gsm[:, p, 4 + k, :], iota8[:, :], gcol[:, p, 4 + k:5 + k],
                                          gsm[:, p, 3, k:k + 1], ALU.is_equal, ALU.mult).then_inc(s[name], 1)
                    squares(front, 3)
                    dve.wait_ge(s["b_c1"], n + 1)
                    dve.wait_ge(s["b_c2"], n + 1)
                    dve.tensor_tensor(comb[:, p, :], gsm[:, p, 4, :], gsm[:, p, 5, :], ALU.add).then_inc(s["b_comb"], 1)
                if back is not None:
                    for e in range(4, 8):
                        weighted(back, e)

            dve.wait_ge(s["iota_ready"], NEXP)
            dve.wait_ge(s["v_zeroed"], 2)
            dve.sem_inc(s["b_y"], 8)
            def attn1(t):
                cur, front, back = t.before(0), t.before(1), t.before(2)
                if back is not None:
                    b = back
                    dve.wait_ge(s["c_exp"], b.n + 1)
                    dve.wait_ge(s["c_ctx_ps"], b.n + 1)
                    vv = kv_all[:, b.n, 1, :].rearrange("p (s h e) -> p h s e", h=H1, e=2)[:, :, :, 0]
                    dve.tensor_tensor(
                        ev[:, b.p, :, :].rearrange("p s (l h e) -> p l h s e", h=H1, e=2)[:, :, :, :, 0],
                        e1[:, b.p, :].rearrange("p (l h s) -> p l h s", h=H1, s=G1),
                        vv.unsqueeze(1).to_broadcast([T, G1, H1, G1]), ALU.mult).then_inc(s["c_ev0"], 1)
                    dve.tensor_reduce(l1[:, b.p, :], e1[:, b.p, :].rearrange("p (g s) -> p g s", s=G1), AX_X,
                                      ALU.add).then_inc(s["c_l"], 1)
                if cur is not None:
                    dve.wait_ge(s["b_y"], 8 * cur.n + 16)
                    ln_stats("c", cur)
                    ln_mean("c", cur)
                    ln_eps("c", cur)
                if front is not None:
                    b = front
                    dve.wait_ge(s["c_sc"], b.n + 3)
                    scores = ps[:, 2, :].rearrange("p (g s) -> p g s", s=G1)
                    dve.tensor_reduce(m1[:, b.p, :], scores, AX_X, ALU.max).then_inc(s["c_m"], 1)
                    dve.wait_ge(s["c_m"], b.n + 1)
                    dve.tensor_tensor(sc1[:, b.p, :].rearrange("p (g s) -> p g s", s=G1), scores,
                                      m1[:, b.p, :].unsqueeze(2).to_broadcast([T, 64, G1]),
                                      ALU.subtract).then_inc(s["c_sub"], 1)
                if back is not None:
                    b = back
                    dve.wait_ge(s["c_l"], b.n + 1)
                    dve.reciprocal(rl1[:, b.p, :], l1[:, b.p, :]).then_inc(s["c_rl"], 1)
                    dve.wait_ge(s["c_rl"], b.n + 1)
                    dve.wait_ge(s["c_ctx_ps"], b.n + 3)
                    dve.tensor_tensor(ctx1[:, b.p, :].rearrange("p (g e) -> p g e", e=2),
                                      ps[:, 3, 0:128].rearrange("p (g e) -> p g e", e=2),
                                      rl1[:, b.p, :].unsqueeze(2).to_broadcast([T, 64, 2]),
                                      ALU.mult).then_inc(s["c_ctx"], 1)
                if cur is not None:
                    ln_apply("c", cur)
                if back is not None:
                    b = back
                    dve.wait_ge(s["c_o_ps"], b.n + 1)
                    dve.wait_ge(s["c_xbo"], b.n + 1)
                    dve.tensor_tensor(x_all[:, b.n, :], ps[:, 4, 128:256], xbo[:, b.p, :],
                                      ALU.add).then_inc(s["c_x"], 1)
                if cur is not None:
                    b = cur
                    dve.wait_ge(s["c_q_ps"], b.n + 1)
                    dve.tensor_tensor(q1[:, b.p, :], ps[:, 0, 128:256], bqkv1_row[:, 0, :],
                                      ALU.add).then_inc(s["c_q"], 1)
                    dve.wait_ge(s["c_q"], b.n + 2)
                    dve.wait_ge(s["c_sc"], b.n + 1)
                    qv = q1[:, b.p, :].rearrange("p (l h e) -> p l h e", h=H1, e=2)[:, :, :, 0]
                    kk = kv_all[:, b.n, 0, :].rearrange("p (s h e) -> p h s e", h=H1, e=2)[:, :, :, 0]
                    dve.tensor_tensor(
                        pr0[:, b.p, :].rearrange("p (l h s) -> p l h s", h=H1, s=G1),
                        qv.unsqueeze(3).to_broadcast([T, G1, H1, G1]),
                        kk.unsqueeze(1).to_broadcast([T, G1, H1, G1]), ALU.mult).then_inc(s["c_pr0"], 1)

            def attn1_start():
                dve.sem_inc(s["c_q"], 1)
                dve.sem_inc(s["c_sub"], 1)
                dve.sem_inc(s["c_ctx"], 1)
                dve.sem_inc(s["c_x"], 2)
                attn1(Batch(None, 0))

            def norm3_stats(b):
                dve.wait_ge(s["c_x"], b + 3)
                for ln_step in (ln_stats, ln_mean, ln_eps):
                    ln_step("n", Batch(None, b))

            def norm3_apply(b):
                if b >= 2:
                    dve.wait_ge(s["n_xnT_ps"], b - 1)
                ln_apply("n", Batch(None, b))

            def norm3_start():
                for b in range(2):
                    norm3_stats(b)
                for b in range(2):
                    norm3_apply(b)

            over_batches(dve, moe, 2, second=fold_weights, last=attn1_start)
            over_batches(dve, attn1, 2, last=norm3_start, first=1)
            dve.wait_ge(s["f_w"], NODES)
            dve.wait_ge(s["f_bias"], 2)

            def nodes(at):
                back = at(4)
                if back is not None:
                    dve.wait_ge(s["d_exp"], 8 * back + 8)
                    dve.reciprocal(rden3[:, back % 2, :], den3[:, back % 2, :]).then_inc(s["d_rden"], 1)
                    dve.wait_ge(s["d_rden"], back + 1)
                    if back >= 2:
                        dve.wait_ge(s["d_r_ps"], back - 1)
                    dve.tensor_copy(rrow[:, back % 2, :].rearrange("p (h d) -> p h d", d=D3),
                                    rden3[:, back % 2, :].unsqueeze(2).to_broadcast([T, H3, D3])).then_inc(s["d_rrow"], 1)
                if (i := at(5)) is not None:
                    c, b = ITEMS[i]
                    dve.wait_ge(s["d_o_ps"], i + 1)
                    dve.scalar_tensor_tensor(out=nodesT[:, c + 1, b, :], in0=ps[:, 7, 256:384],
                                             scalar=act_w[:, c:c + 1], in1=qqk[:, b, 0, :],
                                             op0=ALU.mult, op1=ALU.add).then_inc(s["d_node"], 1)
                if back is not None:
                    dve.wait_ge(s["d_pT_ps"], 2 * back + 1)
                    if back >= 1:
                        dve.wait_ge(s["d_pv_ps"], back)
                    dve.tensor_copy(p3T[:, 0:4, :].rearrange("p h t -> p (h t)"), ps[:, 4, :]).then_inc(s["d_pT_dve"], 1)
                if (i := at(0)) is not None:
                    c, b = ITEMS[i]
                    dve.wait_ge(s["d_proj_ps"], i + 1)
                    dve.tensor_tensor(qqk[:, b, :, :], ps[:, 6, 0:384].rearrange("p (k t) -> p k t", t=T),
                                      bias3[:, c, :].unsqueeze(2).to_broadcast([E, 3, T]),
                                      ALU.add).then_inc(s["d_qqk"], 1)
                    dve.tensor_tensor(spread3(v3[:, b, :]),
                                      ps[:, 6, 384:512].rearrange("p (j v d) -> p v j d", v=2, d=D3),
                                      wf[:, c, 3, :].rearrange("p (j v d) -> p v j d", v=2, d=D3),
                                      ALU.add).then_inc(s["d_v"], 1)
                if (b := to_norm(at, 2)) is not None:
                    norm3_stats(b)
                if (b := to_finish(at, 7)) is not None:
                    dve.wait_ge(s["e_fin"], b + 1)
                    dve.bn_stats(stats_a[:, b, :], fin[:, b, :]).then_inc(s["e_stats"], 1)
                    dve.wait_ge(s["e_stats"], b + 1)
                    dve.bn_aggr(mv_a[:, b, :], stats_a[:, b, :]).then_inc(s["e_mv"], 1)
                    dve.wait_ge(s["e_mv"], b + 1)
                    dve.tensor_scalar(veps_a[:, b:b + 1], mv_a[:, b, 1:2], 1e-6, None, ALU.add).then_inc(s["e_veps"], 1)
                if (i := at(2)) is not None:
                    for k in range(2):
                        dve.wait_ge(s["d_s_ps"], 2 * i + k + 1)
                        dve.tensor_reduce(nmax3[:, i % 2, 4 * k:4 * k + 4],
                                          ps[:, 2 * (i % 2) + k, :].rearrange("p (h k) -> p h k", k=T),
                                          AX_X, ALU.max, negate=True).then_inc(s["d_max"], 1)
                if (b := to_norm(at, 2)) is not None:
                    norm3_apply(b)
                if (b := to_finish(at, 7)) is not None:
                    dve.scalar_tensor_tensor(out=fin[:, b, :], in0=fin[:, b, :], scalar=mv_a[:, b, 0:1], in1=g_row,
                                             op0=ALU.subtract, op1=ALU.mult).then_inc(s["e_g"], 1)
                    dve.wait_ge(s["e_g"], b + 1)
                    dve.wait_ge(s["e_rstd"], b + 1)
                    dve.wait_ge(s["e_xb"], b + 1)
                    dve.scalar_tensor_tensor(out=fin2[:, b, :], in0=fin[:, b, :], scalar=rstd_a[:, b:b + 1],
                                             in1=xb[:, b, :], op0=ALU.mult, op1=ALU.add).then_inc(s["e_out"], 1)
                if back is not None:
                    dve.wait_ge(s["d_pv_ps"], back + 1)
                    dve.wait_ge(s["d_r"], back + 1)
                    if back >= 2:
                        dve.wait_ge(s["d_o_ps"], back - 1)
                    dve.tensor_tensor(ctxn[:, back % 2, :], ps[:, 7, 0:128], r_bc[:, back % 2, :],
                                      ALU.mult).then_inc(s["d_ctxn"], 1)

            over_items(nodes)


def kernel(**inputs):
    import numpy as np
    import concourse.bacc as bacc
    from concourse.bass_utils import run_bass_kernel_spmd

    a = {k: np.asarray(v) for k, v in inputs.items()}

    def by_row(rows_of):
        return np.ascontiguousarray(np.concatenate([r.reshape(128, -1) for r in rows_of], axis=1))

    def on_all(v):
        return np.broadcast_to(v.reshape(1, -1), (128, v.size))

    edges = [node_sources(c)[1] for c in range(NODES)]
    we = a["L1_ffn_We"]
    arrays = {
        "x": np.ascontiguousarray(a["x"].transpose(1, 0, 2)),
        "ctxT": np.ascontiguousarray(a["ctx_1024"].transpose(2, 0, 1)),
        "fside": np.ascontiguousarray(a["fside_Bx16xSxS2_0"].transpose(0, 2, 1, 3)),
        "mask": np.ascontiguousarray(np.broadcast_to(a["mask_BxS2_bf0"].view(np.uint32).reshape(1, -1),
                                                         (128, NB * T // 4))),
        "wa": by_row([a["L0_xattn_Wq"].T, a["L0_xattn_Wk"].T, a["L0_xattn_Wv"].T, a["L0_xattn_Wo"].T,
                      a["fside_SxS2_0"]]),
        "wb": by_row([a["L0_ffn_Wg"], a["L0_ffn_W1"].transpose(1, 0, 2),
                      a["L0_ffn_W2"].reshape(NEXP * HID // 128, 128, E).transpose(1, 0, 2)]),
        "wc": by_row([a["L1_xattn_" + k].T for k in ("Wq", "Wk", "Wv", "Wo")]),
        "wd": by_row([we[e[k]].T for k in range(3) for e in edges]
                     + [a["L1_ffn_" + k][c] for k in ("Wo", "Wq", "Wk", "Wv") for c in range(NODES)]
                     + [we[e[0]] for e in edges]),
        "cols": by_row([a["L0_xattn_bq"], a["L0_xattn_bk"], on_all(a["L1_ffn_ew"]), on_all(a["L1_ffn_act_w"])]
                       + [a["L1_ffn_be"][e[k]] for e in edges for k in range(3)]
                       + [np.zeros((128, 20), np.float32)]),
        "rows": by_row([on_all(a[k]) for k in ("L0_xattn_bv", "L0_xattn_bo", "L1_xattn_bq", "L1_xattn_bk",
                                               "L1_xattn_bv", "L1_xattn_bo", "L1_ffn_ln_g", "L1_ffn_ln_b")]),
    }
    shapes = {"wa": (128, 5, 128), "wc": (128, 4, 128), "wd": (128, 8, NODES, 128), "rows": (128, 8, 128)}
    arrays = {k: v.reshape(shapes.get(k, v.shape)) for k, v in arrays.items()}
    nc = bacc.Bacc("TRN2", target_bir_lowering=False, num_devices=1)
    args = [nc.dram_tensor("in_" + k, v.shape, mybir.dt.from_np(v.dtype), kind="ExternalInput").ap()
            for k, v in arrays.items()]
    out = nc.dram_tensor("out", (T, NB, E), F32, kind="ExternalOutput").ap()
    xattn_ffn_kernel(nc, *args, out)
    r = run_bass_kernel_spmd(nc, [{"in_" + k: v for k, v in arrays.items()}], core_ids=[0])
    return np.ascontiguousarray(r.results[0]["out"].transpose(1, 0, 2))
```

```python
from contextlib import ExitStack

import concourse.bass as bass
from concourse import mybir

F32 = mybir.dt.float32
U8 = mybir.dt.uint8
U32 = mybir.dt.uint32
ALU = mybir.AluOpType
ACT = mybir.ActivationFunctionType
AX_X = mybir.AxisListType.X

NB = 8
T = 128
E = 128
H0, D0 = 16, 8
G1, H1 = 8, 8
NEXP, HID = 8, 256
H3, D3 = 8, 16
NODES = 6
SCALE0 = D0 ** -0.5
SCALE1 = 2 ** -0.5
SCALE3 = D3 ** -0.5
VW0 = 128 + D0
VW3 = 128 + D3


class Batch:

    def __init__(self, reg, off):
        self.reg, self.off = reg, off
        self.n = off if reg is None else 2 * reg + off
        self.p = off % 2
        self.turn = off // 2 if reg is None else reg + off // 2

    def before(self, k):
        off = self.off - k
        if self.reg is None and not 0 <= off < NB:
            return None
        return Batch(self.reg, off)


def over_batches(eng, step, lag, ahead_of={}, first=0):
    ahead = 4 if lag > 2 else 2
    for t in range(first, ahead):
        step(Batch(None, t))
    with eng.Fori(0, (NB - ahead) // 2) as i:
        for off in (ahead, ahead + 1):
            step(Batch(i, off))
    for t in range(NB, NB + lag):
        if t in ahead_of:
            ahead_of[t]()
        step(Batch(None, t))


def node_sources(c):
    nsrc = min(c + 1, 5)
    first = sum(min(k + 1, 5) for k in range(c))
    snode = c - nsrc
    return (c, snode + 1, snode + nsrc // 2 + 1), (first + nsrc - 1, first, first + nsrc // 2)


def xattn_ffn_kernel(nc, x_h, ctxT_h, fside_h, mask_h, wa_h, wb_h, wc_h, wd_h, cols_h, rows_h, out_h):
    ctx = ExitStack()
    with ctx:
        def sb(name, shape, dt=F32):
            return ctx.enter_context(nc.sbuf_tensor(name, shape, dt))

        def sem(name):
            return ctx.enter_context(nc.semaphore(name))

        x_all = sb("x_all", [T, NB, E])
        ctxT = sb("ctxT", [E, NB, T])
        mask_u32 = sb("mask_u32", [T, NB * T // 4], U32)
        mask_u8 = mask_u32[:, :].bitcast(U8).rearrange("p (b t) -> p b t", t=T)
        wa = sb("wa", [E, 5, 128])
        wb = sb("wb", [E, 8 + 2 * NEXP * HID // 128 * 128])
        wc = sb("wc", [E, 4, 128])
        wd = sb("wd", [E, 8, NODES, 128])
        cols = sb("cols", [E, 64])
        rows = sb("rows", [T, 8, 128])
        wg = wb[:, 0:NEXP]
        w1 = wb[:, NEXP:NEXP + NEXP * HID].rearrange("p (k m) -> p k m", m=128)
        w2 = wb[:, NEXP + NEXP * HID:].rearrange("p (k m) -> p k m", m=128)
        bq_col, bk_col = cols[:, 0:1], cols[:, 1:2]
        ew = cols[:, 2:20].rearrange("p (c k) -> p c k", k=3)
        act_w = cols[:, 20:26]
        beT = cols[:, 26:44].rearrange("p (c k) -> p c k", k=3)
        bv_row, bo_row, bqkv1_row, bo1_row, g_row, b_row = (
            rows[:, 0, :], rows[:, 1, :], rows[:, 2:5, :], rows[:, 5, :], rows[:, 6, :], rows[:, 7, :])

        ident = sb("ident", [128, 128])
        bk_half = sb("bk_half", [128, 1])
        head0 = sb("head0", [128, H0])
        head3 = sb("head3", [128, H3])
        minus_half = sb("minus_half", [128, NB])
        iota8 = sb("iota8", [128, NEXP])
        half_am = sb("half_am", [T, T])
        pad_all = sb("pad_all", [T, NB, T])

        nodesT = sb("nodesT", [E, NODES + 1, NB, T])
        big_a = sb("big_a", [128, 2, H0 * T])
        big_b = sb("big_b", [128, 2, H0 * T])
        big_c = sb("big_c", [128, 2, H0 * T])
        big_d = sb("big_d", [128, H0 * T])

        def part(tile2, start, *shape):
            size = 1
            for n in shape:
                size *= n
            names = "abcd"[:len(shape)]
            return tile2[:, start:start + size].rearrange(
                "p (%s) -> p %s" % (" ".join(names), " ".join(names)), **dict(zip(names, shape)))

        flat_a, flat_b, flat_c = (t.rearrange("p a b -> p (a b)") for t in (big_a[:, :, :], big_b[:, :, :], big_c[:, :, :]))

        stats, mv, veps, rstd, xn = {}, {}, {}, {}, {}
        for norm in "bc":
            stats[norm] = sb("stats_" + norm, [T, 2, 6])
            mv[norm] = sb("mv_" + norm, [T, 2, 2])
            veps[norm] = sb("veps_" + norm, [T, 2])
            rstd[norm] = sb("rstd_" + norm, [T, 2])
            xn[norm] = sb("xn_" + norm, [T, 2, E])
        for tiles in (stats, mv, veps, rstd, xn):
            tiles["n"] = tiles["c"]
        xnT = sb("xnT", [E, 2, T])
        xn1T = sb("xn1T", [E, 2, T])
        stats_a = sb("stats_a", [T, NB, 6])
        mv_a = sb("mv_a", [T, NB, 2])
        veps_a = sb("veps_a", [T, NB])
        rstd_a = sb("rstd_a", [T, NB])

        xn_a, xnT_a = nodesT[:, 1, :, :], nodesT[:, 2, :, :]
        kT_all = nodesT[:, 3, :, :]
        qT_all, v_all = nodesT[:, 4, :, :], nodesT[:, 5, :, :]
        qT = sb("qT", [E, 2, T])
        v_spread = sb("v_spread", [T, 2, 4 * VW0])
        am = sb("am", [T, 2, T])
        fs = part(flat_a, 0, 2, H0, T)
        km = part(flat_b, 0, 2, H0, T)
        nmax = sb("nmax", [T, 2, H0])
        prob = part(flat_c, 0, 2, H0, T)
        den = sb("den", [T, 2, H0])
        rden = sb("rden", [T, 2, H0])
        probT = part(big_d, 0, H0, T)
        rrow = sb("rrow", [T, 2, E])
        r_bc = sb("r_bc", [E, 2, T])
        ctxn = sb("ctxn", [E, 2, T])
        xbo = sb("xbo", [T, 2, E])

        gsm = sb("gsm", [T, 2, 8, NEXP])
        gidx = sb("gidx", [T, 2, 8], U32)
        gcol = sb("gcol", [T, 2, 8])
        comb = sb("comb", [T, 2, NEXP])
        relu_h = part(flat_c, 0, 2, 4, T)
        h2 = part(flat_b, 0, 2, 16, T)

        kv_all = sb("kv_all", [T, NB, 2, E])
        q1 = sb("q1", [T, 2, E])
        pr0 = part(flat_a, 0, 2, 512)
        pr1 = part(flat_a, 1024, 2, 512)
        sc1 = part(flat_a, 2048, 2, 512)
        m1 = sb("m1", [T, 2, 64])
        e1 = part(flat_a, 3072, 2, 512)
        l1 = sb("l1", [T, 2, 64])
        rl1 = sb("rl1", [T, 2, 64])
        ev = part(flat_c, 1024, 2, G1, E)
        ctx1 = sb("ctx1", [T, 2, E])
        ctx1T = sb("ctx1T", [E, 2, T])

        scl = sb("scl", [128, NODES, 4])
        wf = sb("wf", [E, NODES, 4, 128])
        wres = sb("wres", [E, NODES, 128])
        bias3 = sb("bias3", [E, NODES, 3])
        qqk = part(flat_a, 0, NB, 3, T)
        v3 = sb("v3", [T, NB, 2 * VW3])
        km3 = part(flat_b, 0, 3, H3, T)
        nmax3 = sb("nmax3", [T, 2, H3])
        den3 = sb("den3", [T, 2, H3])
        rden3 = sb("rden3", [T, 2, H3])
        p3 = part(flat_c, 0, 2, H3, T)
        p3T = part(big_d, 0, H3, T)
        fin, fin2, xb = part(wb, 0, NB, E), part(wb, NB * E, NB, E), part(wb, 2 * NB * E, NB, E)

        ps = ctx.enter_context(nc.psum_tensor("ps", [128, 8, 512], F32))

        ld = {k: sem("ld_" + k) for k in ("x", "ctx", "mask", "wa", "wb", "wc", "wd", "cols", "rows")}
        fs_landed = [[sem("fs_landed%d%d" % (p, half)) for half in range(2)] for p in range(2)]
        s = {}
        for name in """zeroed ident_ready const_ready v_zeroed iota_ready passed half_am_ready pad_ready
            a_stats a_mv a_veps a_rstd a_xn a_xnT_ps a_xnT a_proj_ps a_bk a_k a_q a_v a_v_ps
            a_am a_bias a_qT a_vs a_km_dve a_km_pool a_s_ps a_nmax a_exp a_rden a_rrow
            a_pT_ps a_pT_act a_pT_dve a_r_ps a_r a_pv_ps a_ctxn a_o_ps a_x a_xbo
            kv_ps kv
            b_stats b_mv b_veps b_rstd b_xn b_xnT_ps b_xnT b_gate_ps b_h_ps b_relu b_h2
            b_gmax b_gexp b_rsum b_prob b_top b_idx b_idxf b_gden b_rgden b_w b_c1 b_c2 b_comb b_y_ps b_y
            c_stats c_mv c_veps c_rstd c_xn c_xnT_ps c_xnT c_q_ps c_q c_pr0 c_pr1 c_sc c_m c_sub c_exp
            c_l c_rl c_ev0 c_ev1 c_ev c_ctx_ps c_ctx c_ctxT_ps c_ctxT c_o_ps c_xbo c_x
            n_stats n_mv n_veps n_rstd n_xn n_xnT_ps n_xnT
            f_w_ps f_scl f_w f_wres f_b_ps f_bias
            d_proj_ps d_qqk d_v d_km d_s_ps d_max d_exp d_rden d_rrow d_pT_ps d_pT_act d_pT_dve d_r_ps d_r
            d_pv_ps d_ctxn d_o_ps d_node
            e_T_ps e_fin e_stats e_mv e_veps e_rstd e_g e_xb e_out out_done""".split():
            s[name] = sem(name)

        block = ctx.enter_context(nc.Block())

        def spread0(tile2):
            return tile2.rearrange("p (v x) -> p v x", x=VW0)[:, :, 0:128].rearrange(
                "p v (j u d) -> p v j u d", u=4, d=D0)[:, :, :, 0, :]

        def spread3(tile2):
            return tile2.rearrange("p (v x) -> p v x", x=VW3)[:, :, 0:128].rearrange(
                "p v (j u d) -> p v j u d", u=2, d=D3)[:, :, :, 0, :]

        FOLD_BANKS = (0, 1, 2)
        LAST = Batch(None, NB - 1)
        ITEMS = [(c, b) for c in range(NODES) for b in range(NB)]
        NI = len(ITEMS)

        def over_items(step, first, end):
            for t in range(first, end):
                step(lambda k, t=t: t - k if 0 <= t - k < NI else None)

        def to_norm(at, k):
            i = at(-k)
            return i if i is not None and k <= i < NB else None

        def to_finish(at, k):
            i = at(k)
            return i % NB if i is not None and i // NB == NODES - 1 else None

        @block.sync
        def _(sp):
            sp.dma_start(x_all[:, :, :], x_h).then_inc(ld["x"], 16)
            sp.dma_start(ctxT[:, :, :], ctxT_h).then_inc(ld["ctx"], 16)
            sp.dma_start(wa[:, :, :], wa_h).then_inc(ld["wa"], 16)
            sp.dma_start(cols[:, :], cols_h).then_inc(ld["cols"], 16)
            sp.dma_start(rows[:, :, :], rows_h).then_inc(ld["rows"], 16)
            sp.dma_start(mask_u32[:, :], mask_h).then_inc(ld["mask"], 16)

            def step(t):
                if (b := t.before(0)) is not None:
                    for half in range(2):
                        if b.reg is not None or b.off >= 2:
                            sp.wait_ge(s["a_exp"], 4 * b.n + 2 * half - 6)
                        sp.dma_start(fs[:, b.p, 8 * half:8 * half + 8, :],
                                     fside_h[b.n][:, 8 * half:8 * half + 8, :]).then_inc(fs_landed[b.p][half], 16)

            for t in range(2):
                step(Batch(None, t))
            sp.dma_start(wc[:, :, :], wc_h).then_inc(ld["wc"], 16)
            sp.dma_start(wb[:, :], wb_h).then_inc(ld["wb"], 16)
            with sp.Fori(0, NB // 2 - 1) as i:
                for off in (2, 3):
                    b = Batch(i, off)
                    step(b)
                    sp.dma_start(wd[:, :, b.n - 2, :], wd_h[:, :, b.n - 2, :]).then_inc(ld["wd"], 16)
            for b in range(NB):
                sp.wait_ge(s["e_out"], b + 1)
                sp.dma_start(out_h[:, b, :], fin2[:, b, :]).then_inc(s["out_done"], 16)
            sp.wait_ge(s["out_done"], 16 * NB)

        @block.gpsimd
        def _(pool):
            pool.memset(ident[:, :], 0.0).then_inc(s["zeroed"], 1)
            pool.memset(head0[:, :], 1.0).then_inc(s["zeroed"], 1)
            pool.memset(head3[:, :], 1.0).then_inc(s["zeroed"], 1)
            pool.memset(minus_half[:, :], -0.5).then_inc(s["zeroed"], 1)
            pool.wait_ge(s["zeroed"], 4)
            pool.affine_select(out=ident[:, :], in_=ident[:, :], compare_op=ALU.not_equal, fill=1.0,
                               base=0, pattern=[[-1, 128]], channel_multiplier=1).then_inc(s["ident_ready"], 1)
            for tile, heads, width in ((head0, H0, D0), (head3, H3, D3)):
                pool.affine_select(out=tile[:, :], in_=tile[:, :], compare_op=ALU.is_ge, fill=0.0, base=0,
                                   pattern=[[-width, heads]], channel_multiplier=1).then_inc(s["zeroed"], 1)
            pool.wait_ge(s["zeroed"], 6)
            for tile, heads, width in ((head0, H0, D0), (head3, H3, D3)):
                pool.affine_select(out=tile[:, :], in_=tile[:, :], compare_op=ALU.is_ge, fill=0.0,
                                   base=width - 1, pattern=[[width, heads]],
                                   channel_multiplier=-1).then_inc(s["const_ready"], 1)
            for tile in (v_spread, v3):
                pool.memset(tile[:, :, :], 0.0).then_inc(s["v_zeroed"], 1)
            pool.wait_ge(s["a_veps"], 1)
            pool.tensor_tensor(rstd_a[:, :], veps_a[:, :], minus_half[:, :], ALU.pow).then_inc(s["a_rstd"], 1)
            pool.wait_ge(ld["mask"], 16)
            pool.tensor_scalar(pad_all[:, :, :], mask_u8, -3.0e38, 3.0e38, ALU.mult,
                               ALU.mult).then_inc(s["pad_ready"], 1)
            pool.wait_ge(s["pad_ready"], 1)
            pool.wait_ge(s["half_am_ready"], 1)
            pool.wait_ge(s["const_ready"], 2)

            def attn0(t):
                def mask_keys(b):
                    pool.wait_ge(s["a_k"], 2)
                    pool.wait_ge(s["a_s_ps"], 4 * b.n + 4)
                    pool.tensor_tensor(km[:, b.p, 8:16, :],
                                       kT_all[:, b.n, :].unsqueeze(1).to_broadcast([E, 8, T]),
                                       head0[:, 8:16].unsqueeze(2).to_broadcast([E, 8, T]),
                                       ALU.mult).then_inc(s["a_km_pool"], 1)

                def biases(b):
                    pool.wait_ge(s["a_bias"], 2 * b.n + 2)
                    pool.tensor_tensor(am[:, b.p, :], half_am[:, :], pad_all[:, b.n, :],
                                       ALU.add).then_inc(s["a_am"], 1)
                    pool.wait_ge(s["a_am"], b.n + 1)
                    for half in range(2):
                        pool.wait_ge(fs_landed[b.p][half], 16 * (b.turn + 1))
                        heads = fs[:, b.p, 8 * half:8 * half + 8, :]
                        pool.tensor_tensor(heads, heads, am[:, b.p, :].unsqueeze(1).to_broadcast([T, 8, T]),
                                           ALU.add).then_inc(s["a_bias"], 1)

                cur = t.before(0)
                starts = t.reg is None and t.off == 0
                if starts:
                    biases(cur)
                if cur is not None:
                    mask_keys(cur)
                if (b := t.before(2)) is not None:
                    pool.wait_ge(s["a_x"], b.n + 1)
                    pool.wait_ge(ld["rows"], 16)
                    pool.tensor_tensor(xbo[:, b.p, :], x_all[:, b.n, :], bo_row, ALU.add).then_inc(s["a_xbo"], 1)
                if cur is not None and not starts:
                    biases(cur)

            pool.sem_inc(s["a_bias"], 4)
            over_batches(pool, attn0, 2)

            def rstd_of(name, b):
                pool.wait_ge(s[name + "_veps"], b.n + 1)
                pool.tensor_tensor(rstd[name][:, b.p:b.p + 1], veps[name][:, b.p:b.p + 1], minus_half[:, 0:1],
                                   ALU.pow).then_inc(s[name + "_rstd"], 1)

            def weigh_values(b):
                pool.wait_ge(s["c_exp"], b.n + 1)
                pool.wait_ge(s["c_ctx_ps"], b.n + 1)
                vv = kv_all[:, b.n, 1, :].rearrange("p (s h e) -> p h s e", h=H1, e=2)[:, :, :, 1]
                pool.tensor_tensor(
                    ev[:, b.p, :, :].rearrange("p s (l h e) -> p l h s e", h=H1, e=2)[:, :, :, :, 1],
                    e1[:, b.p, :].rearrange("p (l h s) -> p l h s", h=H1, s=G1),
                    vv.unsqueeze(1).to_broadcast([T, G1, H1, G1]), ALU.mult).then_inc(s["c_ev1"], 1)
                pool.wait_ge(s["c_ev0"], b.n + 1)
                pool.wait_ge(s["c_ev1"], b.n + 1)
                pool.tensor_tensor(ev[:, b.p, 0:4, :], ev[:, b.p, 0:4, :], ev[:, b.p, 4:8, :],
                                   ALU.add).then_inc(s["c_ev"], 1)
                pool.wait_ge(s["c_x"], b.n + 1)
                pool.tensor_tensor(xbo[:, b.p, :], x_all[:, b.n, :], bo1_row, ALU.add).then_inc(s["c_xbo"], 1)

            def moe_attn1(t):
                cur, cur1, back1 = t.before(0), t.before(3), t.before(4)
                if cur1 is not None:
                    rstd_of("c", cur1)
                if cur is not None:
                    rstd_of("b", cur)
                if back1 is not None:
                    weigh_values(back1)
                if cur1 is not None:
                    b = cur1
                    pool.wait_ge(s["c_q"], b.n + 2)
                    pool.wait_ge(s["c_sc"], b.n + 1)
                    qv = q1[:, b.p, :].rearrange("p (l h e) -> p l h e", h=H1, e=2)[:, :, :, 1]
                    kv = kv_all[:, b.n, 0, :].rearrange("p (s h e) -> p h s e", h=H1, e=2)[:, :, :, 1]
                    pool.tensor_tensor(
                        pr1[:, b.p, :].rearrange("p (l h s) -> p l h s", h=H1, s=G1),
                        qv.unsqueeze(3).to_broadcast([T, G1, H1, G1]),
                        kv.unsqueeze(1).to_broadcast([T, G1, H1, G1]), ALU.mult).then_inc(s["c_pr1"], 1)
                    pool.wait_ge(s["c_pr0"], b.n + 1)
                    pool.wait_ge(s["c_pr1"], b.n + 1)
                    pool.tensor_tensor(sc1[:, b.p, :], pr0[:, b.p, :], pr1[:, b.p, :], ALU.add).then_inc(s["c_sc"], 1)

            def norm3(b):
                rstd_of("n", Batch(None, b))

            def norm3_start():
                for b in range(2):
                    norm3(b)

            pool.sem_inc(s["c_sc"], 2)
            over_batches(pool, moe_attn1, 3)
            norm3_start()

            def nodes(at):
                if (b := to_norm(at, 2)) is not None:
                    norm3(b)
                if (i := at(0)) is not None:
                    c, b = ITEMS[i]
                    pool.wait_ge(s["d_qqk"], i + 1)
                    if i >= 3:
                        pool.wait_ge(s["d_s_ps"], 2 * (i - 2))
                    pool.tensor_tensor(km3[:, i % 3, :, :],
                                       qqk[:, b, 2, :].unsqueeze(1).to_broadcast([E, H3, T]),
                                       head3[:, :].unsqueeze(2).to_broadcast([E, H3, T]),
                                       ALU.mult).then_inc(s["d_km"], 1)
                if (b := to_finish(at, 7)) is not None:
                    pool.tensor_tensor(xb[:, b, :], x_all[:, b, :], b_row, ALU.add).then_inc(s["e_xb"], 1)
                    pool.wait_ge(s["e_veps"], b + 1)
                    pool.tensor_tensor(rstd_a[:, b:b + 1], veps_a[:, b:b + 1], minus_half[:, 0:1],
                                       ALU.pow).then_inc(s["e_rstd"], 1)

            weigh_values(LAST)
            over_items(nodes, 0, NI + 8)

        @block.tensor
        def _(pe):
            pe.sem_inc(s["a_s_ps"], 8)
            pe.wait_ge(s["ident_ready"], 1)
            pe.wait_ge(ld["wa"], 16)
            pe.wait_ge(ld["ctx"], 16)
            for n in range(2):
                pe.matmul(ps[:, 4 + n, :], wa[:, 1, :], ctxT[:, 4 * n:4 * n + 4, :],
                          start=True, stop=True).then_inc(s["a_proj_ps"], 1)
            for b in range(NB):
                pe.wait_ge(s["a_xn"], b + 1)
                pe.transpose(ps[:, b // 4, 128 * (b % 4):128 * (b % 4) + 128], xn_a[:, b, :],
                             ident[:, :]).then_inc(s["a_xnT_ps"], 1)
            for n in range(2):
                for b in range(4 * n, 4 * n + 4):
                    last = pe.matmul(ps[:, 6 + n, 128 * (b % 4):128 * (b % 4) + 128], ctxT[:, b, :], wa[:, 2, :],
                                     start=True, stop=True)
                last.then_inc(s["a_v_ps"], 1)
                pe.wait_ge(s["a_xnT"], n + 1)
                pe.matmul(ps[:, 2 + n, :], wa[:, 0, :], xnT_a[:, 4 * n:4 * n + 4, :],
                          start=True, stop=True).then_inc(s["a_proj_ps"], 1)
            pe.wait_ge(s["a_q"], 2)
            pe.wait_ge(s["a_v"], 2)
            pe.wait_ge(s["a_k"], 2)
            pe.sem_inc(s["a_pT_ps"], 4)
            pe.sem_inc(s["a_pv_ps"], 1)

            def attn0(t):
                front, back, done = t.before(1), t.before(2), t.before(3)

                def scores(b, k):
                    if k == 0:
                        pe.wait_ge(s["a_qT"], b.n + 1)
                        pe.wait_ge(s["a_km_dve"], b.n + 1)
                    if k == 2:
                        pe.wait_ge(s["a_km_pool"], b.n + 1)
                    pe.wait_ge(s["a_nmax"], 4 * b.n + k + 1)
                    pe.matmul(ps[:, k, :], qT[:, b.p, :], km[:, b.p, 4 * k:4 * k + 4, :],
                              start=True, stop=True).then_inc(s["a_s_ps"], 1)

                def turn(b, k):
                    pe.wait_ge(s["a_exp"], 4 * b.n + k + 1)
                    pe.wait_ge(s["a_pT_dve" if k % 2 == 0 else "a_pT_act"], 2 * b.n + k // 2 + 2)
                    for h in range(4):
                        last = pe.transpose(ps[:, 4 + k % 2, 128 * h:128 * h + 128], prob[:, b.p, 4 * k + h, :],
                                            ident[:, :])
                    last.then_inc(s["a_pT_ps"], 1)

                if front is not None:
                    scores(front, 0)
                    scores(front, 1)
                if done is not None:
                    b = done
                    pe.wait_ge(s["a_vs"], b.n + 1)
                    pe.wait_ge(s["a_pT_dve"], 2 * b.n + 4)
                    pe.wait_ge(s["a_pT_act"], 2 * b.n + 4)
                    pe.wait_ge(s["a_x"], b.n + 2)
                    for u in range(4):
                        for j in range(4):
                            last = pe.matmul(ps[32 * j:32 * j + 32, 7, 0:128],
                                             v_spread[:, b.p, 128 * u + 32 * j:128 * u + 32 * j + 32],
                                             probT[:, 4 * j + u, :], start=(u == 0), stop=(u == 3))
                    last.then_inc(s["a_pv_ps"], 1)
                if back is not None:
                    turn(back, 0)
                    turn(back, 1)
                if done is not None:
                    pe.wait_ge(s["a_ctxn"], done.n + 1)
                    pe.matmul(ps[:, 7, 128:256], ctxn[:, done.p, :], wa[:, 3, :],
                              start=True, stop=True).then_inc(s["a_o_ps"], 1)
                if front is not None:
                    scores(front, 2)
                if back is not None:
                    turn(back, 2)
                    turn(back, 3)
                    pe.wait_ge(s["a_rrow"], back.n + 1)
                    pe.wait_ge(s["a_r"], back.n + 1)
                    pe.transpose(ps[:, 6, 0:128], rrow[:, back.p, :], ident[:, :]).then_inc(s["a_r_ps"], 1)
                if front is not None:
                    scores(front, 3)

            def keys_values1():
                pe.wait_ge(ld["wd"], 16 * NODES)
                pe.wait_ge(ld["cols"], 16)
                pe.wait_ge(s["a_r"], NB)
                for c in range(NODES):
                    for k in range(2):
                        last = pe.matmul(ps[:, 6, 128 + 2 * c + k:129 + 2 * c + k], wd[:, 4 + k, c, :],
                                         beT[:, c, k:k + 1], start=True, stop=True)
                last.then_inc(s["f_b_ps"], 1)
                pe.wait_ge(ld["wc"], 16)
                pe.wait_ge(s["a_nmax"], 4 * NB + 4)
                for b in range(NB):
                    last = pe.matmul(ps[:, b // 2, 256 * (b % 2):256 * (b % 2) + 256], ctxT[:, b, :],
                                     wc[:, 1:3, :], start=True, stop=True)
                    if b % 2:
                        last.then_inc(s["kv_ps"], 1)
                pe.wait_ge(s["f_bias"], 1)

            def fold_weights():
                pe.wait_ge(s["kv"], 4)
                for c in range(NODES):
                    bank = FOLD_BANKS[c % 3]
                    if c >= 3:
                        pe.wait_ge(s["f_w"], c - 2)
                    pe.matmul(ps[:, bank, 0:128], wd[:, 0, c, :], wd[:, 4, c, :], start=True, stop=True)
                    pe.matmul(ps[:, bank, 128:256], wd[:, 1, c, :], wd[:, 5, c, :], start=True, stop=True)
                    pe.matmul(ps[:, bank, 256:384], wd[:, 2, c, :], wd[:, 6, c, :], start=True, stop=True)
                    pe.matmul(ps[:, bank, 384:512], beT[:, c, 2:3].to_broadcast([E, 128]), wd[:, 6, c, :],
                              start=True, stop=True).then_inc(s["f_w_ps"], 1)

            def context1(b):
                pe.wait_ge(s["c_ev"], b.n + 1)
                pe.wait_ge(s["c_ctx"], b.n + 1)
                for g in range(G1 // 2):
                    last = pe.matmul(ps[:, 3, 0:128], ident[:, :], ev[:, b.p, g, :],
                                     start=(g == 0), stop=(g == G1 // 2 - 1))
                last.then_inc(s["c_ctx_ps"], 1)

            def turn_context1(b):
                pe.wait_ge(s["c_ctx"], b.n + 2)
                pe.wait_ge(s["c_x"], b.n + 2)
                pe.transpose(ps[:, 7, 0:128], ctx1[:, b.p, :], ident[:, :]).then_inc(s["c_ctxT_ps"], 1)

            def output1(b):
                pe.wait_ge(s["c_ctxT"], b.n + 1)
                pe.matmul(ps[:, 7, 128:256], ctx1T[:, b.p, :], wc[:, 3, :], start=True,
                          stop=True).then_inc(s["c_o_ps"], 1)

            def moe_attn1(t):
                cur, front, back, cur1, back1 = (t.before(k) for k in range(5))

                def experts_out(b, e):
                    pe.wait_ge(s["b_h2"], 4 * b.n + e // 2 + 1)
                    if e % 4 == 0:
                        pe.wait_ge(s["b_y"], 8 * b.n + 4 + e)
                    for k in (2 * e, 2 * e + 1):
                        last = pe.matmul(ps[:, 4 + e // 4, 128 * (e % 4):128 * (e % 4) + 128], h2[:, b.p, k, :],
                                         w2[:, k, :], start=(k % 2 == 0), stop=(k % 2 == 1))
                    if e % 4 == 3:
                        last.then_inc(s["b_y_ps"], 1)

                def experts_in(b, k):
                    if b.reg is not None or b.off >= 1 or k >= 2:
                        pe.wait_ge(s["b_relu"], 4 * b.n + k - 1)
                    for m in range(4):
                        last = pe.matmul(ps[:, k % 2, 128 * m:128 * m + 128], w1[:, 4 * k + m, :], xnT[:, b.p, :],
                                         start=True, stop=True)
                    last.then_inc(s["b_h_ps"], 1)

                if front is not None:
                    pe.wait_ge(s["b_xnT"], front.n + 1)
                    pe.matmul(ps[:, 6, 128:128 + NEXP], xnT[:, front.p, :], wg, start=True,
                              stop=True).then_inc(s["b_gate_ps"], 1)
                    experts_in(front, 0)
                if back is not None:
                    experts_out(back, 0)
                    experts_out(back, 1)
                if front is not None:
                    experts_in(front, 1)
                if back is not None:
                    experts_out(back, 2)
                    experts_out(back, 3)
                    if front is None:
                        for e in range(4, 8):
                            experts_out(back, e)
                if cur1 is not None:
                    b = cur1
                    pe.wait_ge(s["c_xn"], b.n + 1)
                    pe.wait_ge(s["c_q"], b.n + 1)
                    pe.transpose(ps[:, 2, 0:128], xn["c"][:, b.p, :], ident[:, :]).then_inc(s["c_xnT_ps"], 1)
                if back is not None and front is not None:
                    experts_out(back, 4)
                    experts_out(back, 5)
                if cur1 is not None:
                    pe.wait_ge(s["c_xnT"], b.n + 1)
                    pe.matmul(ps[:, 2, 128:256], xn1T[:, b.p, :], wc[:, 0, :], start=True,
                              stop=True).then_inc(s["c_q_ps"], 1)
                if back is not None and front is not None:
                    experts_out(back, 6)
                    experts_out(back, 7)
                if back1 is not None:
                    context1(back1)
                if front is not None:
                    experts_in(front, 2)
                if back1 is not None:
                    turn_context1(back1)
                if (b := cur) is not None:
                    pe.wait_ge(s["b_xn"], b.n + 1)
                    pe.wait_ge(s["b_gexp"], b.n + 1)
                    pe.transpose(ps[:, 6, 0:128], xn["b"][:, b.p, :], ident[:, :]).then_inc(s["b_xnT_ps"], 1)
                if front is not None:
                    experts_in(front, 3)
                if back1 is not None:
                    output1(back1)

            def moe_start():
                pe.wait_ge(s["a_r"], NB + 1)
                moe_attn1(Batch(None, 0))
                fold_weights()

            over_batches(pe, attn0, 3, {NB + 1: keys_values1, NB + 2: moe_start})
            pe.wait_ge(ld["wb"], 16)
            pe.wait_ge(s["f_w"], NODES)

            def norm3(b):
                pe.wait_ge(s["n_xn"], b + 1)
                if b >= 1:
                    pe.wait_ge(s["n_xnT"], b)
                if b <= 2:
                    pe.wait_ge(s["c_x"], NB + 1)
                elif b == 3:
                    pe.wait_ge(s["c_ctxT"], NB)
                pe.transpose(ps[:, 7, 384:512], xn["n"][:, b % 2, :], ident[:, :]).then_inc(s["n_xnT_ps"], 1)

            pe.sem_inc(s["c_ctx_ps"], 2)
            over_batches(pe, moe_attn1, 3, first=1)
            norm3(0)
            pe.wait_ge(s["f_wres"], 1)

            def nodes(at):
                def turn(i, k):
                    pe.wait_ge(s["d_exp"], 8 * i + 4 * k + 4)
                    if i >= 1:
                        pe.wait_ge(s["d_pT_act" if k else "d_pT_dve"], i)
                    for h in range(4):
                        last = pe.transpose(ps[:, 4 + k, 128 * h:128 * h + 128], p3[:, i % 2, 4 * k + h, :],
                                            ident[:, :])
                    last.then_inc(s["d_pT_ps"], 1)

                back = at(4)
                if back is not None:
                    turn(back, 0)
                if (i := at(0)) is not None:
                    c, b = ITEMS[i]
                    (sq, sk, sv), _ = node_sources(c)
                    if c:
                        pe.wait_ge(s["d_node"], i - NB + 1)
                    else:
                        pe.wait_ge(s["n_xnT"], b + 1)
                    if i >= 1:
                        pe.wait_ge(s["d_v"], i)
                    pe.matmul(ps[:, 6, 0:128], wres[:, c, :], nodesT[:, sq, b, :], start=True, stop=True)
                    pe.matmul(ps[:, 6, 128:256], wf[:, c, 0, :], nodesT[:, sq, b, :], start=True, stop=True)
                    pe.matmul(ps[:, 6, 256:384], wf[:, c, 1, :], nodesT[:, sk, b, :], start=True, stop=True)
                    pe.matmul(ps[:, 6, 384:512], nodesT[:, sv, b, :], wf[:, c, 2, :], start=True,
                              stop=True).then_inc(s["d_proj_ps"], 1)
                if (i := at(5)) is not None:
                    c, b = ITEMS[i]
                    pe.wait_ge(s["d_ctxn"], i + 1)
                    pe.matmul(ps[:, 7, 256:384], wd[:, 3, c, :], ctxn[:, i % 2, :], start=True,
                              stop=True).then_inc(s["d_o_ps"], 1)
                if back is not None:
                    turn(back, 1)

                def scores(i, k):
                    c, b = ITEMS[i]
                    pe.wait_ge(s["d_km"], i + 1)
                    if i >= 2:
                        pe.wait_ge(s["d_exp"], 8 * (i - 2) + 4 * k + 4)
                    pe.matmul(ps[:, 2 * (i % 2) + k, :], qqk[:, b, 1, :], km3[:, i % 3, 4 * k:4 * k + 4, :],
                              start=True, stop=True).then_inc(s["d_s_ps"], 1)

                if (i := at(2)) is not None:
                    scores(i, 0)
                if back is not None:
                    pe.wait_ge(s["d_rrow"], back + 1)
                    if back >= 1:
                        pe.wait_ge(s["d_node"], back)
                    pe.transpose(ps[:, 7, 128:256], rrow[:, back % 2, :], ident[:, :]).then_inc(s["d_r_ps"], 1)
                if (b := to_norm(at, 1)) is not None:
                    norm3(b)
                if (b := to_finish(at, 6)) is not None:
                    pe.wait_ge(s["d_node"], min(NI - NB + b + 2, NI))
                    if b >= 1:
                        pe.wait_ge(s["e_fin"], b)
                    pe.transpose(ps[:, 7, 384:512], nodesT[:, NODES, b, :], ident[:, :]).then_inc(s["e_T_ps"], 1)
                if (i := at(2)) is not None:
                    scores(i, 1)
                if back is not None:
                    b = back % NB
                    pe.wait_ge(s["d_pT_dve"], back + 1)
                    pe.wait_ge(s["d_pT_act"], back + 1)
                    pe.wait_ge(s["d_r"], back + 1)
                    if (n := to_norm(at, 1)) is not None:
                        pe.wait_ge(s["n_xnT"], n + 1)
                    if (n := to_finish(at, 6)) is not None:
                        pe.wait_ge(s["e_fin"], n + 1)
                    for u in range(2):
                        for j in range(4):
                            last = pe.matmul(ps[32 * j:32 * j + 32, 7, 0:128],
                                             v3[:, b, 128 * u + 32 * j:128 * u + 32 * j + 32],
                                             p3T[:, 2 * j + u, :], start=(u == 0), stop=(u == 1))
                    last.then_inc(s["d_pv_ps"], 1)

            over_items(nodes, 0, 1)
            context1(LAST)
            over_items(nodes, 1, 2)
            pe.wait_ge(s["n_xnT"], 3)
            turn_context1(LAST)
            over_items(nodes, 2, 3)
            pe.wait_ge(s["n_xnT"], 4)
            output1(LAST)
            pe.wait_ge(s["c_x"], NB + 2)
            over_items(nodes, 3, NI + 8)

        @block.scalar
        def _(act):
            act.wait_ge(ld["wa"], 16)
            act.activation(half_am[:, :], wa[:, 4, :], ACT.Copy, scale=0.5).then_inc(s["half_am_ready"], 1)
            act.wait_ge(ld["cols"], 16)
            act.activation(bk_half[:, :], bk_col, ACT.Copy, scale=0.5 * SCALE0).then_inc(s["a_bk"], 1)
            act.wait_ge(s["a_bk"], 1)
            for n in range(2):
                act.wait_ge(s["a_proj_ps"], n + 1)
                act.activation(kT_all[:, 4 * n:4 * n + 4, :], ps[:, 4 + n, :], ACT.Identity, bias=bk_half[:, 0:1],
                               scale=0.5 * SCALE0).then_inc(s["a_k"], 1)
            for n in range(2):
                act.wait_ge(s["a_xnT_ps"], 4 * n + 4)
                act.activation(xnT_a[:, 4 * n:4 * n + 4, :], ps[:, n, :], ACT.Copy).then_inc(s["a_xnT"], 1)
            for n in range(2):
                act.wait_ge(s["a_proj_ps"], 3 + n)
                act.activation(qT_all[:, 4 * n:4 * n + 4, :], ps[:, 2 + n, :], ACT.Identity,
                               bias=bq_col).then_inc(s["a_q"], 1)
            act.sem_inc(s["a_pT_act"], 2)
            act.sem_inc(s["a_r"], 1)

            def attn0(t):
                front, back = t.before(1), t.before(2)

                def turned(b, k):
                    act.wait_ge(s["a_pT_ps"], 4 * b.n + k + 5)
                    act.wait_ge(s["a_pv_ps"], b.n + 1)
                    act.activation(probT[:, 4 * k:4 * k + 4, :], ps[:, 5, :], ACT.Copy).then_inc(s["a_pT_act"], 1)

                def exps(b, k):
                    act.wait_ge(s["a_nmax"], 4 * b.n + k + 5)
                    for h in range(4 * k, 4 * k + 4):
                        last = act.activation(prob[:, b.p, h, :], fs[:, b.p, h, :], ACT.Exp, scale=-1.0,
                                              bias=nmax[:, b.p, h:h + 1], accum_out=den[:, b.p, h:h + 1])
                    last.then_inc(s["a_exp"], 1)

                if front is not None:
                    if front.reg is not None or front.off >= 1:
                        act.wait_ge(s["a_rden"], front.n)
                        act.wait_ge(s["a_pT_ps"], 4 * front.n)
                    exps(front, 0)
                if back is not None:
                    turned(back, 1)
                if front is not None:
                    exps(front, 1)
                    exps(front, 2)
                if back is not None:
                    turned(back, 3)
                    act.wait_ge(s["a_r_ps"], back.n + 1)
                    act.activation(r_bc[:, back.p, :], ps[:, 6, 0:128], ACT.Copy).then_inc(s["a_r"], 1)
                if front is not None:
                    exps(front, 3)

            over_batches(act, attn0, 2)

            def context1T(b):
                act.wait_ge(s["c_ctxT_ps"], b.n + 1)
                act.activation(ctx1T[:, b.p, :], ps[:, 7, 0:128], ACT.Copy).then_inc(s["c_ctxT"], 1)

            def moe_attn1(t):
                cur, front, cur1, back1 = (t.before(k) for k in (0, 1, 3, 4))

                def relu(b, k):
                    act.wait_ge(s["b_h_ps"], 4 * b.n + k + 1)
                    if b.reg is not None or b.off >= 1 or k >= 2:
                        act.wait_ge(s["b_h2"], 4 * b.n + k - 1)
                    act.activation(relu_h[:, k % 2, :, :], ps[:, k % 2, :], ACT.Relu).then_inc(s["b_relu"], 1)

                def square(b, k):
                    act.wait_ge(s["b_relu"], 4 * b.n + k + 1)
                    act.activation(h2[:, b.p, 4 * k:4 * k + 4, :], relu_h[:, k % 2, :, :],
                                   ACT.Square).then_inc(s["b_h2"], 1)

                if front is not None:
                    b = front
                    act.wait_ge(s["b_gmax"], b.n + 1)
                    act.activation(gsm[:, b.p, 0, :], ps[:, 6, 128:128 + NEXP], ACT.Exp, bias=gcol[:, b.p, 0:1],
                                   accum_out=gcol[:, b.p, 1:2]).then_inc(s["b_gexp"], 1)
                    for k in range(2):
                        relu(b, k)
                        square(b, k)
                if (b := cur1) is not None:
                    act.wait_ge(s["c_xnT_ps"], b.n + 1)
                    act.activation(xn1T[:, b.p, :], ps[:, 2, 0:128], ACT.Copy).then_inc(s["c_xnT"], 1)
                if front is not None:
                    relu(front, 2)
                if back1 is not None:
                    context1T(back1)
                if (b := cur) is not None:
                    act.wait_ge(s["b_xnT_ps"], b.n + 1)
                    act.activation(xnT[:, b.p, :], ps[:, 6, 0:128], ACT.Copy).then_inc(s["b_xnT"], 1)
                if front is not None:
                    square(front, 2)
                    relu(front, 3)
                if (b := cur1) is not None:
                    act.wait_ge(s["c_sub"], b.n + 1)
                    act.activation(e1[:, b.p, :], sc1[:, b.p, :], ACT.Exp, scale=SCALE1).then_inc(s["c_exp"], 1)
                if front is not None:
                    square(front, 3)

            act.sem_inc(s["b_gexp"], 1)

            def norm3(b):
                act.wait_ge(s["n_xnT_ps"], b + 1)
                act.activation(nodesT[:, 0, b, :], ps[:, 7, 384:512], ACT.Copy).then_inc(s["n_xnT"], 1)

            over_batches(act, moe_attn1, 3)
            norm3(0)

            def nodes(at):
                def exps(i, k):
                    act.wait_ge(s["d_max"], 2 * i + k + 1)
                    if i >= 2:
                        act.wait_ge(s["d_pT_ps"], 2 * i - 3 + k)
                        act.wait_ge(s["d_rden"], i - 1)
                    for h in range(4):
                        act.activation(p3[:, i % 2, 4 * k + h, :],
                                       ps[:, 2 * (i % 2) + k, 128 * h:128 * h + 128], ACT.Exp,
                                       bias=nmax3[:, i % 2, 4 * k + h:4 * k + h + 1],
                                       accum_out=den3[:, i % 2, 4 * k + h:4 * k + h + 1]).then_inc(s["d_exp"], 1)

                if (i := at(3)) is not None:
                    exps(i, 0)
                if (i := at(4)) is not None:
                    act.wait_ge(s["d_pT_ps"], 2 * i + 2)
                    if i >= 1:
                        act.wait_ge(s["d_pv_ps"], i)
                    act.activation(p3T[:, 4:8, :], ps[:, 5, :], ACT.Copy).then_inc(s["d_pT_act"], 1)
                if (b := to_norm(at, 1)) is not None:
                    act.wait_ge(s["n_xnT_ps"], b + 1)
                if (b := to_finish(at, 6)) is not None:
                    act.wait_ge(s["e_T_ps"], b + 1)
                if (i := at(4)) is not None:
                    act.wait_ge(s["d_r_ps"], i + 1)
                    act.activation(r_bc[:, i % 2, :], ps[:, 7, 128:256], ACT.Copy).then_inc(s["d_r"], 1)
                if (b := to_norm(at, 1)) is not None:
                    norm3(b)
                if (b := to_finish(at, 6)) is not None:
                    act.activation(fin[:, b, :], ps[:, 7, 384:512], ACT.Copy).then_inc(s["e_fin"], 1)
                if (i := at(3)) is not None:
                    exps(i, 1)

            over_items(nodes, 0, 2)
            context1T(LAST)
            over_items(nodes, 2, NI + 8)

        @block.vector
        def _(dve):
            for k in range(NEXP):
                dve.memset(iota8[:, k:k + 1], float(k)).then_inc(s["iota_ready"], 1)
            dve.wait_ge(ld["x"], 16)
            for b in range(NB):
                dve.bn_stats(stats_a[:, b, :], x_all[:, b, :]).then_inc(s["a_stats"], 1)
            for b in range(NB):
                dve.wait_ge(s["a_stats"], b + 1)
                dve.bn_aggr(mv_a[:, b, :], stats_a[:, b, :]).then_inc(s["a_mv"], 1)
            dve.wait_ge(s["a_mv"], NB)
            dve.tensor_scalar(veps_a[:, :], mv_a[:, :, 1], 1e-5, None, ALU.add).then_inc(s["a_veps"], 1)
            dve.wait_ge(s["a_rstd"], 1)
            for b in range(NB):
                dve.tensor_scalar(xn_a[:, b, :], x_all[:, b, :], mv_a[:, b, 0:1], rstd_a[:, b:b + 1],
                                  ALU.subtract, ALU.mult).then_inc(s["a_xn"], 1)
            dve.wait_ge(ld["rows"], 16)
            for n in range(2):
                dve.wait_ge(s["a_v_ps"], n + 1)
                dve.tensor_tensor(v_all[:, 4 * n:4 * n + 4, :], ps[:, 6 + n, :].rearrange("p (b e) -> p b e", e=E),
                                  bv_row.unsqueeze(1).to_broadcast([T, 4, E]), ALU.add).then_inc(s["a_v"], 1)
            dve.wait_ge(s["const_ready"], 2)
            dve.wait_ge(s["v_zeroed"], 1)
            dve.wait_ge(s["a_v"], 2)
            dve.sem_inc(s["a_nmax"], 4)
            dve.sem_inc(s["a_pT_dve"], 2)
            dve.sem_inc(s["a_x"], 2)
            dve.sem_inc(s["a_rden"], 1)

            def attn0(t):
                front, back, done = t.before(1), t.before(2), t.before(3)

                def turned(b, k):
                    dve.wait_ge(s["a_pT_ps"], 4 * b.n + k + 5)
                    dve.wait_ge(s["a_pv_ps"], b.n + 1)
                    dve.tensor_copy(probT[:, 4 * k:4 * k + 4, :].rearrange("p h t -> p (h t)"),
                                    ps[:, 4, :]).then_inc(s["a_pT_dve"], 1)

                def neg_scores(b, k):
                    dve.wait_ge(s["a_s_ps"], 4 * b.n + k + 9)
                    if k % 2 == 0:
                        dve.wait_ge(s["a_bias"], 2 * b.n + k // 2 + 5)
                    dve.sem_inc(s["passed"], 1)
                    for h in range(4 * k, 4 * k + 4):
                        last = dve.tensor_tensor_reduce(
                            fs[:, b.p, h, :], ps[:, k, 128 * (h % 4):128 * (h % 4) + 128], fs[:, b.p, h, :],
                            -2.0, 3.0e38, ALU.add, ALU.min, nmax[:, b.p, h:h + 1])
                    last.then_inc(s["a_nmax"], 1)

                if front is not None:
                    neg_scores(front, 0)
                    neg_scores(front, 1)
                if done is not None:
                    dve.wait_ge(s["a_pv_ps"], done.n + 2)
                    dve.wait_ge(s["a_r"], done.n + 2)
                    dve.tensor_tensor(ctxn[:, done.p, :], ps[:, 7, 0:128], r_bc[:, done.p, :],
                                      ALU.mult).then_inc(s["a_ctxn"], 1)
                if back is not None:
                    dve.wait_ge(s["a_exp"], 4 * back.n + 4)
                    dve.reciprocal(rden[:, back.p, :], den[:, back.p, :]).then_inc(s["a_rden"], 1)
                    turned(back, 0)
                    dve.wait_ge(s["a_rden"], back.n + 2)
                    dve.tensor_copy(rrow[:, back.p, :].rearrange("p (h d) -> p h d", d=D0),
                                    rden[:, back.p, :].unsqueeze(2).to_broadcast([T, H0, D0])).then_inc(s["a_rrow"], 1)
                if done is not None:
                    dve.wait_ge(s["a_o_ps"], done.n + 1)
                    dve.wait_ge(s["a_xbo"], done.n + 1)
                    dve.tensor_tensor(x_all[:, done.n, :], ps[:, 7, 128:256], xbo[:, done.p, :],
                                      ALU.add).then_inc(s["a_x"], 1)
                if front is not None:
                    b = front
                    if b.reg is not None or b.off >= 1:
                        dve.wait_ge(s["a_pv_ps"], b.n)
                    dve.tensor_copy(spread0(v_spread[:, b.p, :]),
                                    v_all[:, b.n, :].rearrange("p (j v d) -> p v j d", v=4, d=D0)).then_inc(s["a_vs"], 1)
                    neg_scores(front, 2)
                if (b := t.before(0)) is not None:
                    dve.wait_ge(s["a_k"], 2)
                    dve.wait_ge(s["a_s_ps"], 4 * b.n + 4)
                    dve.tensor_tensor(km[:, b.p, 0:8, :],
                                      kT_all[:, b.n, :].unsqueeze(1).to_broadcast([E, 8, T]),
                                      head0[:, 0:8].unsqueeze(2).to_broadcast([E, 8, T]),
                                      ALU.mult).then_inc(s["a_km_dve"], 1)
                    dve.wait_ge(s["a_q"], 2)
                    dve.tensor_copy(qT[:, b.p, :], qT_all[:, b.n, :]).then_inc(s["a_qT"], 1)
                if back is not None:
                    turned(back, 2)
                if front is not None:
                    neg_scores(front, 3)

            def keys_values1():
                for k, e, f in ((0, 0, 1.0), (1, 1, SCALE3), (2, 2, 1.0), (3, 2, 1.0)):
                    dve.tensor_scalar(scl[:, :, k], ew[:, :, e], f, None, ALU.mult).then_inc(s["f_scl"], 1)
                dve.wait_ge(s["f_scl"], 4)
                dve.wait_ge(ld["wd"], 16 * NODES)
                for n in range(4):
                    dve.wait_ge(s["kv_ps"], n + 1)
                    dve.tensor_tensor(kv_all[:, 2 * n:2 * n + 2, :, :],
                                      ps[:, n, :].rearrange("p (b k e) -> p b k e", k=2, e=E),
                                      bqkv1_row[:, 1:3, :].unsqueeze(1).to_broadcast([T, 2, 2, E]),
                                      ALU.add).then_inc(s["kv"], 1)
                dve.wait_ge(s["f_b_ps"], 1)
                dve.tensor_tensor(bias3[:, :, 1:3], ps[:, 6, 128:128 + 2 * NODES].rearrange("p (c k) -> p c k", k=2),
                                  scl[:, :, 0:2], ALU.mult).then_inc(s["f_bias"], 1)
                dve.tensor_tensor(wres[:, :, :], wd[:, 7, :, :], ew[:, :, 0:1].to_broadcast([E, NODES, 128]),
                                  ALU.mult).then_inc(s["f_wres"], 1)
                dve.tensor_tensor(bias3[:, :, 0], beT[:, :, 0], ew[:, :, 0], ALU.mult).then_inc(s["f_bias"], 1)

            def fold_weights():
                for c in range(NODES):
                    dve.wait_ge(s["f_w_ps"], c + 1)
                    dve.tensor_tensor(wf[:, c, :, :], ps[:, FOLD_BANKS[c % 3], :].rearrange("p (k e) -> p k e", e=128),
                                      scl[:, c, :].unsqueeze(2).to_broadcast([E, 4, 128]),
                                      ALU.mult).then_inc(s["f_w"], 1)

            def ln_stats(name, b):
                dve.sem_inc(s["passed"], 1)
                dve.bn_stats(stats[name][:, b.p, :], x_all[:, b.n, :]).then_inc(s[name + "_stats"], 1)

            def ln_mean(name, b):
                dve.wait_ge(s[name + "_stats"], b.n + 1)
                dve.sem_inc(s["passed"], 1)
                dve.bn_aggr(mv[name][:, b.p, :], stats[name][:, b.p, :]).then_inc(s[name + "_mv"], 1)

            def ln_eps(name, b):
                dve.wait_ge(s[name + "_mv"], b.n + 1)
                dve.tensor_scalar(veps[name][:, b.p:b.p + 1], mv[name][:, b.p, 1:2], 1e-5, None,
                                  ALU.add).then_inc(s[name + "_veps"], 1)

            def ln_apply(name, b):
                dve.wait_ge(s[name + "_rstd"], b.n + 1)
                dve.tensor_scalar(xn[name][:, b.p, :], x_all[:, b.n, :], mv[name][:, b.p, 0:1],
                                  rstd[name][:, b.p:b.p + 1], ALU.subtract, ALU.mult).then_inc(s[name + "_xn"], 1)

            def norm3_stats(b):
                dve.wait_ge(s["c_x"], b + 3)
                for ln_step in (ln_stats, ln_mean, ln_eps):
                    ln_step("n", Batch(None, b))

            def weigh_values(b):
                dve.wait_ge(s["c_exp"], b.n + 1)
                dve.wait_ge(s["c_ctx_ps"], b.n + 1)
                vv = kv_all[:, b.n, 1, :].rearrange("p (s h e) -> p h s e", h=H1, e=2)[:, :, :, 0]
                dve.tensor_tensor(
                    ev[:, b.p, :, :].rearrange("p s (l h e) -> p l h s e", h=H1, e=2)[:, :, :, :, 0],
                    e1[:, b.p, :].rearrange("p (l h s) -> p l h s", h=H1, s=G1),
                    vv.unsqueeze(1).to_broadcast([T, G1, H1, G1]), ALU.mult).then_inc(s["c_ev0"], 1)

            def sums1(b):
                dve.tensor_reduce(l1[:, b.p, :], e1[:, b.p, :].rearrange("p (g s) -> p g s", s=G1), AX_X,
                                  ALU.add).then_inc(s["c_l"], 1)

            def reciprocals1(b):
                dve.wait_ge(s["c_l"], b.n + 1)
                dve.reciprocal(rl1[:, b.p, :], l1[:, b.p, :]).then_inc(s["c_rl"], 1)

            def context1(b):
                dve.wait_ge(s["c_rl"], b.n + 1)
                dve.wait_ge(s["c_ctx_ps"], b.n + 3)
                dve.tensor_tensor(ctx1[:, b.p, :].rearrange("p (g e) -> p g e", e=2),
                                  ps[:, 3, 0:128].rearrange("p (g e) -> p g e", e=2),
                                  rl1[:, b.p, :].unsqueeze(2).to_broadcast([T, 64, 2]),
                                  ALU.mult).then_inc(s["c_ctx"], 1)

            def residual1(b):
                dve.wait_ge(s["c_o_ps"], b.n + 1)
                dve.wait_ge(s["c_xbo"], b.n + 1)
                dve.tensor_tensor(x_all[:, b.n, :], ps[:, 7, 128:256], xbo[:, b.p, :],
                                  ALU.add).then_inc(s["c_x"], 1)

            def moe_attn1(t):
                cur, front, back, cur1, back1 = (t.before(k) for k in range(5))

                def weighted(b, e):
                    if e % 4 == 0:
                        dve.wait_ge(s["b_y_ps"], 2 * b.n + e // 4 + 1)
                    dve.wait_ge(s["b_y"], 8 * b.n + e + 8)
                    dve.scalar_tensor_tensor(out=x_all[:, b.n, :], in0=ps[:, 4 + e // 4, 128 * (e % 4):128 * (e % 4) + 128],
                                             scalar=comb[:, b.p, e:e + 1], in1=x_all[:, b.n, :],
                                             op0=ALU.mult, op1=ALU.add).then_inc(s["b_y"], 1)

                if back is not None:
                    dve.wait_ge(s["b_comb"], back.n + 1)
                if cur1 is not None:
                    dve.wait_ge(s["b_y"], 8 * cur1.n + 16)
                    ln_stats("c", cur1)
                if cur is not None:
                    dve.wait_ge(s["a_x"], cur.n + 3)
                    ln_stats("b", cur)
                if cur1 is not None:
                    ln_mean("c", cur1)
                if cur is not None:
                    ln_mean("b", cur)
                if front is not None:
                    b = front
                    n, p = b.n, b.p
                    dve.wait_ge(s["b_gate_ps"], n + 1)
                    dve.tensor_reduce(gcol[:, p, 0:1], ps[:, 6, 128:128 + NEXP], AX_X, ALU.max,
                                      negate=True).then_inc(s["b_gmax"], 1)
                if cur1 is not None:
                    ln_eps("c", cur1)
                if cur is not None:
                    ln_eps("b", cur)
                if back1 is not None:
                    weigh_values(back1)
                if front is not None:
                    dve.wait_ge(s["b_gexp"], n + 2)
                    dve.reciprocal(gcol[:, p, 2:3], gcol[:, p, 1:2]).then_inc(s["b_rsum"], 1)
                if cur1 is not None:
                    ln_apply("c", cur1)
                if front is not None:
                    dve.wait_ge(s["b_rsum"], n + 1)
                    dve.tensor_scalar(gsm[:, p, 1, :], gsm[:, p, 0, :], gcol[:, p, 2:3], None,
                                      ALU.mult).then_inc(s["b_prob"], 1)
                if back1 is not None:
                    sums1(back1)
                if front is not None:
                    dve.wait_ge(s["b_prob"], n + 1)
                    dve.sem_inc(s["passed"], 1)
                    dve.max(gsm[:, p, 2, :], gsm[:, p, 1, :]).then_inc(s["b_top"], 1)
                if cur is not None:
                    ln_apply("b", cur)
                if front is not None:
                    dve.wait_ge(s["b_top"], n + 1)
                    dve.sem_inc(s["passed"], 1)
                    dve.max_index(gidx[:, p, :], gsm[:, p, 2, :], gsm[:, p, 1, :]).then_inc(s["b_idx"], 1)
                    dve.scalar_tensor_tensor(out=gcol[:, p, 3:4], in0=gsm[:, p, 2, 0:1], scalar=1e-8,
                                             in1=gsm[:, p, 2, 1:2], op0=ALU.add, op1=ALU.add).then_inc(s["b_gden"], 1)
                if back1 is not None:
                    reciprocals1(back1)
                if front is not None:
                    dve.wait_ge(s["b_idx"], n + 1)
                    dve.tensor_copy(gcol[:, p, 4:6], gidx[:, p, 0:2]).then_inc(s["b_idxf"], 1)
                    dve.wait_ge(s["b_gden"], n + 1)
                    dve.reciprocal(gcol[:, p, 6:7], gcol[:, p, 3:4]).then_inc(s["b_rgden"], 1)
                if back is not None:
                    weighted(back, 0)
                if cur1 is not None:
                    b = cur1
                    dve.wait_ge(s["c_q_ps"], b.n + 1)
                    dve.wait_ge(s["c_sc"], b.n + 1)
                    dve.tensor_tensor(q1[:, b.p, :], ps[:, 2, 128:256], bqkv1_row[:, 0, :],
                                      ALU.add).then_inc(s["c_q"], 1)
                if back is not None:
                    weighted(back, 1)
                if cur1 is not None:
                    dve.wait_ge(s["c_q"], b.n + 2)
                    qv = q1[:, b.p, :].rearrange("p (l h e) -> p l h e", h=H1, e=2)[:, :, :, 0]
                    kk = kv_all[:, b.n, 0, :].rearrange("p (s h e) -> p h s e", h=H1, e=2)[:, :, :, 0]
                    dve.tensor_tensor(
                        pr0[:, b.p, :].rearrange("p (l h s) -> p l h s", h=H1, s=G1),
                        qv.unsqueeze(3).to_broadcast([T, G1, H1, G1]),
                        kk.unsqueeze(1).to_broadcast([T, G1, H1, G1]), ALU.mult).then_inc(s["c_pr0"], 1)
                    if b.reg is None and b.off == NB - 1:
                        for first in range(2):
                            norm3_stats(first)
                if back is not None:
                    weighted(back, 2)
                if front is not None:
                    dve.wait_ge(s["b_rgden"], n + 1)
                    dve.tensor_scalar(gsm[:, p, 3, 0:2], gsm[:, p, 2, 0:2], gcol[:, p, 6:7], None,
                                      ALU.mult).then_inc(s["b_w"], 1)
                if back is not None:
                    weighted(back, 3)
                if back1 is not None:
                    context1(back1)
                if back is not None:
                    weighted(back, 4)
                if front is not None:
                    dve.wait_ge(s["b_w"], n + 1)
                    dve.wait_ge(s["b_idxf"], n + 1)
                for k, name in ((0, "b_c1"), (1, "b_c2")):
                    if front is not None:
                        dve.tensor_scalar(gsm[:, p, 4 + k, :], iota8[:, :], gcol[:, p, 4 + k:5 + k],
                                          gsm[:, p, 3, k:k + 1], ALU.is_equal, ALU.mult).then_inc(s[name], 1)
                    if back is not None:
                        weighted(back, 5 + k)
                if front is not None:
                    dve.wait_ge(s["b_c1"], n + 1)
                    dve.wait_ge(s["b_c2"], n + 1)
                    dve.tensor_tensor(comb[:, p, :], gsm[:, p, 4, :], gsm[:, p, 5, :], ALU.add).then_inc(s["b_comb"], 1)
                if back is not None:
                    weighted(back, 7)
                if cur1 is not None:
                    b = cur1
                    dve.wait_ge(s["c_sc"], b.n + 3)
                    scores = sc1[:, b.p, :].rearrange("p (g s) -> p g s", s=G1)
                    dve.tensor_reduce(m1[:, b.p, :], scores, AX_X, ALU.max).then_inc(s["c_m"], 1)
                    dve.wait_ge(s["c_m"], b.n + 1)
                    dve.tensor_tensor(scores, scores, m1[:, b.p, :].unsqueeze(2).to_broadcast([T, 64, G1]),
                                      ALU.subtract).then_inc(s["c_sub"], 1)
                if back1 is not None:
                    residual1(back1)

            def moe_start():
                dve.wait_ge(s["iota_ready"], NEXP)
                dve.wait_ge(s["v_zeroed"], 2)
                dve.sem_inc(s["b_y"], 8)
                dve.sem_inc(s["c_q"], 1)
                dve.sem_inc(s["c_ctx"], 1)
                dve.sem_inc(s["c_x"], 2)
                moe_attn1(Batch(None, 0))
                fold_weights()

            over_batches(dve, attn0, 3, {NB + 1: keys_values1, NB + 2: moe_start})

            def norm3_apply(b):
                if b >= 2:
                    dve.wait_ge(s["n_xnT_ps"], b - 1)
                ln_apply("n", Batch(None, b))

            over_batches(dve, moe_attn1, 3, first=1)
            for b in range(2):
                norm3_apply(b)
            dve.wait_ge(s["f_w"], NODES)
            dve.wait_ge(s["f_bias"], 2)

            def nodes(at):
                back = at(4)
                if back is not None:
                    dve.wait_ge(s["d_exp"], 8 * back + 8)
                    dve.reciprocal(rden3[:, back % 2, :], den3[:, back % 2, :]).then_inc(s["d_rden"], 1)
                    dve.wait_ge(s["d_rden"], back + 1)
                    if back >= 2:
                        dve.wait_ge(s["d_r_ps"], back - 1)
                    dve.tensor_copy(rrow[:, back % 2, :].rearrange("p (h d) -> p h d", d=D3),
                                    rden3[:, back % 2, :].unsqueeze(2).to_broadcast([T, H3, D3])).then_inc(s["d_rrow"], 1)
                if (i := at(5)) is not None:
                    c, b = ITEMS[i]
                    dve.wait_ge(s["d_o_ps"], i + 1)
                    dve.scalar_tensor_tensor(out=nodesT[:, c + 1, b, :], in0=ps[:, 7, 256:384],
                                             scalar=act_w[:, c:c + 1], in1=qqk[:, b, 0, :],
                                             op0=ALU.mult, op1=ALU.add).then_inc(s["d_node"], 1)
                if back is not None:
                    dve.wait_ge(s["d_pT_ps"], 2 * back + 1)
                    if back >= 1:
                        dve.wait_ge(s["d_pv_ps"], back)
                    dve.tensor_copy(p3T[:, 0:4, :].rearrange("p h t -> p (h t)"), ps[:, 4, :]).then_inc(s["d_pT_dve"], 1)
                if (i := at(0)) is not None:
                    c, b = ITEMS[i]
                    dve.wait_ge(s["d_proj_ps"], i + 1)
                    dve.tensor_tensor(qqk[:, b, :, :], ps[:, 6, 0:384].rearrange("p (k t) -> p k t", t=T),
                                      bias3[:, c, :].unsqueeze(2).to_broadcast([E, 3, T]),
                                      ALU.add).then_inc(s["d_qqk"], 1)
                    dve.tensor_tensor(spread3(v3[:, b, :]),
                                      ps[:, 6, 384:512].rearrange("p (j v d) -> p v j d", v=2, d=D3),
                                      wf[:, c, 3, :].rearrange("p (j v d) -> p v j d", v=2, d=D3),
                                      ALU.add).then_inc(s["d_v"], 1)
                if (b := to_norm(at, 2)) is not None:
                    norm3_stats(b)
                if (b := to_finish(at, 7)) is not None:
                    dve.wait_ge(s["e_fin"], b + 1)
                    dve.bn_stats(stats_a[:, b, :], fin[:, b, :]).then_inc(s["e_stats"], 1)
                    dve.wait_ge(s["e_stats"], b + 1)
                    dve.bn_aggr(mv_a[:, b, :], stats_a[:, b, :]).then_inc(s["e_mv"], 1)
                    dve.wait_ge(s["e_mv"], b + 1)
                    dve.tensor_scalar(veps_a[:, b:b + 1], mv_a[:, b, 1:2], 1e-6, None, ALU.add).then_inc(s["e_veps"], 1)
                if (i := at(2)) is not None:
                    for k in range(2):
                        dve.wait_ge(s["d_s_ps"], 2 * i + k + 1)
                        dve.tensor_reduce(nmax3[:, i % 2, 4 * k:4 * k + 4],
                                          ps[:, 2 * (i % 2) + k, :].rearrange("p (h k) -> p h k", k=T),
                                          AX_X, ALU.max, negate=True).then_inc(s["d_max"], 1)
                if (b := to_norm(at, 2)) is not None:
                    norm3_apply(b)
                if (b := to_finish(at, 7)) is not None:
                    dve.scalar_tensor_tensor(out=fin[:, b, :], in0=fin[:, b, :], scalar=mv_a[:, b, 0:1], in1=g_row,
                                             op0=ALU.subtract, op1=ALU.mult).then_inc(s["e_g"], 1)
                    dve.wait_ge(s["e_g"], b + 1)
                    dve.wait_ge(s["e_rstd"], b + 1)
                    dve.wait_ge(s["e_xb"], b + 1)
                    dve.scalar_tensor_tensor(out=fin2[:, b, :], in0=fin[:, b, :], scalar=rstd_a[:, b:b + 1],
                                             in1=xb[:, b, :], op0=ALU.mult, op1=ALU.add).then_inc(s["e_out"], 1)
                if back is not None:
                    dve.wait_ge(s["d_pv_ps"], back + 1)
                    dve.wait_ge(s["d_r"], back + 1)
                    if back >= 2:
                        dve.wait_ge(s["d_o_ps"], back - 1)
                    dve.tensor_tensor(ctxn[:, back % 2, :], ps[:, 7, 0:128], r_bc[:, back % 2, :],
                                      ALU.mult).then_inc(s["d_ctxn"], 1)

            for attn_step in (weigh_values, sums1, reciprocals1):
                attn_step(LAST)
            over_items(nodes, 0, 1)
            context1(LAST)
            over_items(nodes, 1, 3)
            residual1(LAST)
            over_items(nodes, 3, NI + 8)


def kernel(**inputs):
    import numpy as np
    import concourse.bacc as bacc
    from concourse.bass_utils import run_bass_kernel_spmd

    a = {k: np.asarray(v) for k, v in inputs.items()}

    def by_row(rows_of):
        return np.ascontiguousarray(np.concatenate([r.reshape(128, -1) for r in rows_of], axis=1))

    def on_all(v):
        return np.broadcast_to(v.reshape(1, -1), (128, v.size))

    edges = [node_sources(c)[1] for c in range(NODES)]
    we = a["L1_ffn_We"]
    arrays = {
        "x": np.ascontiguousarray(a["x"].transpose(1, 0, 2)),
        "ctxT": np.ascontiguousarray(a["ctx_1024"].transpose(2, 0, 1)),
        "fside": np.ascontiguousarray(a["fside_Bx16xSxS2_0"].transpose(0, 2, 1, 3)),
        "mask": np.ascontiguousarray(np.broadcast_to(a["mask_BxS2_bf0"].view(np.uint32).reshape(1, -1),
                                                         (128, NB * T // 4))),
        "wa": by_row([a["L0_xattn_Wq"].T, a["L0_xattn_Wk"].T, a["L0_xattn_Wv"].T, a["L0_xattn_Wo"].T,
                      a["fside_SxS2_0"]]),
        "wb": by_row([a["L0_ffn_Wg"], a["L0_ffn_W1"].transpose(1, 0, 2),
                      a["L0_ffn_W2"].reshape(NEXP * HID // 128, 128, E).transpose(1, 0, 2)]),
        "wc": by_row([a["L1_xattn_" + k].T for k in ("Wq", "Wk", "Wv", "Wo")]),
        "wd": by_row([we[e[k]].T for k in range(3) for e in edges]
                     + [a["L1_ffn_" + k][c] for k in ("Wo", "Wq", "Wk", "Wv") for c in range(NODES)]
                     + [we[e[0]] for e in edges]),
        "cols": by_row([a["L0_xattn_bq"], a["L0_xattn_bk"], on_all(a["L1_ffn_ew"]), on_all(a["L1_ffn_act_w"])]
                       + [a["L1_ffn_be"][e[k]] for e in edges for k in range(3)]
                       + [np.zeros((128, 20), np.float32)]),
        "rows": by_row([on_all(a[k]) for k in ("L0_xattn_bv", "L0_xattn_bo", "L1_xattn_bq", "L1_xattn_bk",
                                               "L1_xattn_bv", "L1_xattn_bo", "L1_ffn_ln_g", "L1_ffn_ln_b")]),
    }
    shapes = {"wa": (128, 5, 128), "wc": (128, 4, 128), "wd": (128, 8, NODES, 128), "rows": (128, 8, 128)}
    arrays = {k: v.reshape(shapes.get(k, v.shape)) for k, v in arrays.items()}
    nc = bacc.Bacc("TRN2", target_bir_lowering=False, num_devices=1)
    args = [nc.dram_tensor("in_" + k, v.shape, mybir.dt.from_np(v.dtype), kind="ExternalInput").ap()
            for k, v in arrays.items()]
    out = nc.dram_tensor("out", (T, NB, E), F32, kind="ExternalOutput").ap()
    xattn_ffn_kernel(nc, *args, out)
    r = run_bass_kernel_spmd(nc, [{"in_" + k: v for k, v in arrays.items()}], core_ids=[0])
    return np.ascontiguousarray(r.results[0]["out"].transpose(1, 0, 2))
```
